# Optimizing a Trainium2 kernel written in Bass

```python
import numpy as np
import jax
import jax.numpy as jnp

def _softmax(x, axis=-1):
    return jax.nn.softmax(x, axis=axis)

def _gelu(x):
    return jax.nn.gelu(x, approximate=True)

def _silu(x):
    return jax.nn.silu(x)

def _sigmoid(x):
    return jax.nn.sigmoid(x)

def _layernorm(x, axis=-1, eps=1e-05):
    m = jnp.mean(x, axis=axis, keepdims=True)
    v = jnp.var(x, axis=axis, keepdims=True)
    return (x - m) / jnp.sqrt(v + eps)

def _scatter_add(tgt, idx, src, axis=0):
    return tgt.at[idx].add(src)

def _segment_sum(src, seg, n):
    return jax.ops.segment_sum(src, seg, n)
kernel_name = 'mk_early_fusion_d1_tok_img768_r4_e365ab'

def setup_inputs(seed: int=0):
    np.random.seed(seed)
    _w = jnp.asarray

    def _rec_inputs():
        import jax
        import jax.numpy as jnp
        _rk = jax.random.key(seed)
        x = 7.57192e-06 + 1.00007 * jax.random.normal(jax.random.fold_in(_rk, 1), (64, 3, 224, 224), jnp.float32)
        txt = 0.363415 + 0.567636 * jax.random.normal(jax.random.fold_in(_rk, 2), (64, 77, 192), jnp.float32)
        return (x, txt)
    x, txt = _rec_inputs()

    def _L0_tok_setup():
        import jax, jax.numpy as jnp
        import numpy as np
        K = 4
        STRIDE = 4
        EPS = 1e-05
        SLOPE = 0.01

        def conv2d(x, w, b, stride):
            out = jax.lax.conv_general_dilated(x, w, (stride, stride), 'VALID', dimension_numbers=('NCHW', 'OIHW', 'NCHW'))
            return out + b[None, :, None, None]

        def batchnorm(x, g, b, m, v):
            inv = g / jnp.sqrt(v + EPS)
            return x * inv[None, :, None, None] + (b - m * inv)[None, :, None, None]

        def leaky_relu(x):
            return jnp.where(x >= 0, x, SLOPE * x)

        def deform_conv(x, offset, w, b):
            B, C, H, W = x.shape
            Ho, Wo = (offset.shape[2], offset.shape[3])
            KK = K * K
            off = offset.reshape(B, KK, 2, Ho, Wo)
            kh = jnp.repeat(jnp.arange(K), K).astype(x.dtype)
            kw = jnp.tile(jnp.arange(K), K).astype(x.dtype)
            base_y = (jnp.arange(Ho) * STRIDE).astype(x.dtype)
            base_x = (jnp.arange(Wo) * STRIDE).astype(x.dtype)
            py = base_y[None, None, :, None] + kh[None, :, None, None] + off[:, :, 0]
            px = base_x[None, None, None, :] + kw[None, :, None, None] + off[:, :, 1]
            y0 = jnp.floor(py)
            x0 = jnp.floor(px)
            wy = py - y0
            wx = px - x0

            def corner(yc, xc):
                yi = yc.astype(jnp.int32)
                xi = xc.astype(jnp.int32)
                valid = (yi >= 0) & (yi < H) & (xi >= 0) & (xi < W)
                yi = jnp.clip(yi, 0, H - 1)
                xi = jnp.clip(xi, 0, W - 1)
                v = jax.vmap(lambda img, a, c: img[:, a, c])(x, yi, xi)
                return v * valid[:, None].astype(x.dtype)
            v00 = corner(y0, x0)
            v01 = corner(y0, x0 + 1)
            v10 = corner(y0 + 1, x0)
            v11 = corner(y0 + 1, x0 + 1)
            wy_ = wy[:, None]
            wx_ = wx[:, None]
            sampled = v00 * (1 - wy_) * (1 - wx_) + v01 * (1 - wy_) * wx_ + v10 * wy_ * (1 - wx_) + v11 * wy_ * wx_
            out = jnp.einsum('bckhw,ock->bohw', sampled, w.reshape(w.shape[0], C, KK))
            return out + b[None, :, None, None]
        key = jax.random.key(seed)
        ks = jax.random.split(key, 16)
        f32 = jnp.float32
        inp = {'x': jax.random.normal(ks[0], (64, 3, 224, 224), f32), 'stem_w': jax.random.normal(ks[1], (96, 3, 4, 4), f32) * 0.1, 'stem_b': jax.random.normal(ks[2], (96,), f32) * 0.05, 'bn1_g': jax.random.uniform(ks[3], (96,), f32, 0.5, 1.5), 'bn1_b': jax.random.normal(ks[4], (96,), f32) * 0.05, 'bn1_m': jax.random.normal(ks[5], (96,), f32) * 0.05, 'bn1_v': jax.random.uniform(ks[6], (96,), f32, 0.5, 1.5), 'off_w': jax.random.normal(ks[7], (32, 96, 4, 4), f32) * 0.02, 'off_b': jax.random.normal(ks[8], (32,), f32) * 0.02, 'dcn_w': jax.random.normal(ks[9], (192, 96, 4, 4), f32) * 0.05, 'dcn_b': jax.random.normal(ks[10], (192,), f32) * 0.05, 'bn2_g': jax.random.uniform(ks[11], (192,), f32, 0.5, 1.5), 'bn2_b': jax.random.normal(ks[12], (192,), f32) * 0.05, 'bn2_m': jax.random.normal(ks[13], (192,), f32) * 0.05, 'bn2_v': jax.random.uniform(ks[14], (192,), f32, 0.5, 1.5)}
        return inp
    _L0_tok_all = _L0_tok_setup()
    _L0_tok_in = {k: v for k, v in _L0_tok_all.items() if k in ('stem_w', 'stem_b', 'bn1_g', 'bn1_b', 'bn1_m', 'bn1_v', 'off_w', 'off_b', 'dcn_w', 'dcn_b', 'bn2_g', 'bn2_b', 'bn2_m', 'bn2_v')}
    del _L0_tok_all

    def _L0_attn_setup():
        import jax, jax.numpy as jnp
        import numpy as np
        from jax import lax
        LAYERS = 4
        D_MODEL = 192
        D_STATE = 16
        D_CONV = 4
        EXPAND = 2
        D_INNER = EXPAND * D_MODEL
        DT_RANK = (D_MODEL + 15) // 16
        B_SZ = 4
        SEQ = 1024

        def _silu(x):
            return x * jax.nn.sigmoid(x)

        def _mamba_block(h, in_w, cw, cb, xp_w, dt_w, dt_b, A_log, Dp, out_w):
            B, L, _ = h.shape
            xz = h @ in_w
            xi, z = jnp.split(xz, 2, axis=-1)
            xt = xi.transpose(0, 2, 1)
            conv = lax.conv_general_dilated(xt, cw[:, None, :], (1,), ((D_CONV - 1, 0),), feature_group_count=D_INNER, dimension_numbers=('NCH', 'OIH', 'NCH'))
            xc = _silu((conv + cb[None, :, None]).transpose(0, 2, 1))
            x_dbl = xc @ xp_w
            dt = jax.nn.softplus(x_dbl[..., :DT_RANK] @ dt_w + dt_b)
            Bc = x_dbl[..., DT_RANK:DT_RANK + D_STATE]
            Cc = x_dbl[..., DT_RANK + D_STATE:]
            A = -jnp.exp(A_log)

            def step(hs, ins):
                dt_t, B_t, C_t, u_t = ins
                dA = jnp.exp(dt_t[:, :, None] * A)
                hs = dA * hs + (dt_t * u_t)[:, :, None] * B_t[:, None, :]
                y = jnp.einsum('bds,bs->bd', hs, C_t)
                return (hs, y)
            h0 = jnp.zeros((B, D_INNER, D_STATE), xc.dtype)
            tm = lambda a: a.transpose(1, 0, 2)
            _, ys = lax.scan(step, h0, (tm(dt), tm(Bc), tm(Cc), tm(xc)))
            y = ys.transpose(1, 0, 2) + xc * Dp
            y = y * _silu(z)
            return y @ out_w
        key = jax.random.key(seed)
        ks = jax.random.split(key, 12)
        s = 0.02
        f = lambda k, shp: jax.random.normal(k, shp, dtype=jnp.float32)
        inp = {'x': f(ks[0], (B_SZ, SEQ, D_MODEL)), 'u': f(ks[1], (B_SZ, SEQ, D_MODEL)), 'in_proj_w': f(ks[2], (LAYERS, D_MODEL, 2 * D_INNER)) * s, 'conv_w': f(ks[3], (LAYERS, D_INNER, D_CONV)) * s, 'conv_b': jnp.zeros((LAYERS, D_INNER), jnp.float32), 'x_proj_w': f(ks[4], (LAYERS, D_INNER, DT_RANK + 2 * D_STATE)) * s, 'dt_proj_w': f(ks[5], (LAYERS, DT_RANK, D_INNER)) * s, 'dt_proj_b': f(ks[6], (LAYERS, D_INNER)) * s, 'A_log': jnp.broadcast_to(jnp.log(jnp.arange(1, D_STATE + 1, dtype=jnp.float32)), (LAYERS, D_INNER, D_STATE)).copy(), 'D': jnp.ones((LAYERS, D_INNER), jnp.float32), 'out_proj_w': f(ks[7], (LAYERS, D_INNER, D_MODEL)) * s, 'head_w1': f(ks[8], (D_MODEL, D_MODEL)) * s, 'head_b1': jnp.zeros((D_MODEL,), jnp.float32), 'head_w2': f(ks[9], (D_MODEL, D_MODEL)) * s, 'head_b2': jnp.zeros((D_MODEL,), jnp.float32)}
        return inp
    _L0_attn_all = _L0_attn_setup()
    _L0_attn_in = {k: v for k, v in _L0_attn_all.items() if k in ('u', 'in_proj_w', 'conv_w', 'conv_b', 'x_proj_w', 'dt_proj_w', 'dt_proj_b', 'A_log', 'D', 'out_proj_w', 'head_w1', 'head_b1', 'head_w2', 'head_b2')}
    del _L0_attn_all

    def _L0_ffn_setup():
        import jax, jax.numpy as jnp
        import numpy as np
        EPS = 1e-05

        def ter_quant(w):
            gamma = jnp.mean(jnp.abs(w)) + EPS
            wq = jnp.clip(jnp.round(w / gamma), -1.0, 1.0) * gamma
            return wq
        key = jax.random.key(seed)
        k_x, k_w1, k_w2 = jax.random.split(key, 3)
        B, S, D, H = (64, 197, 192, 768)
        x = jax.random.normal(k_x, (B, S, D), dtype=jnp.float32)
        w1 = jax.random.normal(k_w1, (H, D), dtype=jnp.float32) * (1.0 / np.sqrt(D))
        b1 = jnp.zeros((H,), dtype=jnp.float32)
        w2 = jax.random.normal(k_w2, (D, H), dtype=jnp.float32) * (1.0 / np.sqrt(H))
        b2 = jnp.zeros((D,), dtype=jnp.float32)
        return {'x': x, 'w1': w1, 'b1': b1, 'w2': w2, 'b2': b2}
    _L0_ffn_all = _L0_ffn_setup()
    _L0_ffn_in = {k: v for k, v in _L0_ffn_all.items() if k in ('w1', 'b1', 'w2', 'b2')}
    del _L0_ffn_all
    return {'x': x, 'txt': txt, 'L0_tok_stem_w': _L0_tok_in['stem_w'], 'L0_tok_stem_b': _L0_tok_in['stem_b'], 'L0_tok_bn1_g': _L0_tok_in['bn1_g'], 'L0_tok_bn1_b': _L0_tok_in['bn1_b'], 'L0_tok_bn1_m': _L0_tok_in['bn1_m'], 'L0_tok_bn1_v': _L0_tok_in['bn1_v'], 'L0_tok_off_w': _L0_tok_in['off_w'], 'L0_tok_off_b': _L0_tok_in['off_b'], 'L0_tok_dcn_w': _L0_tok_in['dcn_w'], 'L0_tok_dcn_b': _L0_tok_in['dcn_b'], 'L0_tok_bn2_g': _L0_tok_in['bn2_g'], 'L0_tok_bn2_b': _L0_tok_in['bn2_b'], 'L0_tok_bn2_m': _L0_tok_in['bn2_m'], 'L0_tok_bn2_v': _L0_tok_in['bn2_v'], 'L0_attn_u': _L0_attn_in['u'], 'L0_attn_in_proj_w': _L0_attn_in['in_proj_w'], 'L0_attn_conv_w': _L0_attn_in['conv_w'], 'L0_attn_conv_b': _L0_attn_in['conv_b'], 'L0_attn_x_proj_w': _L0_attn_in['x_proj_w'], 'L0_attn_dt_proj_w': _L0_attn_in['dt_proj_w'], 'L0_attn_dt_proj_b': _L0_attn_in['dt_proj_b'], 'L0_attn_A_log': _L0_attn_in['A_log'], 'L0_attn_D': _L0_attn_in['D'], 'L0_attn_out_proj_w': _L0_attn_in['out_proj_w'], 'L0_attn_head_w1': _L0_attn_in['head_w1'], 'L0_attn_head_b1': _L0_attn_in['head_b1'], 'L0_attn_head_w2': _L0_attn_in['head_w2'], 'L0_attn_head_b2': _L0_attn_in['head_b2'], 'L0_ffn_w1': _L0_ffn_in['w1'], 'L0_ffn_b1': _L0_ffn_in['b1'], 'L0_ffn_w2': _L0_ffn_in['w2'], 'L0_ffn_b2': _L0_ffn_in['b2']}

def reference(x, txt, L0_tok_stem_w, L0_tok_stem_b, L0_tok_bn1_g, L0_tok_bn1_b, L0_tok_bn1_m, L0_tok_bn1_v, L0_tok_off_w, L0_tok_off_b, L0_tok_dcn_w, L0_tok_dcn_b, L0_tok_bn2_g, L0_tok_bn2_b, L0_tok_bn2_m, L0_tok_bn2_v, L0_attn_u, L0_attn_in_proj_w, L0_attn_conv_w, L0_attn_conv_b, L0_attn_x_proj_w, L0_attn_dt_proj_w, L0_attn_dt_proj_b, L0_attn_A_log, L0_attn_D, L0_attn_out_proj_w, L0_attn_head_w1, L0_attn_head_b1, L0_attn_head_w2, L0_attn_head_b2, L0_ffn_w1, L0_ffn_b1, L0_ffn_w2, L0_ffn_b2):
    import jax
    import jax.numpy as jnp

    def _L0_tok_ref(x, stem_w, stem_b, bn1_g, bn1_b, bn1_m, bn1_v, off_w, off_b, dcn_w, dcn_b, bn2_g, bn2_b, bn2_m, bn2_v):
        import jax, jax.numpy as jnp
        import numpy as np
        K = 4
        STRIDE = 4
        EPS = 1e-05
        SLOPE = 0.01

        def conv2d(x, w, b, stride):
            out = jax.lax.conv_general_dilated(x, w, (stride, stride), 'VALID', dimension_numbers=('NCHW', 'OIHW', 'NCHW'))
            return out + b[None, :, None, None]

        def batchnorm(x, g, b, m, v):
            inv = g / jnp.sqrt(v + EPS)
            return x * inv[None, :, None, None] + (b - m * inv)[None, :, None, None]

        def leaky_relu(x):
            return jnp.where(x >= 0, x, SLOPE * x)

        def deform_conv(x, offset, w, b):
            B, C, H, W = x.shape
            Ho, Wo = (offset.shape[2], offset.shape[3])
            KK = K * K
            off = offset.reshape(B, KK, 2, Ho, Wo)
            kh = jnp.repeat(jnp.arange(K), K).astype(x.dtype)
            kw = jnp.tile(jnp.arange(K), K).astype(x.dtype)
            base_y = (jnp.arange(Ho) * STRIDE).astype(x.dtype)
            base_x = (jnp.arange(Wo) * STRIDE).astype(x.dtype)
            py = base_y[None, None, :, None] + kh[None, :, None, None] + off[:, :, 0]
            px = base_x[None, None, None, :] + kw[None, :, None, None] + off[:, :, 1]
            y0 = jnp.floor(py)
            x0 = jnp.floor(px)
            wy = py - y0
            wx = px - x0

            def corner(yc, xc):
                yi = yc.astype(jnp.int32)
                xi = xc.astype(jnp.int32)
                valid = (yi >= 0) & (yi < H) & (xi >= 0) & (xi < W)
                yi = jnp.clip(yi, 0, H - 1)
                xi = jnp.clip(xi, 0, W - 1)
                v = jax.vmap(lambda img, a, c: img[:, a, c])(x, yi, xi)
                return v * valid[:, None].astype(x.dtype)
            v00 = corner(y0, x0)
            v01 = corner(y0, x0 + 1)
            v10 = corner(y0 + 1, x0)
            v11 = corner(y0 + 1, x0 + 1)
            wy_ = wy[:, None]
            wx_ = wx[:, None]
            sampled = v00 * (1 - wy_) * (1 - wx_) + v01 * (1 - wy_) * wx_ + v10 * wy_ * (1 - wx_) + v11 * wy_ * wx_
            out = jnp.einsum('bckhw,ock->bohw', sampled, w.reshape(w.shape[0], C, KK))
            return out + b[None, :, None, None]
        h = conv2d(x, stem_w, stem_b, 4)
        h = leaky_relu(batchnorm(h, bn1_g, bn1_b, bn1_m, bn1_v))
        offset = conv2d(h, off_w, off_b, 4)
        h = deform_conv(h, offset, dcn_w, dcn_b)
        h = leaky_relu(batchnorm(h, bn2_g, bn2_b, bn2_m, bn2_v))
        B, C, Ho, Wo = h.shape
        return h.reshape(B, C, Ho * Wo).transpose(0, 2, 1)

    def _L0_attn_ref(x, u, in_proj_w, conv_w, conv_b, x_proj_w, dt_proj_w, dt_proj_b, A_log, D, out_proj_w, head_w1, head_b1, head_w2, head_b2):
        import jax, jax.numpy as jnp
        import numpy as np
        from jax import lax
        LAYERS = 4
        D_MODEL = 192
        D_STATE = 16
        D_CONV = 4
        EXPAND = 2
        D_INNER = EXPAND * D_MODEL
        DT_RANK = (D_MODEL + 15) // 16
        B_SZ = 4
        SEQ = 1024

        def _silu(x):
            return x * jax.nn.sigmoid(x)

        def _mamba_block(h, in_w, cw, cb, xp_w, dt_w, dt_b, A_log, Dp, out_w):
            B, L, _ = h.shape
            xz = h @ in_w
            xi, z = jnp.split(xz, 2, axis=-1)
            xt = xi.transpose(0, 2, 1)
            conv = lax.conv_general_dilated(xt, cw[:, None, :], (1,), ((D_CONV - 1, 0),), feature_group_count=D_INNER, dimension_numbers=('NCH', 'OIH', 'NCH'))
            xc = _silu((conv + cb[None, :, None]).transpose(0, 2, 1))
            x_dbl = xc @ xp_w
            dt = jax.nn.softplus(x_dbl[..., :DT_RANK] @ dt_w + dt_b)
            Bc = x_dbl[..., DT_RANK:DT_RANK + D_STATE]
            Cc = x_dbl[..., DT_RANK + D_STATE:]
            A = -jnp.exp(A_log)

            def step(hs, ins):
                dt_t, B_t, C_t, u_t = ins
                dA = jnp.exp(dt_t[:, :, None] * A)
                hs = dA * hs + (dt_t * u_t)[:, :, None] * B_t[:, None, :]
                y = jnp.einsum('bds,bs->bd', hs, C_t)
                return (hs, y)
            h0 = jnp.zeros((B, D_INNER, D_STATE), xc.dtype)
            tm = lambda a: a.transpose(1, 0, 2)
            _, ys = lax.scan(step, h0, (tm(dt), tm(Bc), tm(Cc), tm(xc)))
            y = ys.transpose(1, 0, 2) + xc * Dp
            y = y * _silu(z)
            return y @ out_w
        h = x
        for i in range(LAYERS):
            h = _mamba_block(h, in_proj_w[i], conv_w[i], conv_b[i], x_proj_w[i], dt_proj_w[i], dt_proj_b[i], A_log[i], D[i], out_proj_w[i])
        h1 = jax.nn.relu(h @ head_w1 + head_b1)
        return h1 @ head_w2 + head_b2

    def _L0_ffn_ref(x, w1, b1, w2, b2):
        import jax, jax.numpy as jnp
        import numpy as np
        EPS = 1e-05

        def ter_quant(w):
            gamma = jnp.mean(jnp.abs(w)) + EPS
            wq = jnp.clip(jnp.round(w / gamma), -1.0, 1.0) * gamma
            return wq
        h = jnp.einsum('bsd,hd->bsh', x, ter_quant(w1)) + b1
        h = jax.nn.gelu(h, approximate=False)
        y = jnp.einsum('bsh,dh->bsd', h, ter_quant(w2)) + b2
        return y
    h = _L0_tok_ref(x, L0_tok_stem_w, L0_tok_stem_b, L0_tok_bn1_g, L0_tok_bn1_b, L0_tok_bn1_m, L0_tok_bn1_v, L0_tok_off_w, L0_tok_off_b, L0_tok_dcn_w, L0_tok_dcn_b, L0_tok_bn2_g, L0_tok_bn2_b, L0_tok_bn2_m, L0_tok_bn2_v)
    h = jnp.concatenate([h, txt], axis=1)
    h = h + _L0_attn_ref(_layernorm(h, axis=-1), L0_attn_u, L0_attn_in_proj_w, L0_attn_conv_w, L0_attn_conv_b, L0_attn_x_proj_w, L0_attn_dt_proj_w, L0_attn_dt_proj_b, L0_attn_A_log, L0_attn_D, L0_attn_out_proj_w, L0_attn_head_w1, L0_attn_head_b1, L0_attn_head_w2, L0_attn_head_b2)
    h = h + _L0_ffn_ref(_layernorm(h, axis=-1), L0_ffn_w1, L0_ffn_b1, L0_ffn_w2, L0_ffn_b2)
    return h

_drawn_inputs = setup_inputs


def setup_inputs(seed=0):
    import zlib

    import numpy as np

    out = dict(_drawn_inputs(seed))
    spreads = {'L0_attn_conv_b': (0.0, 0.1),
     'L0_attn_D': (1.0, 0.2),
     'L0_attn_head_b1': (0.0, 0.331),
     'L0_attn_head_b2': (0.0, 0.1),
     'L0_ffn_b1': (0.0, 0.1),
     'L0_ffn_b2': (0.0, 0.1)}
    factors = {}
    for name, (base, spread) in spreads.items():
        noise = np.random.default_rng([zlib.crc32(name.encode()), seed]).standard_normal(out[name].shape)
        drawn = base * np.exp(spread * noise) if base else spread * noise
        out[name] = jnp.asarray(drawn.astype(out[name].dtype))
    for name, factor in factors.items():
        out[name] = (out[name] * factor).astype(out[name].dtype)
    return out
```

```python
from contextlib import ExitStack

import concourse.bass as bass
from concourse import mybir

ALU = mybir.AluOpType
ACT = mybir.ActivationFunctionType
F32 = mybir.dt.float32
BF16 = mybir.dt.bfloat16
I32 = mybir.dt.int32
U32 = mybir.dt.uint32

EPS = 1e-5
SLOPE = 0.01
D = 192
KLO, KHI = 128, 64
DI = 384
MT = DI // 128
NS = 16
RANK = 12
LAYERS = 4
TXT = 77
GRID = 14
NPOS = GRID * GRID
T = NPOS + TXT
TT = T // 3
CO = 96
HS = 56
TAPS = 16
PIT = HS + 3
NENT = PIT * PIT
QP = NPOS // 2
FH = 768
FM = FH // 128
XDR = 96 + RANK
NY = MT * T


def bcast(ap, parts):
    return ap.unsqueeze(0).to_broadcast([parts] + list(ap.shape))


def program(nc, w, out):
    NB = w["x"].shape[0]
    tab = nc.dram_tensor("tab", [2 * NENT, 4 * CO], F32, kind="Internal").ap()
    h0 = nc.dram_tensor("h0", [NB, T, D], F32, kind="Internal").ap()
    wcd = nc.dram_tensor("wcd", [LAYERS, 128, 6 * DI], F32, kind="Internal").ap()
    pad = nc.dram_tensor("pad", [LAYERS, 128, MT * NS + MT], F32, kind="Internal").ap()
    with ExitStack() as keep:
        sb = lambda n, s, d=F32: keep.enter_context(nc.sbuf_tensor(n, s, d))
        c = dict(
            ident=sb("ident", [128, 128]), ones=sb("ones", [1, 128]),
            w1q=sb("w1q", [128, 2, FH]), w2q=sb("w2q", [128, FM, D]),
            ws=sb("ws", [49, CO]), wd=sb("wd", [97, TAPS, D]), wo=sb("wo", [CO, TAPS, 32]),
            base=sb("base", [QP, 2, 32]), sel=sb("sel", [96, 2 * NS, 128], BF16),
        )
        setup(nc, w, c, tab, wcd, pad)
        tokens(nc, w, c, tab, h0, NB)
        mixer(nc, w, c, h0, wcd, pad, out, NB)


def setup(nc, w, c, tab, wcd, pad):
    with ExitStack() as ctx:
        sb = lambda n, s, d=F32: ctx.enter_context(nc.sbuf_tensor(n, s, d))
        sem = lambda n: ctx.enter_context(nc.semaphore(n))
        zero = sb("zero", [118, 4 * CO])
        g1, v1, b1, m1 = (sb(n, [49, CO]) for n in ("g1", "v1", "b1", "m1"))
        g2, v2 = sb("g2", [97, D]), sb("v2", [97, D])
        b2, m2 = sb("b2", [97, D]), sb("m2", [97, D])
        offb = sb("offb", [QP, 32])
        self32 = sb("self32", [96, 2 * NS, 128])
        wx = sb("wx", [128, 2, DI])
        cw = sb("cw", [128, 6, DI])
        wc = sb("wc", [128, 6, DI])
        pa = sb("pa", [128, MT * NS + MT])
        ab = sb("ab", [128, 2 * FH])
        asum = sb("asum", [128, 2])
        gam = sb("gam", [128, 2])
        half = sb("half", [128, 2])
        nhalf = sb("nhalf", [128, 2])
        onesq = sb("onesq", [128, 128])
        neg = sb("neg", [128, 2 * FH])
        tot = ctx.enter_context(nc.psum_tensor("tot", [128, 2], F32))
        loads, zeroed, tabz = sem("loads"), sem("zeroed"), sem("tabz")
        step, act_step, summed = sem("step"), sem("act_step"), sem("summed")
        lay_ld, lay_done, lay_st = sem("lay_ld"), sem("lay_done"), sem("lay_st")
        pa_exp = sem("pa_exp")
        rows = [
            (c["ident"][:, :], w["ident"]), (c["ws"][:, :], w["stem"]),
            (g1[:, :], bcast(w["bn1_g"], 49)), (v1[:, :], bcast(w["bn1_v"], 49)),
            (b1[48:49, :], bcast(w["bn1_b"], 1)), (m1[48:49, :], bcast(w["bn1_m"], 1)),
            (c["wd"][0:96, :, :], w["dcn_w"]), (c["wd"][96:97, 0, :], bcast(w["dcn_b"], 1)),
            (g2[:, :], bcast(w["bn2_g"], 97)), (v2[:, :], bcast(w["bn2_v"], 97)),
            (b2[96:97, :], bcast(w["bn2_b"], 1)), (m2[96:97, :], bcast(w["bn2_m"], 1)),
            (c["wo"][:, :, :], w["off_w"]), (c["base"][:, :, :], w["base"]),
            (offb[:, :], bcast(w["off_b"], QP)),
            (c["w1q"][:, 0, :], w["ffn_w1"][0:KLO, :]), (c["w1q"][0:KHI, 1, :], w["ffn_w1"][KLO:D, :]),
            (c["w2q"][:, :, :], w["ffn_w2"]), (self32[:, :, :], w["sel"]),
        ]
        NZ = 2
        block = ctx.enter_context(nc.Block())

        @block.sync
        def _(sp):
            sp.wait_ge(zeroed, 5)
            for dst, src in rows:
                sp.dma_start(dst, src).then_inc(loads, 16)
            t = tab.rearrange("(n p) c -> n p c", p=118)
            for n in range(2 * NENT // 118):
                sp.dma_start(t[n], zero[:, :]).then_inc(tabz, 16)
            sp.wait_ge(tabz, 16 * (2 * NENT // 118))
            for l in range(LAYERS):
                sp.wait_ge(lay_st, 32 * l)
                sp.dma_start(wx[:, :, :], w["in_x"][l]).then_inc(lay_ld, 16)
                taps = w["conv_w"][l]
                for j in range(4):
                    sp.dma_start(cw[:, j, :], bcast(taps[j], 128)).then_inc(lay_ld, 16)
                for q in range(2):
                    sp.dma_start(cw[0:64, 4 + q, :], bcast(taps[3 - 2 * q], 64)).then_inc(lay_ld, 16)
                    sp.dma_start(cw[64:128, 4 + q, :], bcast(taps[2 - 2 * q], 64)).then_inc(lay_ld, 16)
                sp.dma_start(pa[:, :], w["pa"][l]).then_inc(lay_ld, 16)
                sp.wait_ge(lay_done, 2 * (l + 1))
                sp.dma_start(wcd[l], wc[:, :, :].rearrange("p a b -> p (a b)")).then_inc(lay_st, 16)
                sp.dma_start(pad[l], pa[:, :]).then_inc(lay_st, 16)
            sp.wait_ge(lay_st, 32 * LAYERS)

        @block.gpsimd
        def _(pool):
            nc.gpsimd.memset(zero[:, :], 0.0).then_inc(zeroed, 1)
            nc.gpsimd.memset(b1[:, :], 0.0).then_inc(zeroed, 1)
            nc.gpsimd.memset(m1[:, :], 0.0).then_inc(zeroed, 1)
            nc.gpsimd.memset(c["w1q"][:, :, :], 0.0).then_inc(zeroed, 1)
            nc.gpsimd.memset(c["ones"][:, :], 1.0).then_inc(zeroed, 1)
            nc.gpsimd.memset(onesq[:, :], 1.0).then_inc(zeroed, 1)

        @block.scalar
        def _(act):
            act.wait_ge(step, 2)
            nc.scalar.activation(v1[:, :], v1[:, :], ACT.Sqrt).then_inc(act_step, 1)
            nc.scalar.activation(v2[:, :], v2[:, :], ACT.Sqrt).then_inc(act_step, 1)
            nc.scalar.activation(ab[:, :], c["w1q"][:, :, :].rearrange("p a b -> p (a b)"), ACT.Abs,
                                 accum_out=asum[:, 0:1]).then_inc(act_step, 1)
            act.wait_ge(act_step, 3)
            nc.scalar.activation(ab[:, 0:FM * D], c["w2q"][:, :, :].rearrange("p a b -> p (a b)"), ACT.Abs,
                                 accum_out=asum[:, 1:2]).then_inc(act_step, 1)
            for l in range(LAYERS):
                act.wait_ge(lay_ld, 16 * 10 * (l + 1))
                nc.scalar.activation(pa[:, 0:MT * NS], pa[:, 0:MT * NS], ACT.Exp).then_inc(pa_exp, 1)

        @block.tensor
        def _(pe):
            pe.wait_ge(act_step, 4)
            pe.wait_ge(zeroed, 6)
            nc.tensor.matmul(tot[:, :], onesq[:, :], asum[:, :], start=True, stop=True).then_inc(summed, 1)

        @block.vector
        def _(dve):
            n = [0]

            def then(ins):
                n[0] += 1
                ins.then_inc(step, 1)
                dve.wait_ge(step, n[0])

            dve.wait_ge(loads, 16 * len(rows))
            then(nc.vector.tensor_scalar(v1[:, :], v1[:, :], EPS, None, ALU.add))
            then(nc.vector.tensor_scalar(v2[:, :], v2[:, :], EPS, None, ALU.add))
            dve.wait_ge(act_step, 2)
            ws, wd = c["ws"], c["wd"]
            then(nc.vector.reciprocal(v1[:, :], v1[:, :]))
            then(nc.vector.tensor_tensor(g1[:, :], g1[:, :], v1[:, :], ALU.mult))
            then(nc.vector.tensor_tensor(ws[:, :], ws[:, :], g1[:, :], ALU.mult))
            then(nc.vector.tensor_tensor(m1[:, :], m1[:, :], g1[:, :], ALU.mult))
            then(nc.vector.tensor_tensor(b1[:, :], b1[:, :], m1[:, :], ALU.subtract))
            then(nc.vector.tensor_tensor(ws[:, :], ws[:, :], b1[:, :], ALU.add))
            then(nc.vector.reciprocal(v2[:, :], v2[:, :]))
            then(nc.vector.tensor_tensor(g2[:, :], g2[:, :], v2[:, :], ALU.mult))
            then(nc.vector.tensor_tensor(wd[0:96, :, :], wd[0:96, :, :],
                                         g2[0:96, :].unsqueeze(1).to_broadcast([96, TAPS, D]), ALU.mult))
            then(nc.vector.tensor_tensor(wd[96:97, 0, :], wd[96:97, 0, :], g2[96:97, :], ALU.mult))
            then(nc.vector.tensor_tensor(m2[96:97, :], m2[96:97, :], g2[96:97, :], ALU.mult))
            then(nc.vector.tensor_tensor(b2[96:97, :], b2[96:97, :], m2[96:97, :], ALU.subtract))
            then(nc.vector.tensor_tensor(wd[96:97, 0, :], wd[96:97, 0, :], b2[96:97, :], ALU.add))
            then(nc.vector.tensor_tensor(c["base"][:, :, :], c["base"][:, :, :],
                                         offb[:, :].unsqueeze(1).to_broadcast([QP, 2, 32]), ALU.add))
            then(nc.vector.tensor_copy(c["sel"][:, :, :], self32[:, :, :]))
            dve.wait_ge(summed, 1)
            then(nc.vector.tensor_scalar(gam[:, :], tot[:, :], 1.0 / (FH * D), EPS, ALU.mult, ALU.add))
            then(nc.vector.tensor_scalar(half[:, :], gam[:, :], 0.5, None, ALU.mult))
            then(nc.vector.tensor_scalar(nhalf[:, :], gam[:, :], -0.5, None, ALU.mult))
            for i, q in enumerate((c["w1q"], c["w2q"])):
                q = q[:, :, :].rearrange("p a b -> p (a b)")
                k = q.shape[1]
                then(nc.vector.tensor_scalar(neg[:, 0:k], q, nhalf[:, i:i + 1], gam[:, i:i + 1], ALU.is_lt, ALU.mult))
                then(nc.vector.tensor_scalar(q, q, half[:, i:i + 1], gam[:, i:i + 1], ALU.is_gt, ALU.mult))
                then(nc.vector.tensor_tensor(q, q, neg[:, 0:k], ALU.subtract))
            for l in range(LAYERS):
                dve.wait_ge(lay_ld, 16 * 10 * (l + 1))
                dve.wait_ge(lay_st, 32 * l)
                nc.vector.tensor_tensor(wc[:, 0:4, :], cw[:, 0:4, :],
                                        wx[:, 0, :].unsqueeze(1).to_broadcast([128, 4, DI]), ALU.mult)
                nc.vector.tensor_tensor(wc[:, 4:6, :], cw[:, 4:6, :],
                                        wx[:, 1, :].unsqueeze(1).to_broadcast([128, 2, DI]),
                                        ALU.mult).then_inc(lay_done, 1)
                dve.wait_ge(pa_exp, l + 1)
                nc.vector.tensor_scalar(pa[:, 0:MT * NS], pa[:, 0:MT * NS], -1.0, None,
                                        ALU.mult).then_inc(lay_done, 1)


def tokens(nc, w, c, tab, h0, NB):
    with ExitStack() as ctx:
        sb = lambda n, s, d=F32: ctx.enter_context(nc.sbuf_tensor(n, s, d))
        ps = lambda n, s: ctx.enter_context(nc.psum_tensor(n, s, F32))
        sem = lambda n: ctx.enter_context(nc.semaphore(n))
        HR = HS // 2
        xh = [sb(f"xh{i}", [64, HR, 224]) for i in range(2)]
        hp = [sb(f"hp{i}", [112, HR, CO]) for i in range(2)]
        hc = sb("hc", [CO, HS * HS])
        lk = sb("lk", [112, 2, 480])
        G = [sb(f"G{i}", [QP, TAPS, 4, CO]) for i in range(2)]
        sk = [sb(f"sk{i}", [97, TAPS, QP]) for i in range(2)]
        pos = sb("pos", [QP, 64])
        fli = sb("fli", [QP, 64], I32)
        flo = sb("flo", [QP, 64])
        fgt = sb("fgt", [QP, 64])
        fr = sb("fr", [QP, 64])
        om = sb("om", [QP, 64])
        idf = sb("idf", [QP, 32])
        idx = [sb(f"idx{i}", [QP, 32], U32) for i in range(2)]
        wt = [sb(f"wt{i}", [QP, 32, 4]) for i in range(2)]
        lk2 = sb("lk2", [QP, 2, D])
        scr = sb("scr", [1, 2])
        ot = [sb(f"ot{i}", [QP, D]) for i in range(2)]
        pc = ps("pc", [128, 2, 512])
        po = ps("po", [128, 512])
        pt = ps("pt", [128, 2, 512])
        pd = ps("pd", [128, 2, 512])
        ready = sem("ready")
        x_ld = [sem(f"x_ld{i}") for i in range(2)]
        cv_full, cv_leak, cv_used = sem("cv_full"), sem("cv_leak"), sem("cv_used")
        tab_st = [sem(f"tab_st{i}") for i in range(2)]
        off_full, idx_done, dstep = sem("off_full"), sem("idx_done"), sem("dstep")
        g_done = [sem(f"g_done{i}") for i in range(2)]
        ip_step, ip_done = sem("ip_step"), sem("ip_done")
        tr_full, tr_used, dc_full, dc_leak, dc_used = (sem(n) for n in (
            "tr_full", "tr_used", "dc_full", "dc_leak", "dc_used"))
        ot_st = [sem(f"ot_st{i}") for i in range(2)]
        txt_st, mark = sem("txt_st"), sem("mark")
        x4 = w["x"].rearrange("b c (oh kh) w -> b c kh oh w", kh=4)
        slot = tab.rearrange("(s n) c -> s n c", s=2)
        hc5 = hc[:, :].rearrange("p (kh oh ow kw) -> p kh (oh ow) kw", kh=4, oh=GRID, kw=4)
        hcw = hc[:, :].rearrange("p (kh oh x) -> p oh kh x", kh=4, oh=GRID)
        PIX = [(0, 5), (5, 5), (10, 4)]
        ROWS = [(0, 8), (8, 8), (16, 8), (24, 4)]
        NCH = len(PIX) + len(ROWS)
        NCV = 2 * NCH

        def walk(eng, head, tail):
            head(0, 0)
            head(1, 1)
            tail(0, 0)
            if NB > 2:
                with eng.Fori(0, (NB - 2) // 2) as i:
                    head(2 * i + 2, 0)
                    tail(2 * i + 1, 1)
                    head(2 * i + 3, 1)
                    tail(2 * i + 2, 0)
            tail(NB - 1, 1)

        block = ctx.enter_context(nc.Block())

        @block.sync
        def _(sp):
            sp.dma_start(h0[:, NPOS:T, :], w["txt"]).then_inc(txt_st, 16)
            sp.wait_ge(ready, 5)

            def head(b, j):
                for hf in range(2):
                    if not isinstance(b, int) or b >= 1:
                        sp.wait_ge(cv_full, b * NCV - (1 - hf) * NCH)
                    for kw in range(4):
                        for ch in range(3):
                            p = kw * 12 + ch * 4
                            sp.dma_start(xh[hf][p:p + 4, :, 0:224 - kw],
                                         x4[b, ch, :, hf * HR:(hf + 1) * HR, kw:224]).then_inc(x_ld[hf], 16)
                sp.wait_ge(cv_used, b * NCV + NCH + len(PIX))
                for dy in range(2):
                    for dx in range(2):
                        ent = slot[j, :, (2 * dy + dx) * CO:(2 * dy + dx + 1) * CO]
                        ent = ent.rearrange("(y x) c -> y x c", y=PIT)[2 - dy:2 - dy + HS, 2 - dx:2 - dx + HS, :]
                        ent = ent.rearrange("(g r) x c -> r x g c", r=2)
                        for r in range(2):
                            sp.dma_start(ent[r], hp[j][r * HS:(r + 1) * HS, :, :]).then_inc(tab_st[j], 16)

            walk(sp, head, lambda b, j: None)
            sp.wait_ge(txt_st, 16)
            for j in range(2):
                sp.wait_ge(tab_st[j], 128 * (NB // 2))
                sp.wait_ge(ot_st[j], 16 * NB)

        @block.gpsimd
        def _(pool):
            nc.gpsimd.memset(scr[:, :], 1.0).then_inc(ready, 1)
            for i in range(2):
                nc.gpsimd.memset(xh[i][:, :, :], 1.0).then_inc(ready, 1)
                nc.gpsimd.memset(sk[i][96:97, :, :], 1.0).then_inc(ready, 1)

            pool.wait_ge(ready, 5)

            def tail(b, j):
                pool.wait_ge(idx_done, b + 1)
                pool.wait_ge(tab_st[j], (b // 2 + 1) * 128 if isinstance(b, int) else b * 64 + (128 - 64 * j))
                for t in range(2):
                    if not isinstance(b, int) or b >= 1:
                        pool.wait_ge(tr_full, (2 * b + t) * 4 - 4)
                    g = G[t][:, :, :, :].rearrange("p k a c -> p k (a c)")
                    pool.wait_ge(mark, 2 * b + t)
                    nc.gpsimd.tensor_tensor(scr[:, 1:2], scr[:, 0:1], scr[:, 0:1], ALU.mult).then_inc(mark, 1)
                    for k in range(TAPS):
                        nc.gpsimd.indirect_dma_start(
                            g[:, k, :], None, tab,
                            bass.IndirectOffsetOnAxis(ap=idx[j][:, t * TAPS + k:t * TAPS + k + 1], axis=0),
                        ).then_inc(g_done[t], 16)

            walk(pool, lambda b, j: None, tail)

        @block.tensor
        def _(pe):
            pe.wait_ge(ready, 5)
            ident = c["ident"]

            def head(b, j):
                n = 0
                for hf in range(2):
                    pe.wait_ge(x_ld[hf], (b + 1) * (16 * 12))
                    for g0, ng in PIX:
                        if not isinstance(b, int) or b * NCV + n >= 2:
                            pe.wait_ge(cv_used, b * NCV + n - 1)
                        for g in range(ng):
                            mm = nc.tensor.matmul(pc[0:112, n % 2, g * CO:(g + 1) * CO],
                                                  xh[hf][0:49, 2 * (g0 + g):2 * (g0 + g) + 2, 0:224:4],
                                                  c["ws"][:, :], start=True, stop=True)
                        mm.then_inc(cv_full, 1)
                        n += 1
                    for r0, nr in ROWS:
                        pe.wait_ge(cv_used, b * NCV + n - 1)
                        nc.tensor.matmul(pc[0:CO, n % 2, 0:nr * HS], c["ws"][:, :],
                                         xh[hf][0:49, r0:r0 + nr, 0:224:4],
                                         start=True, stop=True).then_inc(cv_full, 1)
                        n += 1
                pe.wait_ge(cv_used, (b + 1) * NCV)
                pe.wait_ge(idx_done, b)
                for t in range(2):
                    for k in range(TAPS):
                        mm = nc.tensor.matmul(po[0:QP, t * 32:(t + 1) * 32],
                                              hc5[:, k // 4, t * QP:(t + 1) * QP, k % 4], c["wo"][:, k, :],
                                              start=(k == 0), stop=(k == TAPS - 1))
                mm.then_inc(off_full, 1)

            def tail(b, j):
                for t in range(2):
                    pe.wait_ge(ip_done, 2 * b + t + 1)
                    for f in range(4):
                        n = (2 * b + t) * 4 + f
                        if not isinstance(b, int) or n >= 2:
                            pe.wait_ge(tr_used, n - 1)
                        for q in range(4):
                            mm = nc.tensor.transpose(pt[0:CO, f % 2, q * QP:(q + 1) * QP],
                                                     G[t][:, 4 * f + q, 0, :], ident[0:QP, 0:QP])
                        mm.then_inc(tr_full, 1)
                    pe.wait_ge(tr_used, (2 * b + t) * 4 + 4)
                    if not isinstance(b, int) or b >= 1:
                        pe.wait_ge(dc_used, 2 * b + t - 1)
                    for k in range(TAPS):
                        K = 97 if k == 0 else 96
                        mm = nc.tensor.matmul(pd[0:QP, t, 0:D], sk[t][0:K, k, :], c["wd"][0:K, k, :],
                                              start=(k == 0), stop=(k == TAPS - 1))
                    mm.then_inc(dc_full, 1)

            walk(pe, head, tail)

        @block.scalar
        def _(act):
            def head(b, j):
                n = 0
                for hf in range(2):
                    fills = [(112, ng * CO) for _, ng in PIX] + [(CO, nr * HS) for _, nr in ROWS]
                    for p, cols in fills:
                        act.wait_ge(cv_full, b * NCV + n + 1)
                        nc.scalar.activation(lk[0:p, n % 2, 0:cols], pc[0:p, n % 2, 0:cols], ACT.Copy,
                                             scale=SLOPE).then_inc(cv_leak, 1)
                        n += 1

            def tail(b, j):
                for t in range(2):
                    if not isinstance(b, int) or b >= 1:
                        act.wait_ge(dc_full, 2 * b + t - 1)
                    for f in range(4):
                        act.wait_ge(tr_full, (2 * b + t) * 4 + f + 1)
                        nc.scalar.activation(sk[t][0:CO, 4 * f:4 * f + 4, :],
                                             pt[0:CO, f % 2, 0:4 * QP].rearrange("p (a b) -> p a b", a=4),
                                             ACT.Copy).then_inc(tr_used, 1)
                    act.wait_ge(dc_full, 2 * b + t + 1)
                    nc.scalar.activation(lk2[:, t, :], pd[0:QP, t, 0:D], ACT.Copy,
                                         scale=SLOPE).then_inc(dc_leak, 1)
                    act.wait_ge(dc_used, 2 * b + t + 1)
                    act.dma_start(h0[b, t * QP:(t + 1) * QP, :], ot[t][:, :]).then_inc(ot_st[t], 16)

            walk(act, head, tail)

        @block.vector
        def _(dve):
            def head(b, j):
                n = 0
                if not isinstance(b, int) or b >= 2:
                    dve.wait_ge(tab_st[j], 64 * b - 64 * j)
                for hf in range(2):
                    for g0, ng in PIX:
                        dve.wait_ge(cv_leak, b * NCV + n + 1)
                        o = hp[j][:, hf * 14 + g0:hf * 14 + g0 + ng, :].rearrange("p g c -> p (g c)")
                        nc.vector.tensor_tensor(o, pc[0:112, n % 2, 0:ng * CO], lk[0:112, n % 2, 0:ng * CO],
                                                ALU.max).then_inc(cv_used, 1)
                        n += 1
                    for r0, nr in ROWS:
                        dve.wait_ge(cv_leak, b * NCV + n + 1)
                        if hf == 0 and r0 == 0:
                            dve.wait_ge(off_full, b)
                        o0 = (hf * HR + r0) // 4
                        rows = lambda ap: ap.rearrange("p (oh kh x) -> p oh kh x", kh=4, x=HS)
                        nc.vector.tensor_tensor(hcw[:, o0:o0 + nr // 4, :, :], rows(pc[0:CO, n % 2, 0:nr * HS]),
                                                rows(lk[0:CO, n % 2, 0:nr * HS]), ALU.max).then_inc(cv_used, 1)
                        n += 1
                m = [0]

                def then(ins):
                    m[0] += 1
                    ins.then_inc(dstep, 1)
                    dve.wait_ge(dstep, b * 10 + m[0])

                dve.wait_ge(off_full, b + 1)
                then(nc.vector.tensor_tensor(pos[:, :], po[0:QP, 0:64],
                                             c["base"][:, :, :].rearrange("p a b -> p (a b)"), ALU.add))
                then(nc.vector.tensor_scalar(pos[:, :], pos[:, :], -2.0, HS + 0.5, ALU.max, ALU.min))
                then(nc.vector.tensor_copy(fli[:, :], pos[:, :]))
                then(nc.vector.tensor_copy(flo[:, :], fli[:, :]))
                then(nc.vector.tensor_tensor(fgt[:, :], flo[:, :], pos[:, :], ALU.is_gt))
                then(nc.vector.tensor_tensor(flo[:, :], flo[:, :], fgt[:, :], ALU.subtract))
                then(nc.vector.tensor_tensor(fr[:, :], pos[:, :], flo[:, :], ALU.subtract))
                then(nc.vector.tensor_scalar(om[:, :], fr[:, :], -1.0, 1.0, ALU.mult, ALU.add))
                f2 = flo[:, :].rearrange("p (k a) -> p k a", a=2)
                r2 = fr[:, :].rearrange("p (k a) -> p k a", a=2)
                o2 = om[:, :].rearrange("p (k a) -> p k a", a=2)
                then(nc.vector.tensor_scalar(idf[:, :], f2[:, :, 0], float(PIT), float(2 * PIT + 2 + j * NENT),
                                             ALU.mult, ALU.add))
                then(nc.vector.tensor_tensor(idf[:, :], idf[:, :], f2[:, :, 1], ALU.add))
                nc.vector.tensor_copy(idx[j][:, :], idf[:, :])
                nc.vector.tensor_tensor(wt[j][:, :, 0], o2[:, :, 0], o2[:, :, 1], ALU.mult)
                nc.vector.tensor_tensor(wt[j][:, :, 1], o2[:, :, 0], r2[:, :, 1], ALU.mult)
                nc.vector.tensor_tensor(wt[j][:, :, 2], r2[:, :, 0], o2[:, :, 1], ALU.mult)
                nc.vector.tensor_tensor(wt[j][:, :, 3], r2[:, :, 0], r2[:, :, 1],
                                        ALU.mult).then_inc(idx_done, 1)

            def tail(b, j):
                for t in range(2):
                    dve.wait_ge(g_done[t], (b + 1) * (16 * TAPS))
                    g = G[t]
                    g3 = g[:, :, :, :].rearrange("p k a c -> p (k a) c")
                    wv = wt[j][:, t * TAPS:(t + 1) * TAPS, :].rearrange("p k a -> p (k a)")
                    nc.vector.tensor_tensor(g3, g3, wv.unsqueeze(2).to_broadcast([QP, 4 * TAPS, CO]),
                                            ALU.mult).then_inc(ip_step, 1)
                    dve.wait_ge(ip_step, (2 * b + t) * 2 + 1)
                    nc.vector.tensor_tensor(g[:, :, 0:2, :], g[:, :, 0:2, :], g[:, :, 2:4, :],
                                            ALU.add).then_inc(ip_step, 1)
                    dve.wait_ge(ip_step, (2 * b + t) * 2 + 2)
                    nc.vector.tensor_tensor(g[:, :, 0, :], g[:, :, 0, :], g[:, :, 1, :],
                                            ALU.add).then_inc(ip_done, 1)
                for t in range(2):
                    dve.wait_ge(dc_leak, 2 * b + t + 1)
                    dve.wait_ge(ot_st[t], 16 * b)
                    nc.vector.tensor_tensor(ot[t][:, :], pd[0:QP, t, 0:D], lk2[:, t, :],
                                            ALU.max).then_inc(dc_used, 1)

            walk(dve, head, tail)


NR = 4
FILLS = 12
PAIR_FILLS = 8 * FILLS


def mixer(nc, w, c, h0, wcd, pad, out, NB):
    with ExitStack() as ctx:
        sb = lambda n, s, d=F32: ctx.enter_context(nc.sbuf_tensor(n, s, d))
        ps = lambda n, s: ctx.enter_context(nc.psum_tensor(n, s, F32))
        sem = lambda n: ctx.enter_context(nc.semaphore(n))
        two = lambda n, s, d=F32: [sb(f"{n}{i}", s, d) for i in range(2)]
        ident = c["ident"]
        wc = sb("wct", [128, 6, DI])
        wz = sb("wz", [128, 2, DI])
        xpw = sb("xpw", [128, MT, XDR])
        dtw = sb("dtw", [128, DI])
        cdb = sb("cdb", [128, 2 * MT])
        ow = sb("ow", [128, MT, 256])
        pa = two("pa_", [128, MT * NS + MT])
        hw1, hw2 = sb("hw1", [128, 2, D]), sb("hw2", [128, 2, D])
        hb1, fb1 = sb("hb1", [128, 2]), sb("fb1", [128, FM])
        fb2 = sb("fb2", [1, D])
        sel = c["sel"]
        HT = two("HT", [TT, 3, D])
        X0, X1 = two("X0", [128, 276]), two("X1", [128, 277])
        XC, Z, DT, U, YF = (two(n, [128, MT, T]) for n in ("XC", "Z", "DT", "U", "YF"))
        XD = two("XD", [128, T])
        SP_ = two("SPL", [96, T], BF16)
        rem, unit = sb("rem", [96, T]), sb("unit", [96, T])
        AB = sb("AB", [128, MT, T])
        tiny, pause = sb("tiny", [1, 1]), sb("pause", [1, 1])
        dA = sb("dA", [128, NR, MT, T])
        bx = sb("bx", [128, 2, MT, T])
        hh = sb("hh", [128, 2, MT, T])
        hcr = sb("hcr", [128, 2, MT, T])
        st6, mv = sb("st6", [TT, 3, 6]), sb("mv", [TT, 3, 2])
        rs = sb("rs", [TT, 3])
        xn = sb("xn", [TT, 3, 256])
        xf = sb("xf", [128, 2, T])
        h1 = sb("h1", [128, 2, T])
        f1 = sb("f1", [128, FM, T])
        pY = ps("pY", [128, 1024])
        pB = ps("pB", [128, 512])
        pC = ps("pC", [128, 512])
        pF = ps("pF", [128, 2, 512])
        pQ = ps("pQ", [128, 2, 512])

        const_ld, zeroed = sem("const_ld"), sem("zeroed_m")
        front_ld, ow_ld = sem("front_ld"), sem("ow_ld")
        pa_ld = [sem(f"pa_ld{i}") for i in range(2)]
        ht_ld = [sem(f"ht_ld{i}") for i in range(2)]
        out_st = [sem(f"out_st{i}") for i in range(2)]
        fr_full, fr_used = sem("fr_full"), sem("fr_used")
        silu_x, silu_z = sem("silu_x"), sem("silu_z")
        dt_log, split_step, split_done, dt_done, u_done = (sem(n) for n in (
            "dt_log", "split_step", "split_done", "dt_done", "u_done"))
        ab_step = sem("ab_step")
        b_full, c_full, decay, bx_done, scan_done, hc_done, y_done = (sem(n) for n in (
            "b_full", "c_full", "decay", "bx_done", "scan_done", "hc_done", "y_done"))
        yf_part, yf_done, gated = sem("yf_part"), sem("yf_done"), sem("gated")
        q_full, q_act, q_dve = sem("q_full"), sem("q_act"), sem("q_dve")
        ln_step, ln_var, ln_sd, xn_done = (sem(n) for n in ("ln_step", "ln_var", "ln_sd", "xn_done"))

        consts = [(hw1[:, 0, :], w["head_w1"][0:KLO, :]), (hw1[0:KHI, 1, :], w["head_w1"][KLO:D, :]),
                  (hw2[:, 0, :], w["head_w2"][0:KLO, :]), (hw2[0:KHI, 1, :], w["head_w2"][KLO:D, :]),
                  (hw2[KHI:KHI + 1, 1, :], bcast(w["head_b2"], 1)),
                  (hb1[0:KLO, 0:1], w["head_b1"][0:KLO].unsqueeze(1)), (hb1[0:KHI, 1:2], w["head_b1"][KLO:D].unsqueeze(1)),
                  (fb1[:, :], w["ffn_b1"]), (fb2[:, :], bcast(w["ffn_b2"], 1))]
        FRONT_LD = 16 * 6
        NLN, NLNS = 4, 13
        QF, QA, QD = 36, 24, 12

        PRE, POST = "AA", "AADDDAAAAAAAADDD"
        Q = PRE + PRE + POST + POST
        assert (len(Q), Q.count("A"), Q.count("D")) == (QF, QA, QD)
        qbase = {("pre", 0): 0, ("pre", 1): 2, ("post", 0): 4, ("post", 1): 20}

        def wait_q_free(eng, p, n):
            a, d = (Q[:n - 1].count("A"), Q[:n - 1].count("D")) if n >= 2 else (0, 0)
            if n >= 2:
                k = Q[n - 2]
                eng.wait_ge(q_act if k == "A" else q_dve, p * (QA if k == "A" else QD) + (a if k == "A" else d))
            else:
                eng.wait_ge(q_dve, p * QD)

        def q_count(p, n, k):
            return p * (QA if k == "A" else QD) + Q[:n + 1].count(k)

        def fbase(p, k):
            if isinstance(k, int) and k < 1:
                return p * PAIR_FILLS + 10 * (k + 1)
            return p * PAIR_FILLS + k * FILLS + 8

        def steps(eng, first, step, last):
            with eng.Fori(0, NB // 2) as p:
                first(p)
                step(p, 0, 0, 0, False, True)
                with eng.Fori(0, LAYERS - 1) as l:
                    step(p, l, 2 * l + 1, 1, True, True)
                    step(p, l, 2 * l + 2, 0, True, True)
                step(p, LAYERS - 1, 7, 1, True, False)
                last(p)

        block = ctx.enter_context(nc.Block())

        @block.sync
        def _(sp):
            sp.wait_ge(zeroed, 7)
            for dst, src in consts:
                sp.dma_start(dst, src).then_inc(const_ld, 16)

            def load_front(l):
                for dst, src in ((wc[:, :, :].rearrange("p a b -> p (a b)"), wcd[l]),
                                 (wz[:, 0, :], w["in_z"][l, 0:KLO]), (wz[0:KHI, 1, :], w["in_z"][l, KLO:D]),
                                 (xpw[:, :, :], w["xp"][l]), (dtw[96:96 + RANK, :], w["dtw"][l]),
                                 (cdb[:, :], w["cdb"][l])):
                    sp.dma_start(dst, src).then_inc(front_ld, 16)

            with sp.Fori(0, NB // 2) as p:
                for s in range(2):
                    sp.wait_ge(out_st[s], p * 16)
                    sp.dma_start(HT[s][:, :, :], h0[2 * p + s].rearrange("(t q) d -> q t d", q=TT)).then_inc(ht_ld[s], 16)
                sp.wait_ge(fr_used, p * PAIR_FILLS)
                load_front(0)
                sp.dma_start(ow[:, :, :], w["ow"][0]).then_inc(ow_ld, 16)
                for s in range(2):
                    sp.dma_start(pa[s][:, :], pad[0]).then_inc(pa_ld[s], 16)
                with sp.Fori(0, LAYERS - 1) as l:
                    sp.wait_ge(fr_used, p * PAIR_FILLS + 20 + FILLS * 2 * l)
                    load_front(l + 1)
                    sp.wait_ge(yf_done, 8 * p + 2 * l + 1)
                    sp.dma_start(pa[0][:, :], pad[l + 1]).then_inc(pa_ld[0], 16)
                    sp.wait_ge(yf_done, 8 * p + 2 * l + 2)
                    sp.dma_start(pa[1][:, :], pad[l + 1]).then_inc(pa_ld[1], 16)
                    sp.wait_ge(fr_used, p * PAIR_FILLS + 20 + FILLS * (2 * l + 1) + 2)
                    sp.dma_start(ow[:, :, :], w["ow"][l + 1]).then_inc(ow_ld, 16)
                for s in range(2):
                    sp.wait_ge(q_dve, QD * p + 6 * s + 6)
                    sp.dma_start(out[2 * p + s].rearrange("(t q) d -> q t d", q=TT), HT[s][:, :, :]).then_inc(out_st[s], 16)
            for s in range(2):
                sp.wait_ge(out_st[s], 16 * (NB // 2))

        @block.gpsimd
        def _(pool):
            for i in range(2):
                nc.gpsimd.memset(X0[i][:, :], 0.0).then_inc(zeroed, 1)
                nc.gpsimd.memset(X1[i][:, :], 0.0).then_inc(zeroed, 1)
            nc.gpsimd.memset(dA[:, :, :, :], 0.0).then_inc(zeroed, 1)
            pool.wait_ge(zeroed, 5)
            nc.gpsimd.memset(h1[KHI:KHI + 1, 1, :], 1.0).then_inc(zeroed, 1)
            pool.wait_ge(zeroed, 6)
            nc.gpsimd.memset(unit[:, :], 1.0).then_inc(zeroed, 1)
            pool.wait_ge(zeroed, 7)

            def front(u, f, s):
                hi, x = SP_[s], XD[s]
                n = [0]

                def then(ins):
                    n[0] += 1
                    ins.then_inc(split_step, 1)
                    pool.wait_ge(split_step, u * 5 + n[0])

                pool.wait_ge(u_done, u)
                pool.wait_ge(fr_used, f)
                then(nc.gpsimd.tensor_tensor(hi[:, :], x[0:96, :], unit[:, :], ALU.mult))
                then(nc.gpsimd.tensor_tensor(rem[:, :], x[0:96, :], hi[:, :], ALU.subtract))
                then(nc.gpsimd.tensor_tensor(hi[32:64, :], rem[32:64, :], unit[32:64, :], ALU.mult))
                then(nc.gpsimd.tensor_tensor(hi[64:96, :], rem[64:96, :], unit[64:96, :], ALU.mult))
                then(nc.gpsimd.tensor_tensor(rem[64:96, :], rem[64:96, :], hi[64:96, :], ALU.subtract))
                nc.gpsimd.tensor_tensor(hi[64:96, :], rem[64:96, :], unit[64:96, :], ALU.mult).then_inc(split_done, 1)
                pool.wait_ge(split_done, u + 1)
                pool.wait_ge(dt_log, u + 1)
                nc.gpsimd.tensor_tensor(DT[s][:, :, :], DT[s][:, :, :], AB[:, :, :], ALU.add).then_inc(dt_done, 1)
                pool.wait_ge(dt_done, u + 1)
                nc.gpsimd.tensor_tensor(U[s][:, :, :], DT[s][:, :, :], XC[s][:, :, :], ALU.mult).then_inc(u_done, 1)

            def gate(v, s, units):
                pool.wait_ge(u_done, units)
                pool.wait_ge(yf_done, v + 1)
                pool.wait_ge(silu_z, v + 1)
                nc.gpsimd.tensor_tensor(YF[s][:, :, :], YF[s][:, :, :], Z[s][:, :, :], ALU.mult).then_inc(gated, 1)
                pool.wait_ge(gated, v + 1)

            def step(p, l, k, s, has_out, has_front):
                u = 8 * p + k
                if has_out:
                    gate(u - 1, 1 - s, u + 1)
                if has_front:
                    front(u + 1, fbase(p, k) + (2 if has_out else 0) + 5, 1 - s)

            steps(pool, lambda p: front(8 * p, fbase(p, -1) + 5, 0), step, lambda p: gate(8 * p + 7, 1, 8 * p + 8))

        @block.tensor
        def _(pe):
            pe.wait_ge(const_ld, 16 * len(consts))
            pe.wait_ge(zeroed, 7)

            def fill_free(f, n):
                pe.wait_ge(fr_used, f + n - (1 if n else 0))

            def out_mm(v, f, s):
                pe.wait_ge(gated, v + 1)
                for n in range(2):
                    fill_free(f, n)
                    for k in range(MT):
                        mm = nc.tensor.matmul(pF[:, n, 0:T], ow[:, k, n * 128:(n + 1) * 128], YF[s][:, k, :],
                                              start=(k == 0), stop=(k == MT - 1))
                    mm.then_inc(fr_full, 1)

            def conv_mm(u, f, s, m, half):
                if half == 0:
                    fill_free(f, m)
                o = pF[:, m % 2, 0:T]
                for j in ((0, 1, 2) if half == 0 else (3, 4, 5)):
                    rhs = X0[s][:, j:j + T] if j < 4 else X1[s][:, 3 - 2 * (j - 4):3 - 2 * (j - 4) + T]
                    mm = nc.tensor.matmul(o, wc[:, j, m * 128:(m + 1) * 128], rhs, start=(j == 0), stop=(j == 5))
                if half:
                    mm.then_inc(fr_full, 1)

            def z_mm(f, s, m, n):
                fill_free(f, n)
                o = pF[:, n % 2, 0:T]
                nc.tensor.matmul(o, wz[:, 0, m * 128:(m + 1) * 128], X0[s][:, 3:3 + T], start=True, stop=False)
                nc.tensor.matmul(o, wz[0:KHI, 1, m * 128:(m + 1) * 128], X1[s][0:KHI, 3:3 + T],
                                 start=False, stop=True).then_inc(fr_full, 1)

            def xp_mm(u, f, s, n):
                pe.wait_ge(silu_x, u + 1)
                fill_free(f, n)
                for k in range(MT):
                    mm = nc.tensor.matmul(pF[0:XDR, n % 2, 0:T], xpw[:, k, :], XC[s][:, k, :],
                                          start=(k == 0), stop=(k == MT - 1))
                mm.then_inc(fr_full, 1)

            def dt_mm(f, s, m, n, xp_fill):
                pe.wait_ge(fr_used, f + xp_fill + 1)
                fill_free(f, n)
                nc.tensor.matmul(pF[:, n % 2, 0:T], dtw[96:96 + RANK, m * 128:(m + 1) * 128],
                                 XD[s][96:96 + RANK, :], start=True, stop=True).then_inc(fr_full, 1)

            def front_mm(u, f, s, i):
                if 2 <= i < 8:
                    conv_mm(u, f, s, (i - 2) // 2, (i - 2) % 2)
                if i == 8:
                    z_mm(f, s, 0, 3)
                if i == 9:
                    xp_mm(u, f, s, 4)
                if i == 10:
                    z_mm(f, s, 1, 5)
                if i == 11:
                    dt_mm(f, s, 0, 6, 4)
                    dt_mm(f, s, 1, 7, 4)
                if i == 12:
                    dt_mm(f, s, 2, 8, 4)
                    z_mm(f, s, 2, 9)

            def b_mm(u, s, i):
                pe.wait_ge(bx_done, u * NS + i)
                nc.tensor.matmul(pB[:, 0:T], sel[:, i, :], SP_[s][:, :], start=True, stop=True).then_inc(b_full, 1)

            def c_mm(u, s, i):
                pe.wait_ge(hc_done, u * NS + i)
                nc.tensor.matmul(pC[:, 0:T], sel[:, NS + i, :], SP_[s][:, :], start=True, stop=True).then_inc(c_full, 1)

            def y_mm(u, i):
                pe.wait_ge(hc_done, u * NS + i + 1)
                if i == 0:
                    pe.wait_ge(yf_done, u)
                y = hcr[:, i % 2, :, :].rearrange("p m t -> p (m t)")
                nc.tensor.matmul(pY[:, 0:512], ident[:, :], y[:, 0:512], start=(i == 0), stop=(i == NS - 1))
                nc.tensor.matmul(pY[:, 512:NY], ident[:, :], y[:, 512:NY], start=(i == 0),
                                 stop=(i == NS - 1)).then_inc(y_done, 1)

            def step(p, l, k, s, has_out, has_front):
                u, f, o = 8 * p + k, fbase(p, k), 1 - s
                for i in range(NS):
                    if i < NS - 1:
                        b_mm(u, s, i + 1)
                    elif has_front:
                        pe.wait_ge(split_done, u + 2)
                        b_mm(u + 1, o, 0)
                    if i == 0 and has_out:
                        pe.wait_ge(ow_ld, 16 * (4 * p + l + 1) if has_front else 16 * (4 * p + LAYERS))
                        out_mm(u - 1, f, o)
                    if has_front:
                        if i == 1:
                            pe.wait_ge(front_ld, FRONT_LD * (4 * p + l + (2 if has_out else 1)))
                            if has_out:
                                pe.wait_ge(fr_used, f + 2)
                            else:
                                pe.wait_ge(q_act, q_count(p, 3, "A"))
                        front_mm(u + 1, f + (2 if has_out else 0), o, i)
                    y_mm(u, i)
                    if i < NS - 1:
                        c_mm(u, s, i + 1)
                    elif has_front:
                        c_mm(u + 1, o, 0)

            def turn(p, n):
                for h in range(2):
                    wait_q_free(pe, p, n + h)
                    for t in range(3):
                        mm = nc.tensor.transpose(pQ[:, (n + h) % 2, t * TT:(t + 1) * TT],
                                                 xn[:, t, h * 128:(h + 1) * 128], ident[0:TT, 0:TT])
                    mm.then_inc(q_full, 1)

            def first(p):
                for s in range(2):
                    pe.wait_ge(xn_done, 4 * p + s + 1)
                    turn(p, qbase["pre", s])
                pe.wait_ge(front_ld, FRONT_LD * (4 * p + 1))
                pe.wait_ge(q_act, q_count(p, 1, "A"))
                for i in range(NS):
                    front_mm(8 * p, fbase(p, -1), 0, i)
                pe.wait_ge(split_done, 8 * p + 1)
                b_mm(8 * p, 0, 0)
                c_mm(8 * p, 0, 0)

            def post(p, s):
                n = qbase["post", s]
                pe.wait_ge(fr_used, p * PAIR_FILLS + PAIR_FILLS - 2 + 2 * s)
                for m in range(2):
                    R = (KLO, KHI)[m]
                    wait_q_free(pe, p, n + m)
                    o = pQ[0:R, (n + m) % 2, 0:T]
                    nc.tensor.matmul(o, hw1[:, 0, m * 128:m * 128 + R], X0[s][:, 3:3 + T], start=True, stop=False)
                    nc.tensor.matmul(o, hw1[0:KHI, 1, m * 128:m * 128 + R], X1[s][0:KHI, 3:3 + T],
                                     start=False, stop=True).then_inc(q_full, 1)
                n += 2
                pe.wait_ge(q_act, q_count(p, n - 1, "A"))
                for t in range(3):
                    wait_q_free(pe, p, n + t)
                    o = pQ[0:TT, (n + t) % 2, 0:D]
                    nc.tensor.matmul(o, h1[:, 0, t * TT:(t + 1) * TT], hw2[:, 0, :], start=True, stop=False)
                    nc.tensor.matmul(o, h1[0:KHI + 1, 1, t * TT:(t + 1) * TT], hw2[0:KHI + 1, 1, :],
                                     start=False, stop=True).then_inc(q_full, 1)
                n += 3
                pe.wait_ge(xn_done, 4 * p + 2 + s + 1)
                turn(p, n)
                n += 2
                pe.wait_ge(q_act, q_count(p, n - 1, "A"))
                for m in range(FM):
                    wait_q_free(pe, p, n + m)
                    o = pQ[:, (n + m) % 2, 0:T]
                    nc.tensor.matmul(o, c["w1q"][:, 0, m * 128:(m + 1) * 128], xf[:, 0, :], start=True, stop=False)
                    nc.tensor.matmul(o, c["w1q"][0:KHI, 1, m * 128:(m + 1) * 128], xf[0:KHI, 1, :],
                                     start=False, stop=True).then_inc(q_full, 1)
                n += FM
                pe.wait_ge(q_act, q_count(p, n - 1, "A"))
                for t in range(3):
                    wait_q_free(pe, p, n + t)
                    o = pQ[0:TT, (n + t) % 2, 0:D]
                    for m in range(FM):
                        nc.tensor.matmul(o, f1[:, m, t * TT:(t + 1) * TT], c["w2q"][:, m, :], start=(m == 0), stop=False)
                    nc.tensor.matmul(o, c["ones"][:, 0:TT], fb2[:, :], start=False, stop=True).then_inc(q_full, 1)

            def last(p):
                out_mm(8 * p + 7, p * PAIR_FILLS + PAIR_FILLS - 2, 1)
                post(p, 0)
                post(p, 1)

            steps(pe, first, step, last)

        @block.scalar
        def _(act):
            act.wait_ge(const_ld, 16 * len(consts))
            act.wait_ge(zeroed, 7)

            def evac_out(f, s):
                act.wait_ge(fr_full, f + 1)
                nc.scalar.activation(X0[s][:, 3:3 + T], pF[:, 0, 0:T], ACT.Copy).then_inc(fr_used, 1)
                act.wait_ge(fr_full, f + 2)
                nc.scalar.activation(X1[s][0:KHI, 3:3 + T], pF[0:KHI, 1, 0:T], ACT.Copy)
                nc.scalar.activation(X1[s][KHI:128, 4:4 + T], pF[KHI:128, 1, 0:T], ACT.Copy).then_inc(fr_used, 1)

            def decays(u, s, i, fresh=False):
                if not fresh:
                    act.wait_ge(scan_done, u * NS + i - (NR - 1))
                for m in range(MT):
                    a = nc.scalar.activation(dA[:, i % NR, m, 1:T], DT[s][:, m, 1:T], ACT.Exp,
                                             scale=pa[s][:, m * NS + i:m * NS + i + 1])
                a.then_inc(decay, 1)

            def z_evac(f, s, m, n):
                act.wait_ge(fr_full, f + n + 1)
                nc.scalar.activation(Z[s][:, m, :], pF[:, n % 2, 0:T], ACT.Copy).then_inc(fr_used, 1)

            def do_silu_z(v, s, f_last):
                nc.scalar.activation(Z[s][:, :, :], Z[s][:, :, :], ACT.Silu).then_inc(silu_z, 1)

            def do_silu_x(f, s):
                act.wait_ge(fr_used, f + 3)
                nc.scalar.activation(XC[s][:, :, :], XC[s][:, :, :], ACT.Silu).then_inc(silu_x, 1)

            def ln_table():
                nc.scalar.activation(tiny[:, :], c["ones"][:, 0:1], ACT.Ln)

            def dt_evac(u, f, s, m, n):
                act.wait_ge(fr_full, f + n + 1)
                b = cdb[:, MT + m:MT + m + 1]
                nc.scalar.activation(AB[:, m, :], pF[:, n % 2, 0:T], ACT.Abs, bias=b)
                nc.scalar.activation(DT[s][:, m, :], pF[:, n % 2, 0:T], ACT.Relu, bias=b).then_inc(fr_used, 1)

            def front(u, f, s, i, z_of=None):
                if i in (4, 6, 8):
                    m = (i - 4) // 2
                    act.wait_ge(fr_full, f + m + 1)
                    nc.scalar.activation(XC[s][:, m, :], pF[:, m % 2, 0:T], ACT.Identity,
                                         bias=cdb[:, m:m + 1]).then_inc(fr_used, 1)
                if i == 8:
                    do_silu_x(f, s)
                    if z_of is not None:
                        do_silu_z(z_of, 1 - s, None)
                    ln_table()
                if i == 9:
                    z_evac(f, s, 0, 3)
                if i == 10:
                    act.wait_ge(fr_full, f + 5)
                    nc.scalar.activation(XD[s][0:XDR, :], pF[0:XDR, 0, 0:T], ACT.Copy).then_inc(fr_used, 1)
                if i == 11:
                    z_evac(f, s, 1, 5)
                if i == 12:
                    dt_evac(u, f, s, 0, 6)
                    dt_evac(u, f, s, 1, 7)
                if i == 13:
                    dt_evac(u, f, s, 2, 8)
                    z_evac(f, s, 2, 9)
                    act.wait_ge(fr_used, f + 10)
                    nc.scalar.activation(AB[:, :, :], AB[:, :, :], ACT.Exp, scale=-1.0).then_inc(ab_step, 1)
                    act.wait_ge(ab_step, u + 1)
                    nc.scalar.activation(AB[:, :, :], AB[:, :, :], ACT.Ln, bias=1.0).then_inc(dt_log, 1)

            def step(p, l, k, s, has_out, has_front):
                u, f, o = 8 * p + k, fbase(p, k), 1 - s
                for i in range(NS):
                    if i < NS - 2:
                        decays(u, s, i + 2, fresh=isinstance(k, int) and k == 0 and i + 2 < NR)
                    elif has_front:
                        if i == NS - 2:
                            act.wait_ge(dt_done, u + 2)
                            act.wait_ge(pa_ld[o], 16 * (4 * p + l + (2 if has_out else 1)))
                        decays(u + 1, o, i - (NS - 2))
                    if i == 1 and has_out:
                        evac_out(f, o)
                    if has_front:
                        if i == 4:
                            act.wait_ge(front_ld, FRONT_LD * (4 * p + l + (2 if has_out else 1)))
                        front(u + 1, f + (2 if has_out else 0), o, i, z_of=u)
                    elif i == 8:
                        act.wait_ge(fr_used, f)
                        do_silu_z(u, s, None)
                        ln_table()

            def sqrt_ln(g):
                act.wait_ge(ln_var, g + 1)
                nc.scalar.activation(rs[:, :], rs[:, :], ACT.Sqrt).then_inc(ln_sd, 1)

            def qwait(p, n):
                act.wait_ge(q_full, p * QF + n + 1)

            def first(p):
                for s in range(2):
                    sqrt_ln(4 * p + s)
                    n = qbase["pre", s]
                    qwait(p, n)
                    nc.scalar.activation(X0[s][:, 3:3 + T], pQ[:, 0, 0:T], ACT.Copy).then_inc(q_act, 1)
                    qwait(p, n + 1)
                    nc.scalar.activation(X1[s][0:KHI, 3:3 + T], pQ[0:KHI, 1, 0:T], ACT.Copy)
                    nc.scalar.activation(X1[s][KHI:128, 4:4 + T], pQ[KHI:128, 1, 0:T], ACT.Copy).then_inc(q_act, 1)
                act.wait_ge(front_ld, FRONT_LD * (4 * p + 1))
                for i in range(NS):
                    front(8 * p, fbase(p, -1), 0, i)
                act.wait_ge(dt_done, 8 * p + 1)
                act.wait_ge(pa_ld[0], 16 * (4 * p + 1))
                decays(8 * p, 0, 0, fresh=True)
                decays(8 * p, 0, 1, fresh=True)

            def post(p, s):
                n = qbase["post", s]
                for m in range(2):
                    R = (KLO, KHI)[m]
                    qwait(p, n + m)
                    nc.scalar.activation(h1[0:R, m, :], pQ[0:R, (n + m) % 2, 0:T], ACT.Relu,
                                         bias=hb1[0:R, m:m + 1]).then_inc(q_act, 1)
                sqrt_ln(4 * p + 2 + s)
                n += 5
                for m in range(2):
                    R = (KLO, KHI)[m]
                    qwait(p, n + m)
                    nc.scalar.activation(xf[0:R, m, :], pQ[0:R, (n + m) % 2, 0:T], ACT.Copy).then_inc(q_act, 1)
                n += 2
                for m in range(FM):
                    qwait(p, n + m)
                    nc.scalar.activation(f1[:, m, :], pQ[:, (n + m) % 2, 0:T], ACT.Gelu,
                                         bias=fb1[:, m:m + 1]).then_inc(q_act, 1)

            def last(p):
                evac_out(p * PAIR_FILLS + PAIR_FILLS - 2, 1)
                post(p, 0)
                post(p, 1)

            steps(act, first, step, last)

        @block.vector
        def _(dve):
            dve.wait_ge(zeroed, 7)

            def layernorm(g, s, dup):
                n = [0]

                def then(ins):
                    n[0] += 1
                    ins.then_inc(ln_step, 1)
                    dve.wait_ge(ln_step, g * 3 + n[0])

                for t in range(3):
                    last = nc.vector.bn_stats(st6[:, t, :], HT[s][:, t, :])
                then(last)
                nc.vector.memset(pause[:, :], 0.0)
                for t in range(3):
                    last = nc.vector.bn_aggr(mv[:, t, :], st6[:, t, :])
                then(last)
                nc.vector.tensor_scalar(rs[:, :], mv[:, :, 1], EPS, None, ALU.add).then_inc(ln_var, 1)
                dve.wait_ge(ln_sd, g + 1)
                then(nc.vector.reciprocal(rs[:, :], rs[:, :]))
                for t in range(3):
                    nc.vector.tensor_scalar(xn[:, t, 0:D], HT[s][:, t, :], mv[:, t, 0:1], rs[:, t:t + 1],
                                            ALU.subtract, ALU.mult)
                    last = nc.vector.tensor_scalar(xn[:, t, D:256], HT[s][:, t, KLO:D], mv[:, t, 0:1], rs[:, t:t + 1],
                                                   ALU.subtract, ALU.mult)
                last.then_inc(xn_done, 1)

            def bx_op(u, s, i):
                dve.wait_ge(b_full, u * NS + i + 1)
                nc.vector.tensor_tensor(bx[:, i % 2, :, :], U[s][:, :, :],
                                        pB[:, 0:T].unsqueeze(1).to_broadcast([128, MT, T]),
                                        ALU.mult).then_inc(bx_done, 1)

            def scan_op(u, s, i):
                dve.wait_ge(decay, u * NS + i + 1)
                dve.wait_ge(bx_done, u * NS + i + 1)
                flat = lambda t: t[:, :, :].rearrange("p m t -> p (m t)")
                nc.vector.tensor_tensor_scan(flat(hh[:, i % 2, :, :]), flat(dA[:, i % NR, :, :]),
                                             flat(bx[:, i % 2, :, :]), 0.0, ALU.mult, ALU.add).then_inc(scan_done, 1)

            def hc_op(u, s, i, fresh):
                dve.wait_ge(c_full, u * NS + i + 1)
                dve.wait_ge(scan_done, u * NS + i + 1)
                if not fresh:
                    dve.wait_ge(y_done, u * NS + i - 1)
                nc.vector.tensor_tensor(hcr[:, i % 2, :, :], hh[:, i % 2, :, :],
                                        pC[:, 0:T].unsqueeze(1).to_broadcast([128, MT, T]),
                                        ALU.mult).then_inc(hc_done, 1)

            def yf_op(v, s):
                dve.wait_ge(y_done, (v + 1) * NS)
                for m in range(MT):
                    last = nc.vector.scalar_tensor_tensor(out=YF[s][:, m, :], in0=XC[s][:, m, :],
                                                          scalar=pa[s][:, MT * NS + m:MT * NS + m + 1],
                                                          in1=pY[:, m * T:(m + 1) * T], op0=ALU.mult, op1=ALU.add)
                last.then_inc(yf_done, 1)

            def step(p, l, k, s, has_out, has_front):
                u, o = 8 * p + k, 1 - s
                for i in range(NS):
                    scan_op(u, s, i)
                    if i == 0 and has_out:
                        yf_op(u - 1, o)
                    if i < NS - 1:
                        bx_op(u, s, i + 1)
                    elif has_front:
                        dve.wait_ge(u_done, u + 2)
                        bx_op(u + 1, o, 0)
                    hc_op(u, s, i, isinstance(k, int) and k == 0 and i == 0)

            def first(p):
                for s in range(2):
                    dve.wait_ge(ht_ld[s], 16 * (p + 1))
                    if s:
                        dve.wait_ge(q_full, p * QF + 2)
                    layernorm(4 * p + s, s, True)
                dve.wait_ge(u_done, 8 * p + 1)
                dve.wait_ge(pa_ld[0], 16 * (4 * p + 1))
                bx_op(8 * p, 0, 0)

            def post(p, s):
                n = qbase["post", s]
                for t in range(3):
                    dve.wait_ge(q_full, p * QF + n + 2 + t + 1)
                    nc.vector.tensor_tensor(HT[s][:, t, :], pQ[0:TT, (n + 2 + t) % 2, 0:D], HT[s][:, t, :],
                                            ALU.add).then_inc(q_dve, 1)
                dve.wait_ge(q_dve, q_count(p, n + 4, "D"))
                layernorm(4 * p + 2 + s, s, False)
                for t in range(3):
                    dve.wait_ge(q_full, p * QF + n + 13 + t + 1)
                    nc.vector.tensor_tensor(HT[s][:, t, :], pQ[0:TT, (n + 13 + t) % 2, 0:D], HT[s][:, t, :],
                                            ALU.add).then_inc(q_dve, 1)

            def last(p):
                yf_op(8 * p + 7, 1)
                post(p, 0)
                post(p, 1)

            steps(dve, first, step, last)


def host_layouts(x):
    import numpy as np

    a = {}
    a["x"], a["txt"] = x["x"], x["txt"]
    stem = x["L0_tok_stem_w"].transpose(3, 1, 2, 0).reshape(48, CO)
    a["stem"] = np.concatenate([stem, x["L0_tok_stem_b"][None]], 0)
    for k in ("g", "b", "m", "v"):
        a[f"bn1_{k}"], a[f"bn2_{k}"] = x[f"L0_tok_bn1_{k}"], x[f"L0_tok_bn2_{k}"]
    a["dcn_w"] = x["L0_tok_dcn_w"].transpose(1, 2, 3, 0).reshape(CO, TAPS, D)
    a["dcn_b"] = x["L0_tok_dcn_b"]
    a["off_w"] = x["L0_tok_off_w"].transpose(1, 2, 3, 0).reshape(CO, TAPS, 32)
    a["off_b"] = x["L0_tok_off_b"]
    q, t, k = np.arange(QP)[:, None, None], np.arange(2)[None, :, None], np.arange(TAPS)[None, None, :]
    y = 4 * (7 * t + q // GRID) + k // 4
    xx = 4 * (q % GRID) + k % 4 + 0 * t
    a["base"] = np.stack(np.broadcast_arrays(y, xx), -1).reshape(QP, 2, 32).astype(np.float32)
    a["ident"] = np.eye(128, dtype=np.float32)
    sel = np.zeros((96, 2 * NS, 128), np.float32)
    for r in range(96):
        sel[r, r % 32, :] = 1
    a["sel"] = sel
    w = x["L0_attn_in_proj_w"]
    wx = w[:, :, :DI]
    a["in_x"] = np.stack([wx[:, 0:128], np.concatenate([wx[:, 128:], wx[:, 128:]], 1)], 2)
    a["in_z"] = w[:, :, DI:]
    a["conv_w"] = x["L0_attn_conv_w"].transpose(0, 2, 1)
    xp = x["L0_attn_x_proj_w"].reshape(LAYERS, MT, 128, RANK + 2 * NS).transpose(0, 2, 1, 3)
    bc = xp[..., RANK:]
    a["xp"] = np.concatenate([bc, bc, bc, xp[..., :RANK]], -1)
    a["dtw"] = x["L0_attn_dt_proj_w"]
    col = lambda v: v.reshape(LAYERS, MT, 128).transpose(0, 2, 1)
    a["cdb"] = np.concatenate([col(x["L0_attn_conv_b"]), col(x["L0_attn_dt_proj_b"])], -1)
    al = x["L0_attn_A_log"].reshape(LAYERS, MT, 128, NS).transpose(0, 2, 1, 3).reshape(LAYERS, 128, MT * NS)
    a["pa"] = np.concatenate([al, col(x["L0_attn_D"])], -1)
    o = x["L0_attn_out_proj_w"]
    o = np.concatenate([o, o[..., KLO:]], -1)
    a["ow"] = o.reshape(LAYERS, MT, 128, 256).transpose(0, 2, 1, 3)
    a["head_w1"], a["head_w2"] = x["L0_attn_head_w1"], x["L0_attn_head_w2"]
    a["head_b1"], a["head_b2"] = x["L0_attn_head_b1"], x["L0_attn_head_b2"]
    a["ffn_w1"] = x["L0_ffn_w1"].T
    a["ffn_w2"] = x["L0_ffn_w2"].T.reshape(FM, 128, D).transpose(1, 0, 2)
    a["ffn_b1"] = x["L0_ffn_b1"].reshape(FM, 128).T
    a["ffn_b2"] = x["L0_ffn_b2"]
    return {k: np.ascontiguousarray(v) for k, v in a.items()}


def kernel(**inputs):
    import numpy as np
    import concourse.bacc as bacc
    from concourse.bass_utils import run_bass_kernel_spmd

    arrays = host_layouts({k: np.asarray(v) for k, v in inputs.items()})
    nc = bacc.Bacc("TRN2", target_bir_lowering=False, num_devices=1)
    w = {k: nc.dram_tensor(f"in_{k}", v.shape, mybir.dt.from_np(v.dtype), kind="ExternalInput").ap()
         for k, v in arrays.items()}
    NB = arrays["x"].shape[0]
    out = nc.dram_tensor("out_0", [NB, T, D], F32, kind="ExternalOutput").ap()
    program(nc, w, out)
    r = run_bass_kernel_spmd(nc, [{f"in_{k}": v for k, v in arrays.items()}], core_ids=[0])
    return r.results[0]["out_0"]
```

```python
from contextlib import ExitStack

import concourse.bass as bass
from concourse import mybir

ALU = mybir.AluOpType
ACT = mybir.ActivationFunctionType
F32 = mybir.dt.float32
BF16 = mybir.dt.bfloat16
I32 = mybir.dt.int32
U32 = mybir.dt.uint32

EPS = 1e-5
SLOPE = 0.01
D = 192
KLO, KHI = 128, 64
DI = 384
MT = DI // 128
NS = 16
RANK = 12
LAYERS = 4
TXT = 77
GRID = 14
NPOS = GRID * GRID
T = NPOS + TXT
TT = T // 3
CO = 96
HS = 56
TAPS = 16
PIT = HS + 3
NENT = PIT * PIT
QP = NPOS // 2
FH = 768
FM = FH // 128
XDR = 96 + RANK
NY = MT * T


def bcast(ap, parts):
    return ap.unsqueeze(0).to_broadcast([parts] + list(ap.shape))


def program(nc, w, out):
    NB = w["x"].shape[0]
    tab = nc.dram_tensor("tab", [2 * NENT, 4 * CO], F32, kind="Internal").ap()
    h0 = nc.dram_tensor("h0", [NB, T, D], F32, kind="Internal").ap()
    wcd = nc.dram_tensor("wcd", [LAYERS, 128, 6 * DI], F32, kind="Internal").ap()
    pad = nc.dram_tensor("pad", [LAYERS, 128, MT * NS + MT], F32, kind="Internal").ap()
    with ExitStack() as keep:
        sb = lambda n, s, d=F32: keep.enter_context(nc.sbuf_tensor(n, s, d))
        c = dict(
            ident=sb("ident", [128, 128]), ones=sb("ones", [1, 128]),
            w1q=sb("w1q", [128, 2, FH]), w2q=sb("w2q", [128, FM, D]),
            ws=sb("ws", [49, CO]), wd=sb("wd", [97, TAPS, D]), wo=sb("wo", [CO, TAPS, 32]),
            base=sb("base", [QP, 2, 32]), sel=sb("sel", [96, 2 * NS, 128], BF16),
        )
        setup(nc, w, c, tab, wcd, pad)
        tokens(nc, w, c, tab, h0, NB)
        mixer(nc, w, c, h0, wcd, pad, out, NB)


def setup(nc, w, c, tab, wcd, pad):
    with ExitStack() as ctx:
        sb = lambda n, s, d=F32: ctx.enter_context(nc.sbuf_tensor(n, s, d))
        sem = lambda n: ctx.enter_context(nc.semaphore(n))
        zero = sb("zero", [118, 4 * CO])
        g1, v1, b1, m1 = (sb(n, [49, CO]) for n in ("g1", "v1", "b1", "m1"))
        g2, v2 = sb("g2", [97, D]), sb("v2", [97, D])
        b2, m2 = sb("b2", [97, D]), sb("m2", [97, D])
        offb = sb("offb", [QP, 32])
        self32 = sb("self32", [96, 2 * NS, 128])
        wx = sb("wx", [128, 2, DI])
        cw = sb("cw", [128, 6, DI])
        wc = sb("wc", [128, 6, DI])
        pa = sb("pa", [128, MT * NS + MT])
        ab = sb("ab", [128, 2 * FH])
        asum = sb("asum", [128, 2])
        gam = sb("gam", [128, 2])
        half = sb("half", [128, 2])
        nhalf = sb("nhalf", [128, 2])
        onesq = sb("onesq", [128, 128])
        neg = sb("neg", [128, 2 * FH])
        tot = ctx.enter_context(nc.psum_tensor("tot", [128, 2], F32))
        loads, zeroed, tabz = sem("loads"), sem("zeroed"), sem("tabz")
        step, act_step, summed = sem("step"), sem("act_step"), sem("summed")
        lay_ld, lay_done, lay_st = sem("lay_ld"), sem("lay_done"), sem("lay_st")
        pa_exp = sem("pa_exp")
        rows = [
            (c["ident"][:, :], w["ident"]), (c["ws"][:, :], w["stem"]),
            (g1[:, :], bcast(w["bn1_g"], 49)), (v1[:, :], bcast(w["bn1_v"], 49)),
            (b1[48:49, :], bcast(w["bn1_b"], 1)), (m1[48:49, :], bcast(w["bn1_m"], 1)),
            (c["wd"][0:96, :, :], w["dcn_w"]), (c["wd"][96:97, 0, :], bcast(w["dcn_b"], 1)),
            (g2[:, :], bcast(w["bn2_g"], 97)), (v2[:, :], bcast(w["bn2_v"], 97)),
            (b2[96:97, :], bcast(w["bn2_b"], 1)), (m2[96:97, :], bcast(w["bn2_m"], 1)),
            (c["wo"][:, :, :], w["off_w"]), (c["base"][:, :, :], w["base"]),
            (offb[:, :], bcast(w["off_b"], QP)),
            (c["w1q"][:, 0, :], w["ffn_w1"][0:KLO, :]), (c["w1q"][0:KHI, 1, :], w["ffn_w1"][KLO:D, :]),
            (c["w2q"][:, :, :], w["ffn_w2"]), (self32[:, :, :], w["sel"]),
        ]
        NZ = 2
        block = ctx.enter_context(nc.Block())

        @block.sync
        def _(sp):
            sp.wait_ge(zeroed, 5)
            for dst, src in rows:
                sp.dma_start(dst, src).then_inc(loads, 16)
            t = tab.rearrange("(n p) c -> n p c", p=118)
            for n in range(2 * NENT // 118):
                sp.dma_start(t[n], zero[:, :]).then_inc(tabz, 16)
            sp.wait_ge(tabz, 16 * (2 * NENT // 118))
            for l in range(LAYERS):
                sp.wait_ge(lay_st, 32 * l)
                sp.dma_start(wx[:, :, :], w["in_x"][l]).then_inc(lay_ld, 16)
                taps = w["conv_w"][l]
                for j in range(4):
                    sp.dma_start(cw[:, j, :], bcast(taps[j], 128)).then_inc(lay_ld, 16)
                for q in range(2):
                    sp.dma_start(cw[0:64, 4 + q, :], bcast(taps[3 - 2 * q], 64)).then_inc(lay_ld, 16)
                    sp.dma_start(cw[64:128, 4 + q, :], bcast(taps[2 - 2 * q], 64)).then_inc(lay_ld, 16)
                sp.dma_start(pa[:, :], w["pa"][l]).then_inc(lay_ld, 16)
                sp.wait_ge(lay_done, 2 * (l + 1))
                sp.dma_start(wcd[l], wc[:, :, :].rearrange("p a b -> p (a b)")).then_inc(lay_st, 16)
                sp.dma_start(pad[l], pa[:, :]).then_inc(lay_st, 16)
            sp.wait_ge(lay_st, 32 * LAYERS)

        @block.gpsimd
        def _(pool):
            nc.gpsimd.memset(zero[:, :], 0.0).then_inc(zeroed, 1)
            nc.gpsimd.memset(b1[:, :], 0.0).then_inc(zeroed, 1)
            nc.gpsimd.memset(m1[:, :], 0.0).then_inc(zeroed, 1)
            nc.gpsimd.memset(c["w1q"][:, :, :], 0.0).then_inc(zeroed, 1)
            nc.gpsimd.memset(c["ones"][:, :], 1.0).then_inc(zeroed, 1)
            nc.gpsimd.memset(onesq[:, :], 1.0).then_inc(zeroed, 1)

        @block.scalar
        def _(act):
            act.wait_ge(step, 2)
            nc.scalar.activation(v1[:, :], v1[:, :], ACT.Sqrt).then_inc(act_step, 1)
            nc.scalar.activation(v2[:, :], v2[:, :], ACT.Sqrt).then_inc(act_step, 1)
            nc.scalar.activation(ab[:, :], c["w1q"][:, :, :].rearrange("p a b -> p (a b)"), ACT.Abs,
                                 accum_out=asum[:, 0:1]).then_inc(act_step, 1)
            act.wait_ge(act_step, 3)
            nc.scalar.activation(ab[:, 0:FM * D], c["w2q"][:, :, :].rearrange("p a b -> p (a b)"), ACT.Abs,
                                 accum_out=asum[:, 1:2]).then_inc(act_step, 1)
            for l in range(LAYERS):
                act.wait_ge(lay_ld, 16 * 10 * (l + 1))
                nc.scalar.activation(pa[:, 0:MT * NS], pa[:, 0:MT * NS], ACT.Exp).then_inc(pa_exp, 1)

        @block.tensor
        def _(pe):
            pe.wait_ge(act_step, 4)
            pe.wait_ge(zeroed, 6)
            nc.tensor.matmul(tot[:, :], onesq[:, :], asum[:, :], start=True, stop=True).then_inc(summed, 1)

        @block.vector
        def _(dve):
            n = [0]

            def then(ins):
                n[0] += 1
                ins.then_inc(step, 1)
                dve.wait_ge(step, n[0])

            dve.wait_ge(loads, 16 * len(rows))
            then(nc.vector.tensor_scalar(v1[:, :], v1[:, :], EPS, None, ALU.add))
            then(nc.vector.tensor_scalar(v2[:, :], v2[:, :], EPS, None, ALU.add))
            dve.wait_ge(act_step, 2)
            ws, wd = c["ws"], c["wd"]
            then(nc.vector.reciprocal(v1[:, :], v1[:, :]))
            then(nc.vector.tensor_tensor(g1[:, :], g1[:, :], v1[:, :], ALU.mult))
            then(nc.vector.tensor_tensor(ws[:, :], ws[:, :], g1[:, :], ALU.mult))
            then(nc.vector.tensor_tensor(m1[:, :], m1[:, :], g1[:, :], ALU.mult))
            then(nc.vector.tensor_tensor(b1[:, :], b1[:, :], m1[:, :], ALU.subtract))
            then(nc.vector.tensor_tensor(ws[:, :], ws[:, :], b1[:, :], ALU.add))
            then(nc.vector.reciprocal(v2[:, :], v2[:, :]))
            then(nc.vector.tensor_tensor(g2[:, :], g2[:, :], v2[:, :], ALU.mult))
            then(nc.vector.tensor_tensor(wd[0:96, :, :], wd[0:96, :, :],
                                         g2[0:96, :].unsqueeze(1).to_broadcast([96, TAPS, D]), ALU.mult))
            then(nc.vector.tensor_tensor(wd[96:97, 0, :], wd[96:97, 0, :], g2[96:97, :], ALU.mult))
            then(nc.vector.tensor_tensor(m2[96:97, :], m2[96:97, :], g2[96:97, :], ALU.mult))
            then(nc.vector.tensor_tensor(b2[96:97, :], b2[96:97, :], m2[96:97, :], ALU.subtract))
            then(nc.vector.tensor_tensor(wd[96:97, 0, :], wd[96:97, 0, :], b2[96:97, :], ALU.add))
            then(nc.vector.tensor_tensor(c["base"][:, :, :], c["base"][:, :, :],
                                         offb[:, :].unsqueeze(1).to_broadcast([QP, 2, 32]), ALU.add))
            then(nc.vector.tensor_copy(c["sel"][:, :, :], self32[:, :, :]))
            dve.wait_ge(summed, 1)
            then(nc.vector.tensor_scalar(gam[:, :], tot[:, :], 1.0 / (FH * D), EPS, ALU.mult, ALU.add))
            then(nc.vector.tensor_scalar(half[:, :], gam[:, :], 0.5, None, ALU.mult))
            then(nc.vector.tensor_scalar(nhalf[:, :], gam[:, :], -0.5, None, ALU.mult))
            for i, q in enumerate((c["w1q"], c["w2q"])):
                q = q[:, :, :].rearrange("p a b -> p (a b)")
                k = q.shape[1]
                then(nc.vector.tensor_scalar(neg[:, 0:k], q, nhalf[:, i:i + 1], gam[:, i:i + 1], ALU.is_lt, ALU.mult))
                then(nc.vector.tensor_scalar(q, q, half[:, i:i + 1], gam[:, i:i + 1], ALU.is_gt, ALU.mult))
                then(nc.vector.tensor_tensor(q, q, neg[:, 0:k], ALU.subtract))
            for l in range(LAYERS):
                dve.wait_ge(lay_ld, 16 * 10 * (l + 1))
                dve.wait_ge(lay_st, 32 * l)
                nc.vector.tensor_tensor(wc[:, 0:4, :], cw[:, 0:4, :],
                                        wx[:, 0, :].unsqueeze(1).to_broadcast([128, 4, DI]), ALU.mult)
                nc.vector.tensor_tensor(wc[:, 4:6, :], cw[:, 4:6, :],
                                        wx[:, 1, :].unsqueeze(1).to_broadcast([128, 2, DI]),
                                        ALU.mult).then_inc(lay_done, 1)
                dve.wait_ge(pa_exp, l + 1)
                nc.vector.tensor_scalar(pa[:, 0:MT * NS], pa[:, 0:MT * NS], -1.0, None,
                                        ALU.mult).then_inc(lay_done, 1)


def tokens(nc, w, c, tab, h0, NB):
    with ExitStack() as ctx:
        sb = lambda n, s, d=F32: ctx.enter_context(nc.sbuf_tensor(n, s, d))
        ps = lambda n, s: ctx.enter_context(nc.psum_tensor(n, s, F32))
        sem = lambda n: ctx.enter_context(nc.semaphore(n))
        HR = HS // 2
        xh = [sb(f"xh{i}", [64, HR, 224]) for i in range(2)]
        hp = [sb(f"hp{i}", [112, HR, CO]) for i in range(2)]
        hc = sb("hc", [CO, HS * HS])
        lk = sb("lk", [112, 2, 480])
        G = [sb(f"G{i}", [QP, TAPS, 4, CO]) for i in range(2)]
        sk = [sb(f"sk{i}", [97, TAPS, QP]) for i in range(2)]
        pos = sb("pos", [QP, 64])
        fli = sb("fli", [QP, 64], I32)
        flo = sb("flo", [QP, 64])
        fgt = sb("fgt", [QP, 64])
        fr = sb("fr", [QP, 64])
        om = sb("om", [QP, 64])
        idf = sb("idf", [QP, 32])
        idx = [sb(f"idx{i}", [QP, 32], U32) for i in range(2)]
        wt = [sb(f"wt{i}", [QP, 32, 4]) for i in range(2)]
        lk2 = sb("lk2", [QP, 2, D])
        scr = sb("scr", [1, 2])
        ot = [sb(f"ot{i}", [QP, D]) for i in range(2)]
        pc = ps("pc", [128, 2, 512])
        po = ps("po", [128, 512])
        pt = ps("pt", [128, 2, 512])
        pd = ps("pd", [128, 2, 512])
        ready = sem("ready")
        x_ld = [sem(f"x_ld{i}") for i in range(2)]
        cv_full, cv_leak, cv_used = sem("cv_full"), sem("cv_leak"), sem("cv_used")
        tab_st = [sem(f"tab_st{i}") for i in range(2)]
        off_full, idx_done, dstep = sem("off_full"), sem("idx_done"), sem("dstep")
        g_done = [sem(f"g_done{i}") for i in range(2)]
        ip_step, ip_done = sem("ip_step"), sem("ip_done")
        tr_full, tr_used, dc_full, dc_leak, dc_used = (sem(n) for n in (
            "tr_full", "tr_used", "dc_full", "dc_leak", "dc_used"))
        ot_st = [sem(f"ot_st{i}") for i in range(2)]
        txt_st, mark = sem("txt_st"), sem("mark")
        x4 = w["x"].rearrange("b c (oh kh) w -> b c kh oh w", kh=4)
        slot = tab.rearrange("(s n) c -> s n c", s=2)
        hc5 = hc[:, :].rearrange("p (kh oh ow kw) -> p kh (oh ow) kw", kh=4, oh=GRID, kw=4)
        hcw = hc[:, :].rearrange("p (kh oh x) -> p oh kh x", kh=4, oh=GRID)
        PIX = [(0, 5), (5, 5), (10, 4)]
        ROWS = [(0, 8), (8, 8), (16, 8), (24, 4)]
        NCH = len(PIX) + len(ROWS)
        NCV = 2 * NCH

        def walk(eng, head, tail):
            head(0, 0)
            head(1, 1)
            tail(0, 0)
            if NB > 2:
                with eng.Fori(0, (NB - 2) // 2) as i:
                    head(2 * i + 2, 0)
                    tail(2 * i + 1, 1)
                    head(2 * i + 3, 1)
                    tail(2 * i + 2, 0)
            tail(NB - 1, 1)

        block = ctx.enter_context(nc.Block())

        @block.sync
        def _(sp):
            sp.dma_start(h0[:, NPOS:T, :], w["txt"]).then_inc(txt_st, 16)
            sp.wait_ge(ready, 5)

            def head(b, j):
                for hf in range(2):
                    if not isinstance(b, int) or b >= 1:
                        sp.wait_ge(cv_full, b * NCV - (1 - hf) * NCH)
                    for kw in range(4):
                        for ch in range(3):
                            p = kw * 12 + ch * 4
                            sp.dma_start(xh[hf][p:p + 4, :, 0:224 - kw],
                                         x4[b, ch, :, hf * HR:(hf + 1) * HR, kw:224]).then_inc(x_ld[hf], 16)
                sp.wait_ge(cv_used, b * NCV + NCH + len(PIX))
                for dy in range(2):
                    for dx in range(2):
                        ent = slot[j, :, (2 * dy + dx) * CO:(2 * dy + dx + 1) * CO]
                        ent = ent.rearrange("(y x) c -> y x c", y=PIT)[2 - dy:2 - dy + HS, 2 - dx:2 - dx + HS, :]
                        ent = ent.rearrange("(g r) x c -> r x g c", r=2)
                        for r in range(2):
                            sp.dma_start(ent[r], hp[j][r * HS:(r + 1) * HS, :, :]).then_inc(tab_st[j], 16)

            walk(sp, head, lambda b, j: None)
            sp.wait_ge(txt_st, 16)
            for j in range(2):
                sp.wait_ge(tab_st[j], 128 * (NB // 2))
                sp.wait_ge(ot_st[j], 16 * NB)

        @block.gpsimd
        def _(pool):
            nc.gpsimd.memset(scr[:, :], 1.0).then_inc(ready, 1)
            for i in range(2):
                nc.gpsimd.memset(xh[i][:, :, :], 1.0).then_inc(ready, 1)
                nc.gpsimd.memset(sk[i][96:97, :, :], 1.0).then_inc(ready, 1)

            pool.wait_ge(ready, 5)

            def tail(b, j):
                pool.wait_ge(idx_done, b + 1)
                pool.wait_ge(tab_st[j], (b // 2 + 1) * 128 if isinstance(b, int) else b * 64 + (128 - 64 * j))
                for t in range(2):
                    if not isinstance(b, int) or b >= 1:
                        pool.wait_ge(tr_full, (2 * b + t) * 4 - 4)
                    g = G[t][:, :, :, :].rearrange("p k a c -> p k (a c)")
                    pool.wait_ge(mark, 2 * b + t)
                    nc.gpsimd.tensor_tensor(scr[:, 1:2], scr[:, 0:1], scr[:, 0:1], ALU.mult).then_inc(mark, 1)
                    for k in range(TAPS):
                        nc.gpsimd.indirect_dma_start(
                            g[:, k, :], None, tab,
                            bass.IndirectOffsetOnAxis(ap=idx[j][:, t * TAPS + k:t * TAPS + k + 1], axis=0),
                        ).then_inc(g_done[t], 16)

            walk(pool, lambda b, j: None, tail)

        @block.tensor
        def _(pe):
            pe.wait_ge(ready, 5)
            ident = c["ident"]

            def head(b, j):
                n = 0
                for hf in range(2):
                    pe.wait_ge(x_ld[hf], (b + 1) * (16 * 12))
                    for g0, ng in PIX:
                        if not isinstance(b, int) or b * NCV + n >= 2:
                            pe.wait_ge(cv_used, b * NCV + n - 1)
                        for g in range(ng):
                            mm = nc.tensor.matmul(pc[0:112, n % 2, g * CO:(g + 1) * CO],
                                                  xh[hf][0:49, 2 * (g0 + g):2 * (g0 + g) + 2, 0:224:4],
                                                  c["ws"][:, :], start=True, stop=True)
                        mm.then_inc(cv_full, 1)
                        n += 1
                    for r0, nr in ROWS:
                        pe.wait_ge(cv_used, b * NCV + n - 1)
                        nc.tensor.matmul(pc[0:CO, n % 2, 0:nr * HS], c["ws"][:, :],
                                         xh[hf][0:49, r0:r0 + nr, 0:224:4],
                                         start=True, stop=True).then_inc(cv_full, 1)
                        n += 1
                pe.wait_ge(cv_used, (b + 1) * NCV)
                pe.wait_ge(idx_done, b)
                for t in range(2):
                    for k in range(TAPS):
                        mm = nc.tensor.matmul(po[0:QP, t * 32:(t + 1) * 32],
                                              hc5[:, k // 4, t * QP:(t + 1) * QP, k % 4], c["wo"][:, k, :],
                                              start=(k == 0), stop=(k == TAPS - 1))
                mm.then_inc(off_full, 1)

            def tail(b, j):
                for t in range(2):
                    pe.wait_ge(ip_done, 2 * b + t + 1)
                    for f in range(4):
                        n = (2 * b + t) * 4 + f
                        if not isinstance(b, int) or n >= 2:
                            pe.wait_ge(tr_used, n - 1)
                        for q in range(4):
                            mm = nc.tensor.transpose(pt[0:CO, f % 2, q * QP:(q + 1) * QP],
                                                     G[t][:, 4 * f + q, 0, :], ident[0:QP, 0:QP])
                        mm.then_inc(tr_full, 1)
                    pe.wait_ge(tr_used, (2 * b + t) * 4 + 4)
                    if not isinstance(b, int) or b >= 1:
                        pe.wait_ge(dc_used, 2 * b + t - 1)
                    for k in range(TAPS):
                        K = 97 if k == 0 else 96
                        mm = nc.tensor.matmul(pd[0:QP, t, 0:D], sk[t][0:K, k, :], c["wd"][0:K, k, :],
                                              start=(k == 0), stop=(k == TAPS - 1))
                    mm.then_inc(dc_full, 1)

            walk(pe, head, tail)

        @block.scalar
        def _(act):
            def head(b, j):
                n = 0
                for hf in range(2):
                    fills = [(112, ng * CO) for _, ng in PIX] + [(CO, nr * HS) for _, nr in ROWS]
                    for p, cols in fills:
                        act.wait_ge(cv_full, b * NCV + n + 1)
                        nc.scalar.activation(lk[0:p, n % 2, 0:cols], pc[0:p, n % 2, 0:cols], ACT.Copy,
                                             scale=SLOPE).then_inc(cv_leak, 1)
                        n += 1

            def tail(b, j):
                for t in range(2):
                    if not isinstance(b, int) or b >= 1:
                        act.wait_ge(dc_full, 2 * b + t - 1)
                    for f in range(4):
                        act.wait_ge(tr_full, (2 * b + t) * 4 + f + 1)
                        nc.scalar.activation(sk[t][0:CO, 4 * f:4 * f + 4, :],
                                             pt[0:CO, f % 2, 0:4 * QP].rearrange("p (a b) -> p a b", a=4),
                                             ACT.Copy).then_inc(tr_used, 1)
                    act.wait_ge(dc_full, 2 * b + t + 1)
                    nc.scalar.activation(lk2[:, t, :], pd[0:QP, t, 0:D], ACT.Copy,
                                         scale=SLOPE).then_inc(dc_leak, 1)
                    act.wait_ge(dc_used, 2 * b + t + 1)
                    act.dma_start(h0[b, t * QP:(t + 1) * QP, :], ot[t][:, :]).then_inc(ot_st[t], 16)

            walk(act, head, tail)

        @block.vector
        def _(dve):
            def head(b, j):
                n = 0
                if not isinstance(b, int) or b >= 2:
                    dve.wait_ge(tab_st[j], 64 * b - 64 * j)
                for hf in range(2):
                    for g0, ng in PIX:
                        dve.wait_ge(cv_leak, b * NCV + n + 1)
                        o = hp[j][:, hf * 14 + g0:hf * 14 + g0 + ng, :].rearrange("p g c -> p (g c)")
                        nc.vector.tensor_tensor(o, pc[0:112, n % 2, 0:ng * CO], lk[0:112, n % 2, 0:ng * CO],
                                                ALU.max).then_inc(cv_used, 1)
                        n += 1
                    for r0, nr in ROWS:
                        dve.wait_ge(cv_leak, b * NCV + n + 1)
                        if hf == 0 and r0 == 0:
                            dve.wait_ge(off_full, b)
                        o0 = (hf * HR + r0) // 4
                        rows = lambda ap: ap.rearrange("p (oh kh x) -> p oh kh x", kh=4, x=HS)
                        nc.vector.tensor_tensor(hcw[:, o0:o0 + nr // 4, :, :], rows(pc[0:CO, n % 2, 0:nr * HS]),
                                                rows(lk[0:CO, n % 2, 0:nr * HS]), ALU.max).then_inc(cv_used, 1)
                        n += 1
                m = [0]

                def then(ins):
                    m[0] += 1
                    ins.then_inc(dstep, 1)
                    dve.wait_ge(dstep, b * 10 + m[0])

                dve.wait_ge(off_full, b + 1)
                then(nc.vector.tensor_tensor(pos[:, :], po[0:QP, 0:64],
                                             c["base"][:, :, :].rearrange("p a b -> p (a b)"), ALU.add))
                then(nc.vector.tensor_scalar(pos[:, :], pos[:, :], -2.0, HS + 0.5, ALU.max, ALU.min))
                then(nc.vector.tensor_copy(fli[:, :], pos[:, :]))
                then(nc.vector.tensor_copy(flo[:, :], fli[:, :]))
                then(nc.vector.tensor_tensor(fgt[:, :], flo[:, :], pos[:, :], ALU.is_gt))
                then(nc.vector.tensor_tensor(flo[:, :], flo[:, :], fgt[:, :], ALU.subtract))
                then(nc.vector.tensor_tensor(fr[:, :], pos[:, :], flo[:, :], ALU.subtract))
                then(nc.vector.tensor_scalar(om[:, :], fr[:, :], -1.0, 1.0, ALU.mult, ALU.add))
                f2 = flo[:, :].rearrange("p (k a) -> p k a", a=2)
                r2 = fr[:, :].rearrange("p (k a) -> p k a", a=2)
                o2 = om[:, :].rearrange("p (k a) -> p k a", a=2)
                then(nc.vector.tensor_scalar(idf[:, :], f2[:, :, 0], float(PIT), float(2 * PIT + 2 + j * NENT),
                                             ALU.mult, ALU.add))
                then(nc.vector.tensor_tensor(idf[:, :], idf[:, :], f2[:, :, 1], ALU.add))
                nc.vector.tensor_copy(idx[j][:, :], idf[:, :])
                nc.vector.tensor_tensor(wt[j][:, :, 0], o2[:, :, 0], o2[:, :, 1], ALU.mult)
                nc.vector.tensor_tensor(wt[j][:, :, 1], o2[:, :, 0], r2[:, :, 1], ALU.mult)
                nc.vector.tensor_tensor(wt[j][:, :, 2], r2[:, :, 0], o2[:, :, 1], ALU.mult)
                nc.vector.tensor_tensor(wt[j][:, :, 3], r2[:, :, 0], r2[:, :, 1],
                                        ALU.mult).then_inc(idx_done, 1)

            def tail(b, j):
                for t in range(2):
                    dve.wait_ge(g_done[t], (b + 1) * (16 * TAPS))
                    g = G[t]
                    g3 = g[:, :, :, :].rearrange("p k a c -> p (k a) c")
                    wv = wt[j][:, t * TAPS:(t + 1) * TAPS, :].rearrange("p k a -> p (k a)")
                    nc.vector.tensor_tensor(g3, g3, wv.unsqueeze(2).to_broadcast([QP, 4 * TAPS, CO]),
                                            ALU.mult).then_inc(ip_step, 1)
                    dve.wait_ge(ip_step, (2 * b + t) * 2 + 1)
                    nc.vector.tensor_tensor(g[:, :, 0:2, :], g[:, :, 0:2, :], g[:, :, 2:4, :],
                                            ALU.add).then_inc(ip_step, 1)
                    dve.wait_ge(ip_step, (2 * b + t) * 2 + 2)
                    nc.vector.tensor_tensor(g[:, :, 0, :], g[:, :, 0, :], g[:, :, 1, :],
                                            ALU.add).then_inc(ip_done, 1)
                for t in range(2):
                    dve.wait_ge(dc_leak, 2 * b + t + 1)
                    dve.wait_ge(ot_st[t], 16 * b)
                    nc.vector.tensor_tensor(ot[t][:, :], pd[0:QP, t, 0:D], lk2[:, t, :],
                                            ALU.max).then_inc(dc_used, 1)

            walk(dve, head, tail)


NR = 4
FILLS = 12
ONE = 1


def mixer(nc, w, c, h0, wcd, pad, out, NB):
    with ExitStack() as ctx:
        sb = lambda n, s, d=F32: ctx.enter_context(nc.sbuf_tensor(n, s, d))
        ps = lambda n, s: ctx.enter_context(nc.psum_tensor(n, s, F32))
        sem = lambda n: ctx.enter_context(nc.semaphore(n))
        two = lambda n, s, d=F32: [sb(f"{n}{i}", s, d) for i in range(2)]
        NP = NB // 2
        UNITS = 8 * NP
        ident, sel = c["ident"], c["sel"]
        wc = sb("wct", [128, 6, DI])
        wz = sb("wz", [128, 2, DI])
        xpw = sb("xpw", [128, MT, XDR])
        dtw = sb("dtw", [128, DI])
        cdb = sb("cdb", [128, 2 * MT])
        ow = sb("ow", [128, MT, 256])
        pa = two("pa_", [128, MT * NS + MT])
        hw1, hw2 = sb("hw1", [128, 2, D]), sb("hw2", [128, 2, D])
        hb1, fb1 = sb("hb1", [128, 2]), sb("fb1", [128, FM])
        fb2 = sb("fb2", [1, D])
        HI, HT = two("HI", [TT, 3, D]), two("HT", [TT, 3, D])
        OT = sb("OT", [TT, 3, D])
        X0, X1 = two("X0", [128, 276]), two("X1", [128, 277])
        XC, Z, DT, U, YF = (two(n, [128, MT, T]) for n in ("XC", "Z", "DT", "U", "YF"))
        XD = two("XD", [128, T])
        SPL = two("SPL", [96, T], BF16)
        rem, unit = sb("rem", [96, T]), sb("unit", [96, T])
        AB = sb("AB", [128, MT, T])
        tiny, pause, pool_one = sb("tiny", [1, 2]), sb("pause", [1, 4]), sb("pool_one", [1, 1])
        dA = sb("dA", [128, NR, MT, T])
        bx = sb("bx", [128, 2, MT, T])
        hh = sb("hh", [128, 2, MT, T])
        hcr = sb("hcr", [128, 2, MT, T])
        st6, mv = sb("st6", [TT, 3, 6]), sb("mv", [TT, 3, 2])
        var, lg, rs, nt = (sb(n, [TT, 3]) for n in ("var", "lg", "rs", "nt"))
        xn = sb("xn", [TT, 3, 256])
        xf = sb("xf", [128, 2, T])
        h1 = sb("h1", [128, 2, T])
        f1 = sb("f1", [128, FM, T])
        pY = ps("pY", [128, 1024])
        pB = ps("pB", [128, 512])
        pC = ps("pC", [128, 512])
        pF = ps("pF", [128, 2, 512])
        pQ = ps("pQ", [128, 2, 512])

        const_ld, zeroed = sem("const_ld"), sem("zeroed_m")
        front_ld, ow_ld = sem("front_ld"), sem("ow_ld")
        pa_ld = [sem(f"pa_ld{i}") for i in range(2)]
        hi_ld = [sem(f"hi_ld{i}") for i in range(2)]
        out_st = sem("out_st")
        fr_full, fr_used = sem("fr_full"), sem("fr_used")
        silu_x, silu_z = sem("silu_x"), sem("silu_z")
        dt_log, split_step, split_done, dt_done, u_done = (sem(n) for n in (
            "dt_log", "split_step", "split_done", "dt_done", "u_done"))
        ab_step = sem("ab_step")
        b_full, c_full, decay, bx_done, scan_done, hc_done, y_done = (sem(n) for n in (
            "b_full", "c_full", "decay", "bx_done", "scan_done", "hc_done", "y_done"))
        yf_done, gated = sem("yf_done"), sem("gated")
        q_full, q_act, q_dve = sem("q_full"), sem("q_act"), sem("q_dve")
        f1_done, ot_done, hi_used = sem("f1_done"), sem("ot_done"), sem("hi_used")
        ln_step, ln_var, ln_log, ln_exp, xn_done = (sem(n) for n in (
            "ln_step", "ln_var", "ln_log", "ln_exp", "xn_done"))

        consts = [(hw1[:, 0, :], w["head_w1"][0:KLO, :]), (hw1[0:KHI, 1, :], w["head_w1"][KLO:D, :]),
                  (hw2[:, 0, :], w["head_w2"][0:KLO, :]), (hw2[0:KHI, 1, :], w["head_w2"][KLO:D, :]),
                  (hw2[KHI:KHI + 1, 1, :], bcast(w["head_b2"], 1)),
                  (hb1[0:KLO, 0:1], w["head_b1"][0:KLO].unsqueeze(1)), (hb1[0:KHI, 1:2], w["head_b1"][KLO:D].unsqueeze(1)),
                  (fb1[:, :], w["ffn_b1"]), (fb2[:, :], bcast(w["ffn_b2"], 1))]
        FRONT_LD = 16 * 6
        LN_STEPS = 6

        QSEQ = "AA" + "AA" + "DDD" + "AA" + "A" * FM + "DDD"
        QEND = "AA" + "DDD" + "AA" + "A" * FM + "DDD"
        TURNS = 4

        class Turn:

            def __init__(self, s, pair, fills, act, dve, norms, seq, nth):
                self.s, self.pair, self.fills, self.act, self.dve, self.norms = s, pair, fills, act, dve, norms
                self.seq, self.nth = seq, nth
                self.pre = 2 if seq == QSEQ else 0

            def count(self, n, kind):
                return (self.act if kind == "A" else ONE + self.dve) + self.seq[:n + 1].count(kind)

        def turn_of(p, s):
            m = 2 * p + s
            return Turn(s, p, TURNS + len(QSEQ) * m, TURNS + QSEQ.count("A") * m, QSEQ.count("D") * m, 2 + 2 * m, QSEQ, m)

        def end_of(s):
            p = NP - 1
            m = 2 * p
            return Turn(s, p, TURNS + len(QSEQ) * m + len(QEND) * s, TURNS + QSEQ.count("A") * m + QEND.count("A") * s,
                        QSEQ.count("D") * m + QEND.count("D") * s, 2 + 2 * m + s, QEND, m + s)

        def steps(eng, enter, step, leave):
            enter()
            step(0, 0, 0, 0, False, True, None)

            def middle(p):
                with eng.Fori(0, LAYERS - 1) as l:
                    step(8 * p + 2 * l + 1, 1, p, l + 1, True, True, None)
                    step(8 * p + 2 * l + 2, 0, p, l + 1, True, True, None)

            if NP > 1:
                with eng.Fori(0, NP - 1) as p:
                    middle(p)
                    step(8 * p + 7, 1, p + 1, 0, True, True, turn_of(p, 0))
                    step(8 * p + 8, 0, p + 1, 0, True, True, turn_of(p, 1))
            middle(NP - 1)
            step(UNITS - 1, 1, 0, 0, True, False, end_of(0))
            leave(end_of(1))

        def fbase(u):
            return FILLS * u + 8

        LAST_OUT = fbase(UNITS - 1) + 2

        block = ctx.enter_context(nc.Block())

        @block.sync
        def _(sp):
            sp.wait_ge(zeroed, 7)
            for n, (dst, src) in enumerate(consts):
                sp.dma_start(dst, src).then_inc(const_ld if n < len(consts) - 1 else out_st, 16)

            def load_front(l):
                for dst, src in ((wc[:, :, :].rearrange("p a b -> p (a b)"), wcd[l]),
                                 (wz[:, 0, :], w["in_z"][l, 0:KLO]), (wz[0:KHI, 1, :], w["in_z"][l, KLO:D]),
                                 (xpw[:, :, :], w["xp"][l]), (dtw[96:96 + RANK, :], w["dtw"][l]),
                                 (cdb[:, :], w["cdb"][l])):
                    sp.dma_start(dst, src).then_inc(front_ld, 16)

            def load_h(n, s):
                sp.dma_start(HI[s][:, :, :], h0[n].rearrange("(t q) d -> q t d", q=TT)).then_inc(hi_ld[s], 16)

            def store(n, nth):
                sp.wait_ge(ot_done, nth + 1)
                sp.dma_start(out[n].rearrange("(t q) d -> q t d", q=TT), OT[:, :, :]).then_inc(out_st, 16)

            def layers(p, u):
                with sp.Fori(0, LAYERS - 1) as l:
                    sp.wait_ge(fr_used, ONE + fbase(8 * p + 2 * l + 1))
                    load_front(l + 1)
                    sp.wait_ge(yf_done, ONE + 8 * p + 2 * l + 1)
                    sp.dma_start(pa[0][:, :], pad[l + 1]).then_inc(pa_ld[0], 16)
                    sp.wait_ge(yf_done, ONE + 8 * p + 2 * l + 2)
                    sp.dma_start(pa[1][:, :], pad[l + 1]).then_inc(pa_ld[1], 16)
                    sp.wait_ge(fr_used, ONE + fbase(8 * p + 2 * l + 2) + 2)
                    sp.dma_start(ow[:, :, :], w["ow"][l + 1]).then_inc(ow_ld, 16)

            for s in range(2):
                load_h(s, s)
            load_front(0)
            sp.dma_start(ow[:, :, :], w["ow"][0]).then_inc(ow_ld, 16)
            for s in range(2):
                sp.dma_start(pa[s][:, :], pad[0]).then_inc(pa_ld[s], 16)
            if NP > 1:
                with sp.Fori(0, NP - 1) as p:
                    for s in range(2):
                        sp.wait_ge(hi_used, 2 * p + s + 1)
                        load_h(2 * p + 2 + s, s)
                    layers(p, 8 * p)
                    sp.wait_ge(fr_used, ONE + fbase(8 * p + 7))
                    load_front(0)
                    sp.wait_ge(yf_done, ONE + 8 * p + 7)
                    sp.dma_start(pa[0][:, :], pad[0]).then_inc(pa_ld[0], 16)
                    store(2 * p, 2 * p)
                    sp.wait_ge(yf_done, ONE + 8 * p + 8)
                    sp.dma_start(pa[1][:, :], pad[0]).then_inc(pa_ld[1], 16)
                    sp.wait_ge(fr_used, ONE + fbase(8 * p + 8) + 2)
                    sp.dma_start(ow[:, :, :], w["ow"][0]).then_inc(ow_ld, 16)
                    store(2 * p + 1, 2 * p + 1)
            layers(NP - 1, UNITS - 8)
            store(NB - 2, NB - 2)
            store(NB - 1, NB - 1)
            sp.wait_ge(out_st, 16 * (NB + 1))

        @block.gpsimd
        def _(pool):
            for i in range(2):
                nc.gpsimd.memset(X0[i][:, :], 0.0).then_inc(zeroed, 1)
                nc.gpsimd.memset(X1[i][:, :], 0.0).then_inc(zeroed, 1)
            nc.gpsimd.memset(dA[:, :, :, :], 0.0).then_inc(zeroed, 1)
            pool.wait_ge(zeroed, 5)
            nc.gpsimd.memset(h1[KHI:KHI + 1, 1, :], 1.0).then_inc(zeroed, 1)
            pool.wait_ge(zeroed, 6)
            nc.gpsimd.memset(unit[:, :], 1.0).then_inc(zeroed, 1)
            pool.wait_ge(zeroed, 7)
            nc.gpsimd.memset(pool_one[:, :], 0.0).then_inc(u_done, ONE)

            def front(u, s):
                hi, x = SPL[s], XD[s]
                n = [0]

                def then(ins):
                    n[0] += 1
                    ins.then_inc(split_step, 1)
                    pool.wait_ge(split_step, u * 5 + n[0])

                pool.wait_ge(u_done, ONE + u)
                pool.wait_ge(fr_used, ONE + fbase(u - 1) + 2 + 5 if not isinstance(u, int) or u else ONE + 5)
                then(nc.gpsimd.tensor_tensor(hi[:, :], x[0:96, :], unit[:, :], ALU.mult))
                then(nc.gpsimd.tensor_tensor(rem[:, :], x[0:96, :], hi[:, :], ALU.subtract))
                then(nc.gpsimd.tensor_tensor(hi[32:64, :], rem[32:64, :], unit[32:64, :], ALU.mult))
                then(nc.gpsimd.tensor_tensor(hi[64:96, :], rem[64:96, :], unit[64:96, :], ALU.mult))
                then(nc.gpsimd.tensor_tensor(rem[64:96, :], rem[64:96, :], hi[64:96, :], ALU.subtract))
                nc.gpsimd.tensor_tensor(hi[64:96, :], rem[64:96, :], unit[64:96, :], ALU.mult).then_inc(split_done, 1)
                pool.wait_ge(split_done, u + 1)
                pool.wait_ge(dt_log, u + 1)
                nc.gpsimd.tensor_tensor(DT[s][:, :, :], DT[s][:, :, :], AB[:, :, :], ALU.add).then_inc(dt_done, 1)
                pool.wait_ge(dt_done, u + 1)
                nc.gpsimd.tensor_tensor(U[s][:, :, :], DT[s][:, :, :], XC[s][:, :, :], ALU.mult).then_inc(u_done, 1)

            def gate(v, s, units):
                pool.wait_ge(u_done, ONE + units)
                pool.wait_ge(yf_done, ONE + v + 1)
                pool.wait_ge(silu_z, v + 1)
                nc.gpsimd.tensor_tensor(YF[s][:, :, :], YF[s][:, :, :], Z[s][:, :, :], ALU.mult).then_inc(gated, 1)
                pool.wait_ge(gated, v + 1)

            def step(u, s, p, l, has_out, has_front, turn):
                if has_out:
                    gate(u - 1, 1 - s, u + 1)
                if has_front:
                    front(u + 1, 1 - s)

            steps(pool, lambda: front(0, 0), step, lambda turn: gate(UNITS - 1, 1, UNITS))

        @block.tensor
        def _(pe):
            pe.wait_ge(const_ld, 16 * (len(consts) - 1))
            pe.wait_ge(out_st, 16)
            pe.wait_ge(zeroed, 7)

            def fill_free(f, n):
                pe.wait_ge(fr_used, ONE + f + n - 1)

            def out_mm(v, f, s, n):
                if n == 0:
                    pe.wait_ge(gated, v + 1)
                fill_free(f, n)
                for k in range(MT):
                    mm = nc.tensor.matmul(pF[:, n, 0:T], ow[:, k, n * 128:(n + 1) * 128], YF[s][:, k, :],
                                          start=(k == 0), stop=(k == MT - 1))
                mm.then_inc(fr_full, 1)

            def conv_mm(f, s, m, half):
                if half == 0 and (not isinstance(f, int) or f + m):
                    fill_free(f, m)
                o = pF[:, m % 2, 0:T]
                for j in ((0, 1, 2) if half == 0 else (3, 4, 5)):
                    rhs = X0[s][:, j:j + T] if j < 4 else X1[s][:, 3 - 2 * (j - 4):3 - 2 * (j - 4) + T]
                    mm = nc.tensor.matmul(o, wc[:, j, m * 128:(m + 1) * 128], rhs, start=(j == 0), stop=(j == 5))
                if half:
                    mm.then_inc(fr_full, 1)

            def z_mm(f, s, m, n):
                fill_free(f, n)
                o = pF[:, n % 2, 0:T]
                nc.tensor.matmul(o, wz[:, 0, m * 128:(m + 1) * 128], X0[s][:, 3:3 + T], start=True, stop=False)
                nc.tensor.matmul(o, wz[0:KHI, 1, m * 128:(m + 1) * 128], X1[s][0:KHI, 3:3 + T],
                                 start=False, stop=True).then_inc(fr_full, 1)

            def xp_mm(u, f, s, n):
                pe.wait_ge(silu_x, u + 1)
                fill_free(f, n)
                for k in range(MT):
                    mm = nc.tensor.matmul(pF[0:XDR, n % 2, 0:T], xpw[:, k, :], XC[s][:, k, :],
                                          start=(k == 0), stop=(k == MT - 1))
                mm.then_inc(fr_full, 1)

            def dt_mm(f, s, m, n, xp_fill):
                pe.wait_ge(fr_used, ONE + f + xp_fill + 1)
                fill_free(f, n)
                nc.tensor.matmul(pF[:, n % 2, 0:T], dtw[96:96 + RANK, m * 128:(m + 1) * 128],
                                 XD[s][96:96 + RANK, :], start=True, stop=True).then_inc(fr_full, 1)

            def front_mm(u, f, s, i):
                if 2 <= i < 8:
                    conv_mm(f, s, (i - 2) // 2, (i - 2) % 2)
                if i == 8:
                    z_mm(f, s, 0, 3)
                if i == 9:
                    xp_mm(u, f, s, 4)
                if i == 10:
                    z_mm(f, s, 1, 5)
                if i == 11:
                    dt_mm(f, s, 0, 6, 4)
                    dt_mm(f, s, 1, 7, 4)
                if i == 12:
                    dt_mm(f, s, 2, 8, 4)
                    z_mm(f, s, 2, 9)

            def b_mm(u, s, i):
                pe.wait_ge(bx_done, ONE + u * NS + i)
                nc.tensor.matmul(pB[:, 0:T], sel[:, i, :], SPL[s][:, :], start=True, stop=True).then_inc(b_full, 1)

            def c_mm(u, s, i):
                pe.wait_ge(hc_done, ONE + u * NS + i)
                nc.tensor.matmul(pC[:, 0:T], sel[:, NS + i, :], SPL[s][:, :], start=True, stop=True).then_inc(c_full, 1)

            def y_mm(u, i):
                pe.wait_ge(hc_done, ONE + u * NS + i + 1)
                if i == 0:
                    pe.wait_ge(yf_done, ONE + u)
                y = hcr[:, i % 2, :, :].rearrange("p m t -> p (m t)")
                nc.tensor.matmul(pY[:, 0:512], ident[:, :], y[:, 0:512], start=(i == 0), stop=(i == NS - 1))
                nc.tensor.matmul(pY[:, 512:NY], ident[:, :], y[:, 512:NY], start=(i == 0),
                                 stop=(i == NS - 1)).then_inc(y_done, 1)

            def q_free(t, n):
                if n >= 2:
                    k = t.seq[n - 2]
                    pe.wait_ge(q_act if k == "A" else q_dve, t.count(n - 2, k))
                elif t.pre or t.s == 0:
                    pe.wait_ge(q_act, t.act)
                    pe.wait_ge(q_dve, ONE + t.dve)
                else:
                    pe.wait_ge(q_dve, ONE + t.dve)

            def transposes(full):
                for h in range(2):
                    for t in range(3):
                        mm = nc.tensor.transpose(pQ[:, h, t * TT:(t + 1) * TT] if full is None else
                                                 pQ[:, (full + h) % 2, t * TT:(t + 1) * TT],
                                                 xn[:, t, h * 128:(h + 1) * 128], ident[0:TT, 0:TT])
                    mm.then_inc(q_full, 1)

            def change(t, i):
                s, P = t.s, t.pre
                if i == 1:
                    for m in range(2):
                        R = (KLO, KHI)[m]
                        q_free(t, m)
                        o = pQ[0:R, m, 0:T]
                        nc.tensor.matmul(o, hw1[:, 0, m * 128:m * 128 + R], X0[s][:, 3:3 + T], start=True, stop=False)
                        nc.tensor.matmul(o, hw1[0:KHI, 1, m * 128:m * 128 + R], X1[s][0:KHI, 3:3 + T],
                                         start=False, stop=True).then_inc(q_full, 1)
                if i == 2 and P:
                    pe.wait_ge(xn_done, t.norms + 1)
                    q_free(t, 3)
                    transposes(2)
                    pe.wait_ge(q_act, t.count(3, "A"))
                if i == 4:
                    pe.wait_ge(q_act, t.count(1, "A"))
                    for k in range(3):
                        n = 2 + P + k
                        q_free(t, n)
                        o = pQ[0:TT, n % 2, 0:D]
                        nc.tensor.matmul(o, h1[:, 0, k * TT:(k + 1) * TT], hw2[:, 0, :], start=True, stop=False)
                        nc.tensor.matmul(o, h1[0:KHI + 1, 1, k * TT:(k + 1) * TT], hw2[0:KHI + 1, 1, :],
                                         start=False, stop=True).then_inc(q_full, 1)
                if i == 7:
                    pe.wait_ge(xn_done, t.norms + (2 if P else 1))
                    q_free(t, 6 + P)
                    transposes(5 + P)
                if 8 <= i < 8 + FM // 2:
                    pe.wait_ge(q_act, t.count(6 + P, "A"))
                    for m in (2 * (i - 8), 2 * (i - 8) + 1):
                        n = 7 + P + m
                        q_free(t, n)
                        o = pQ[:, n % 2, 0:T]
                        nc.tensor.matmul(o, c["w1q"][:, 0, m * 128:(m + 1) * 128], xf[:, 0, :], start=True, stop=False)
                        nc.tensor.matmul(o, c["w1q"][0:KHI, 1, m * 128:(m + 1) * 128], xf[0:KHI, 1, :],
                                         start=False, stop=True).then_inc(q_full, 1)
                if i in (13, 14, 15):
                    k = i - 13
                    pe.wait_ge(f1_done, t.nth + 1)
                    n = 7 + FM + P + k
                    q_free(t, n)
                    o = pQ[0:TT, n % 2, 0:D]
                    for m in range(FM):
                        nc.tensor.matmul(o, f1[:, m, k * TT:(k + 1) * TT], c["w2q"][:, m, :], start=(m == 0), stop=False)
                    nc.tensor.matmul(o, c["ones"][:, 0:TT], fb2[:, :], start=False, stop=True).then_inc(q_full, 1)

            def step(u, s, p, l, has_out, has_front, turn):
                f, o = fbase(u), 1 - s
                for i in range(NS):
                    if i < NS - 1:
                        c_mm(u, s, i + 1) if i else None
                    if i == 0:
                        b_mm(u, s, 1)
                        c_mm(u, s, 1)
                        b_mm(u, s, 2)
                    elif i < NS - 2:
                        b_mm(u, s, i + 2)
                    elif has_front:
                        if i == NS - 2:
                            pe.wait_ge(split_done, u + 2)
                            b_mm(u + 1, o, 0)
                        else:
                            c_mm(u + 1, o, 0)
                    y_mm(u, i)
                    if has_out and i < 2:
                        if i == 0:
                            pe.wait_ge(ow_ld, 16 * (4 * p + l + (0 if has_front else UNITS // 2)))
                        out_mm(u - 1, f, o, i)
                    if has_out and i == 2:
                        pe.wait_ge(fr_used, ONE + f + 2)
                    if turn is not None:
                        if i == 1:
                            pe.wait_ge(fr_used, ONE + f + 2)
                        change(turn, i)
                    if has_front:
                        if i == 2:
                            pe.wait_ge(front_ld, FRONT_LD * (4 * p + l + 1))
                            if not has_out:
                                pe.wait_ge(q_act, 4)
                        front_mm(u + 1, f + 2, o, i)

            def enter():
                for s in range(2):
                    pe.wait_ge(xn_done, s + 1)
                    if s:
                        pe.wait_ge(q_act, 2)
                    transposes(None)
                pe.wait_ge(front_ld, FRONT_LD)
                pe.wait_ge(q_act, 2)
                for i in range(NS):
                    front_mm(0, 0, 0, i)
                pe.wait_ge(split_done, 1)
                b_mm(0, 0, 0)
                c_mm(0, 0, 0)

            def leave(turn):
                f = LAST_OUT
                for n in range(2):
                    out_mm(UNITS - 1, f, 1, n)
                pe.wait_ge(fr_used, ONE + f + 2)
                for i in range(NS):
                    change(turn, i)

            steps(pe, enter, step, leave)

        @block.scalar
        def _(act):
            act.wait_ge(const_ld, 16 * (len(consts) - 1))
            act.wait_ge(zeroed, 7)
            nc.scalar.activation(tiny[:, 1:2], c["ones"][:, 0:1], ACT.Copy).then_inc(fr_used, ONE)

            def evac_out(f, s):
                act.wait_ge(fr_full, f + 1)
                nc.scalar.activation(X0[s][:, 3:3 + T], pF[:, 0, 0:T], ACT.Copy).then_inc(fr_used, 1)
                act.wait_ge(fr_full, f + 2)
                nc.scalar.activation(X1[s][0:KHI, 3:3 + T], pF[0:KHI, 1, 0:T], ACT.Copy)
                nc.scalar.activation(X1[s][KHI:128, 4:4 + T], pF[KHI:128, 1, 0:T], ACT.Copy).then_inc(fr_used, 1)

            def decays(u, s, i, fresh=False):
                if not fresh:
                    act.wait_ge(scan_done, u * NS + i - (NR - 1))
                for m in range(MT):
                    a = nc.scalar.activation(dA[:, i % NR, m, 1:T], DT[s][:, m, 1:T], ACT.Exp,
                                             scale=pa[s][:, m * NS + i:m * NS + i + 1])
                a.then_inc(decay, 1)

            def z_evac(f, s, m, n):
                act.wait_ge(fr_full, f + n + 1)
                nc.scalar.activation(Z[s][:, m, :], pF[:, n % 2, 0:T], ACT.Copy).then_inc(fr_used, 1)

            def gate_silu(s, f):
                act.wait_ge(fr_used, ONE + f)
                nc.scalar.activation(Z[s][:, :, :], Z[s][:, :, :], ACT.Silu).then_inc(silu_z, 1)

            def log_exp_table():
                nc.scalar.activation(tiny[:, 0:1], c["ones"][:, 0:1], ACT.Ln)

            def dt_evac(f, s, m, n):
                act.wait_ge(fr_full, f + n + 1)
                b = cdb[:, MT + m:MT + m + 1]
                nc.scalar.activation(AB[:, m, :], pF[:, n % 2, 0:T], ACT.Abs, bias=b)
                nc.scalar.activation(DT[s][:, m, :], pF[:, n % 2, 0:T], ACT.Relu, bias=b).then_inc(fr_used, 1)

            def front(u, f, s, i, scanned):
                if i in (4, 6, 8):
                    m = (i - 4) // 2
                    act.wait_ge(fr_full, f + m + 1)
                    nc.scalar.activation(XC[s][:, m, :], pF[:, m % 2, 0:T], ACT.Identity,
                                         bias=cdb[:, m:m + 1]).then_inc(fr_used, 1)
                if i == 8:
                    act.wait_ge(fr_used, ONE + f + 3)
                    nc.scalar.activation(XC[s][:, :, :], XC[s][:, :, :], ACT.Silu).then_inc(silu_x, 1)
                    if scanned:
                        gate_silu(1 - s, f)
                    log_exp_table()
                if i == 9:
                    z_evac(f, s, 0, 3)
                if i == 10:
                    act.wait_ge(fr_full, f + 5)
                    nc.scalar.activation(XD[s][0:XDR, :], pF[0:XDR, 0, 0:T], ACT.Copy).then_inc(fr_used, 1)
                if i == 11:
                    z_evac(f, s, 1, 5)
                if i == 12:
                    dt_evac(f, s, 0, 6)
                    dt_evac(f, s, 1, 7)
                if i == 13:
                    dt_evac(f, s, 2, 8)
                    act.wait_ge(fr_used, ONE + f + 9)
                    nc.scalar.activation(AB[:, :, :], AB[:, :, :], ACT.Exp, scale=-1.0).then_inc(ab_step, 1)
                    act.wait_ge(ab_step, u + 1)
                    nc.scalar.activation(AB[:, :, :], AB[:, :, :], ACT.Ln, bias=1.0).then_inc(dt_log, 1)
                    z_evac(f, s, 2, 9)

            def rstd(g):
                act.wait_ge(ln_var, g + 1)
                nc.scalar.activation(lg[:, :], var[:, :], ACT.Ln).then_inc(ln_log, 1)
                act.wait_ge(ln_log, g + 1)
                nc.scalar.activation(rs[:, :], lg[:, :], ACT.Exp, scale=-0.5).then_inc(ln_exp, 1)

            def take_x(fills, s, b):
                act.wait_ge(q_full, fills + 1)
                nc.scalar.activation(X0[s][:, 3:3 + T], pQ[:, b, 0:T], ACT.Copy).then_inc(q_act, 1)
                act.wait_ge(q_full, fills + 2)
                nc.scalar.activation(X1[s][0:KHI, 3:3 + T], pQ[0:KHI, 1 - b, 0:T], ACT.Copy)
                nc.scalar.activation(X1[s][KHI:128, 4:4 + T], pQ[KHI:128, 1 - b, 0:T], ACT.Copy).then_inc(q_act, 1)

            def change(t, i):
                s, P = t.s, t.pre
                if i == 1 and P:
                    rstd(t.norms)
                if i == 2:
                    for m in range(2):
                        R = (KLO, KHI)[m]
                        act.wait_ge(q_full, t.fills + m + 1)
                        nc.scalar.activation(h1[0:R, m, :], pQ[0:R, m, 0:T], ACT.Relu,
                                             bias=hb1[0:R, m:m + 1]).then_inc(q_act, 1)
                    if P:
                        take_x(t.fills + 2, s, 0)
                if i == 6:
                    rstd(t.norms + (1 if P else 0))
                if i == 8:
                    for m in range(2):
                        R, n = (KLO, KHI)[m], 5 + P + m
                        act.wait_ge(q_full, t.fills + n + 1)
                        nc.scalar.activation(xf[0:R, m, :], pQ[0:R, n % 2, 0:T], ACT.Copy).then_inc(q_act, 1)
                if 9 <= i < 9 + FM // 2:
                    for m in (2 * (i - 9), 2 * (i - 9) + 1):
                        n = 7 + P + m
                        act.wait_ge(q_full, t.fills + n + 1)
                        nc.scalar.activation(f1[:, m, :], pQ[:, n % 2, 0:T], ACT.Identity,
                                             bias=fb1[:, m:m + 1]).then_inc(q_act, 1)
                if i == 12:
                    act.wait_ge(q_act, t.count(6 + P + FM, "A"))
                    nc.scalar.activation(f1[:, :, :], f1[:, :, :], ACT.Gelu).then_inc(f1_done, 1)
                    log_exp_table()

            def step(u, s, p, l, has_out, has_front, turn):
                f, o = fbase(u), 1 - s
                for i in range(NS):
                    if i < NS - 2:
                        decays(u, s, i + 2, fresh=isinstance(u, int) and u == 0 and i + 2 < NR)
                    elif has_front:
                        if i == NS - 2:
                            act.wait_ge(dt_done, u + 2)
                            act.wait_ge(pa_ld[o], 16 * (4 * p + l + 1))
                        decays(u + 1, o, i - (NS - 2))
                    if i == 1 and has_out:
                        evac_out(f, o)
                    if turn is not None:
                        change(turn, i)
                    if has_front:
                        if i == 4:
                            act.wait_ge(front_ld, FRONT_LD * (4 * p + l + 1))
                        front(u + 1, f + 2, o, i, True)
                    elif i == 8:
                        gate_silu(s, f)
                        log_exp_table()

            def enter():
                log_exp_table()
                for s in range(2):
                    rstd(s)
                    take_x(2 * s, s, 0)
                act.wait_ge(front_ld, FRONT_LD)
                for i in range(NS):
                    front(0, 0, 0, i, False)
                act.wait_ge(dt_done, 1)
                act.wait_ge(pa_ld[0], 16)
                decays(0, 0, 0, fresh=True)
                decays(0, 0, 1, fresh=True)

            def leave(turn):
                evac_out(LAST_OUT, 1)
                for i in range(NS):
                    change(turn, i)

            steps(act, enter, step, leave)

        @block.vector
        def _(dve):
            dve.wait_ge(zeroed, 7)
            for n, q in enumerate((bx_done, hc_done, yf_done, q_dve)):
                nc.vector.memset(pause[:, n:n + 1], 0.0).then_inc(q, ONE)

            def then(ins, g, n):
                ins.then_inc(ln_step, 1)
                dve.wait_ge(ln_step, g * LN_STEPS + n)

            def moments(src, g):
                for t in range(3):
                    last = nc.vector.bn_stats(st6[:, t, :], src[:, t, :])
                then(last, g, 1)
                nc.vector.memset(nt[:, :], 0.0)
                for t in range(3):
                    last = nc.vector.bn_aggr(mv[:, t, :], st6[:, t, :])
                then(last, g, 2)
                nc.vector.tensor_scalar(var[:, :], mv[:, :, 1], EPS, None, ALU.add).then_inc(ln_var, 1)

            def normalize(src, g):
                dve.wait_ge(ln_exp, g + 1)
                then(nc.vector.tensor_tensor(nt[:, :], rs[:, :], rs[:, :], ALU.mult), g, 3)
                then(nc.vector.tensor_tensor(nt[:, :], nt[:, :], var[:, :], ALU.mult), g, 4)
                then(nc.vector.tensor_scalar(nt[:, :], nt[:, :], -0.5, 1.5, ALU.mult, ALU.add), g, 5)
                then(nc.vector.tensor_tensor(rs[:, :], rs[:, :], nt[:, :], ALU.mult), g, 6)
                for t in range(3):
                    nc.vector.tensor_scalar(xn[:, t, 0:D], src[:, t, :], mv[:, t, 0:1], rs[:, t:t + 1],
                                            ALU.subtract, ALU.mult)
                    last = nc.vector.tensor_scalar(xn[:, t, D:256], src[:, t, KLO:D], mv[:, t, 0:1], rs[:, t:t + 1],
                                                   ALU.subtract, ALU.mult)
                last.then_inc(xn_done, 1)

            def bx_op(u, s, i):
                dve.wait_ge(b_full, u * NS + i + 1)
                nc.vector.tensor_tensor(bx[:, i % 2, :, :], U[s][:, :, :],
                                        pB[:, 0:T].unsqueeze(1).to_broadcast([128, MT, T]),
                                        ALU.mult).then_inc(bx_done, 1)

            def scan_op(u, s, i):
                dve.wait_ge(decay, u * NS + i + 1)
                dve.wait_ge(bx_done, ONE + u * NS + i + 1)
                flat = lambda t: t[:, :, :].rearrange("p m t -> p (m t)")
                nc.vector.tensor_tensor_scan(flat(hh[:, i % 2, :, :]), flat(dA[:, i % NR, :, :]),
                                             flat(bx[:, i % 2, :, :]), 0.0, ALU.mult, ALU.add).then_inc(scan_done, 1)

            def hc_op(u, s, i, fresh):
                dve.wait_ge(c_full, u * NS + i + 1)
                dve.wait_ge(scan_done, u * NS + i + 1)
                if not fresh:
                    dve.wait_ge(y_done, u * NS + i - 1)
                nc.vector.tensor_tensor(hcr[:, i % 2, :, :], hh[:, i % 2, :, :],
                                        pC[:, 0:T].unsqueeze(1).to_broadcast([128, MT, T]),
                                        ALU.mult).then_inc(hc_done, 1)

            def yf_op(v, s):
                dve.wait_ge(y_done, (v + 1) * NS)
                for m in range(MT):
                    last = nc.vector.scalar_tensor_tensor(out=YF[s][:, m, :], in0=XC[s][:, m, :],
                                                          scalar=pa[s][:, MT * NS + m:MT * NS + m + 1],
                                                          in1=pY[:, m * T:(m + 1) * T], op0=ALU.mult, op1=ALU.add)
                last.then_inc(yf_done, 1)

            def change(t, i):
                s, P = t.s, t.pre
                g2 = t.norms + (1 if P else 0)
                if i == 0 and P:
                    dve.wait_ge(hi_ld[s], 16 * (t.pair + 2))
                    moments(HI[s], t.norms)
                if i == 1 and P:
                    normalize(HI[s], t.norms)
                if i == 5:
                    for k in range(3):
                        n = 2 + P + k
                        dve.wait_ge(q_full, t.fills + n + 1)
                        nc.vector.tensor_tensor(HT[s][:, k, :], pQ[0:TT, n % 2, 0:D], HT[s][:, k, :],
                                                ALU.add).then_inc(q_dve, 1)
                    dve.wait_ge(q_dve, t.count(4 + P, "D"))
                    moments(HT[s], g2)
                if i == 6:
                    dve.wait_ge(q_full, t.fills + 2 + P)
                    normalize(HT[s], g2)
                if i == 13:
                    dve.wait_ge(out_st, 16 * (t.nth + 1))
                if i in (13, 14, 15):
                    k = i - 13
                    n = 7 + FM + P + k
                    dve.wait_ge(q_full, t.fills + n + 1)
                    nc.vector.tensor_tensor(OT[:, k, :], pQ[0:TT, n % 2, 0:D], HT[s][:, k, :],
                                            ALU.add).then_inc(q_dve, 1)
                if i == 15:
                    dve.wait_ge(q_dve, t.count(9 + FM + P, "D"))
                    if P:
                        nc.vector.tensor_copy(HT[s][:, :, :], HI[s][:, :, :]).then_inc(hi_used, 1)
                    nc.vector.memset(pause[:, t.s:t.s + 1], 0.0).then_inc(ot_done, 1)

            def step(u, s, p, l, has_out, has_front, turn):
                o = 1 - s
                for i in range(NS):
                    scan_op(u, s, i)
                    if i == 0 and has_out:
                        yf_op(u - 1, o)
                    if i < NS - 1:
                        bx_op(u, s, i + 1)
                    elif has_front:
                        dve.wait_ge(u_done, ONE + u + 2)
                        bx_op(u + 1, o, 0)
                    hc_op(u, s, i, isinstance(u, int) and u == 0 and i < 2)
                    if turn is not None:
                        change(turn, i)

            def enter():
                for s in range(2):
                    dve.wait_ge(hi_ld[s], 16)
                    if s:
                        dve.wait_ge(q_full, 2)
                    moments(HI[s], s)
                    normalize(HI[s], s)
                    nc.vector.tensor_copy(HT[s][:, :, :], HI[s][:, :, :]).then_inc(hi_used, 1)
                dve.wait_ge(u_done, ONE + 1)
                bx_op(0, 0, 0)

            def leave(turn):
                yf_op(UNITS - 1, 1)
                for i in range(NS):
                    change(turn, i)

            steps(dve, enter, step, leave)


def host_layouts(x):
    import numpy as np

    a = {}
    a["x"], a["txt"] = x["x"], x["txt"]
    stem = x["L0_tok_stem_w"].transpose(3, 1, 2, 0).reshape(48, CO)
    a["stem"] = np.concatenate([stem, x["L0_tok_stem_b"][None]], 0)
    for k in ("g", "b", "m", "v"):
        a[f"bn1_{k}"], a[f"bn2_{k}"] = x[f"L0_tok_bn1_{k}"], x[f"L0_tok_bn2_{k}"]
    a["dcn_w"] = x["L0_tok_dcn_w"].transpose(1, 2, 3, 0).reshape(CO, TAPS, D)
    a["dcn_b"] = x["L0_tok_dcn_b"]
    a["off_w"] = x["L0_tok_off_w"].transpose(1, 2, 3, 0).reshape(CO, TAPS, 32)
    a["off_b"] = x["L0_tok_off_b"]
    q, t, k = np.arange(QP)[:, None, None], np.arange(2)[None, :, None], np.arange(TAPS)[None, None, :]
    y = 4 * (7 * t + q // GRID) + k // 4
    xx = 4 * (q % GRID) + k % 4 + 0 * t
    a["base"] = np.stack(np.broadcast_arrays(y, xx), -1).reshape(QP, 2, 32).astype(np.float32)
    a["ident"] = np.eye(128, dtype=np.float32)
    sel = np.zeros((96, 2 * NS, 128), np.float32)
    for r in range(96):
        sel[r, r % 32, :] = 1
    a["sel"] = sel
    w = x["L0_attn_in_proj_w"]
    wx = w[:, :, :DI]
    a["in_x"] = np.stack([wx[:, 0:128], np.concatenate([wx[:, 128:], wx[:, 128:]], 1)], 2)
    a["in_z"] = w[:, :, DI:]
    a["conv_w"] = x["L0_attn_conv_w"].transpose(0, 2, 1)
    xp = x["L0_attn_x_proj_w"].reshape(LAYERS, MT, 128, RANK + 2 * NS).transpose(0, 2, 1, 3)
    bc = xp[..., RANK:]
    a["xp"] = np.concatenate([bc, bc, bc, xp[..., :RANK]], -1)
    a["dtw"] = x["L0_attn_dt_proj_w"]
    col = lambda v: v.reshape(LAYERS, MT, 128).transpose(0, 2, 1)
    a["cdb"] = np.concatenate([col(x["L0_attn_conv_b"]), col(x["L0_attn_dt_proj_b"])], -1)
    al = x["L0_attn_A_log"].reshape(LAYERS, MT, 128, NS).transpose(0, 2, 1, 3).reshape(LAYERS, 128, MT * NS)
    a["pa"] = np.concatenate([al, col(x["L0_attn_D"])], -1)
    o = x["L0_attn_out_proj_w"]
    o = np.concatenate([o, o[..., KLO:]], -1)
    a["ow"] = o.reshape(LAYERS, MT, 128, 256).transpose(0, 2, 1, 3)
    a["head_w1"], a["head_w2"] = x["L0_attn_head_w1"], x["L0_attn_head_w2"]
    a["head_b1"], a["head_b2"] = x["L0_attn_head_b1"], x["L0_attn_head_b2"]
    a["ffn_w1"] = x["L0_ffn_w1"].T
    a["ffn_w2"] = x["L0_ffn_w2"].T.reshape(FM, 128, D).transpose(1, 0, 2)
    a["ffn_b1"] = x["L0_ffn_b1"].reshape(FM, 128).T
    a["ffn_b2"] = x["L0_ffn_b2"]
    return {k: np.ascontiguousarray(v) for k, v in a.items()}


def kernel(**inputs):
    import numpy as np
    import concourse.bacc as bacc
    from concourse.bass_utils import run_bass_kernel_spmd

    arrays = host_layouts({k: np.asarray(v) for k, v in inputs.items()})
    nc = bacc.Bacc("TRN2", target_bir_lowering=False, num_devices=1)
    w = {k: nc.dram_tensor(f"in_{k}", v.shape, mybir.dt.from_np(v.dtype), kind="ExternalInput").ap()
         for k, v in arrays.items()}
    NB = arrays["x"].shape[0]
    out = nc.dram_tensor("out_0", [NB, T, D], F32, kind="ExternalOutput").ap()
    program(nc, w, out)
    r = run_bass_kernel_spmd(nc, [{f"in_{k}": v for k, v in arrays.items()}], core_ids=[0])
    return r.results[0]["out_0"]
```

```python
from contextlib import ExitStack

import concourse.bass as bass
from concourse import mybir

ALU = mybir.AluOpType
ACT = mybir.ActivationFunctionType
F32 = mybir.dt.float32
BF16 = mybir.dt.bfloat16
I32 = mybir.dt.int32
U32 = mybir.dt.uint32

EPS = 1e-5
SLOPE = 0.01
D = 192
KLO, KHI = 128, 64
DI = 384
MT = DI // 128
NS = 16
RANK = 12
LAYERS = 4
TXT = 77
GRID = 14
NPOS = GRID * GRID
T = NPOS + TXT
TT = T // 3
CO = 96
HS = 56
TAPS = 16
NKT = TAPS * CO // 128
PIT = HS + 3
NENT = PIT * PIT
QP = NPOS // 2
FH = 768
FM = FH // 128
XDR = 96 + RANK
NY = MT * T


def bcast(ap, parts):
    return ap.unsqueeze(0).to_broadcast([parts] + list(ap.shape))


def program(nc, w, out):
    NB = w["x"].shape[0]
    tab = nc.dram_tensor("tab", [2 * NENT, 4 * CO], F32, kind="Internal").ap()
    h0 = nc.dram_tensor("h0", [NB, T, D], F32, kind="Internal").ap()
    wcd = nc.dram_tensor("wcd", [LAYERS, 128, 6 * DI], F32, kind="Internal").ap()
    pad = nc.dram_tensor("pad", [LAYERS, 128, MT * NS + MT], F32, kind="Internal").ap()
    with ExitStack() as keep:
        sb = lambda n, s, d=F32: keep.enter_context(nc.sbuf_tensor(n, s, d))
        c = dict(
            ident=sb("ident", [128, 128]), ones=sb("ones", [1, 128]),
            w1q=sb("w1q", [128, 2, FH]), w2q=sb("w2q", [128, FM, D]),
            ws=sb("ws", [49, CO]), wd=sb("wd", [128, NKT, D]), wb=sb("wb", [1, D]), wo=sb("wo", [CO, TAPS, 32]),
            base=sb("base", [QP, 2, 32]), sel=sb("sel", [96, 2 * NS, 128], BF16),
        )
        setup(nc, w, c, tab, wcd, pad)
        tokens(nc, w, c, tab, h0, NB)
        mixer(nc, w, c, h0, wcd, pad, out, NB)


def setup(nc, w, c, tab, wcd, pad):
    with ExitStack() as ctx:
        sb = lambda n, s, d=F32: ctx.enter_context(nc.sbuf_tensor(n, s, d))
        sem = lambda n: ctx.enter_context(nc.semaphore(n))
        zero = sb("zero", [118, 4 * CO])
        g1, v1, b1, m1 = (sb(n, [49, CO]) for n in ("g1", "v1", "b1", "m1"))
        g2, v2 = sb("g2", [128, D]), sb("v2", [128, D])
        b2, m2 = sb("b2", [1, D]), sb("m2", [1, D])
        offb = sb("offb", [QP, 32])
        self32 = sb("self32", [96, 2 * NS, 128])
        wx = sb("wx", [128, 2, DI])
        cw = sb("cw", [128, 6, DI])
        wc = sb("wc", [128, 6, DI])
        pa = sb("pa", [128, MT * NS + MT])
        ab = sb("ab", [128, 2 * FH])
        asum = sb("asum", [128, 2])
        gam = sb("gam", [128, 2])
        half = sb("half", [128, 2])
        nhalf = sb("nhalf", [128, 2])
        onesq = sb("onesq", [128, 128])
        neg = sb("neg", [128, 2 * FH])
        tot = ctx.enter_context(nc.psum_tensor("tot", [128, 2], F32))
        loads, zeroed, tabz = sem("loads"), sem("zeroed"), sem("tabz")
        step, act_step, summed = sem("step"), sem("act_step"), sem("summed")
        lay_ld, lay_done, lay_st = sem("lay_ld"), sem("lay_done"), sem("lay_st")
        pa_exp = sem("pa_exp")
        rows = [
            (c["ident"][:, :], w["ident"]), (c["ws"][:, :], w["stem"]),
            (g1[:, :], bcast(w["bn1_g"], 49)), (v1[:, :], bcast(w["bn1_v"], 49)),
            (b1[48:49, :], bcast(w["bn1_b"], 1)), (m1[48:49, :], bcast(w["bn1_m"], 1)),
            (c["wd"][:, :, :], w["dcn_w"]), (c["wb"][:, :], bcast(w["dcn_b"], 1)),
            (g2[:, :], bcast(w["bn2_g"], 128)), (v2[:, :], bcast(w["bn2_v"], 128)),
            (b2[:, :], bcast(w["bn2_b"], 1)), (m2[:, :], bcast(w["bn2_m"], 1)),
            (c["wo"][:, :, :], w["off_w"]), (c["base"][:, :, :], w["base"]),
            (offb[:, :], bcast(w["off_b"], QP)),
            (c["w1q"][:, 0, :], w["ffn_w1"][0:KLO, :]), (c["w1q"][0:KHI, 1, :], w["ffn_w1"][KLO:D, :]),
            (c["w2q"][:, :, :], w["ffn_w2"]), (self32[:, :, :], w["sel"]),
        ]
        block = ctx.enter_context(nc.Block())

        @block.sync
        def _(sp):
            sp.wait_ge(zeroed, 5)
            for dst, src in rows:
                sp.dma_start(dst, src).then_inc(loads, 16)
            t = tab.rearrange("(n p) c -> n p c", p=118)
            for n in range(2 * NENT // 118):
                sp.dma_start(t[n], zero[:, :]).then_inc(tabz, 16)
            sp.wait_ge(tabz, 16 * (2 * NENT // 118))
            for l in range(LAYERS):
                sp.wait_ge(lay_st, 32 * l)
                sp.dma_start(wx[:, :, :], w["in_x"][l]).then_inc(lay_ld, 16)
                taps = w["conv_w"][l]
                for j in range(4):
                    sp.dma_start(cw[:, j, :], bcast(taps[j], 128)).then_inc(lay_ld, 16)
                for q in range(2):
                    sp.dma_start(cw[0:64, 4 + q, :], bcast(taps[3 - 2 * q], 64)).then_inc(lay_ld, 16)
                    sp.dma_start(cw[64:128, 4 + q, :], bcast(taps[2 - 2 * q], 64)).then_inc(lay_ld, 16)
                sp.dma_start(pa[:, :], w["pa"][l]).then_inc(lay_ld, 16)
                sp.wait_ge(lay_done, 2 * (l + 1))
                sp.dma_start(wcd[l], wc[:, :, :].rearrange("p a b -> p (a b)")).then_inc(lay_st, 16)
                sp.dma_start(pad[l], pa[:, :]).then_inc(lay_st, 16)
            sp.wait_ge(lay_st, 32 * LAYERS)

        @block.gpsimd
        def _(pool):
            nc.gpsimd.memset(zero[:, :], 0.0).then_inc(zeroed, 1)
            nc.gpsimd.memset(b1[:, :], 0.0).then_inc(zeroed, 1)
            nc.gpsimd.memset(m1[:, :], 0.0).then_inc(zeroed, 1)
            nc.gpsimd.memset(c["w1q"][:, :, :], 0.0).then_inc(zeroed, 1)
            nc.gpsimd.memset(c["ones"][:, :], 1.0).then_inc(zeroed, 1)
            nc.gpsimd.memset(onesq[:, :], 1.0).then_inc(zeroed, 1)

        @block.scalar
        def _(act):
            act.wait_ge(step, 2)
            nc.scalar.activation(v1[:, :], v1[:, :], ACT.Sqrt).then_inc(act_step, 1)
            nc.scalar.activation(v2[:, :], v2[:, :], ACT.Sqrt).then_inc(act_step, 1)
            nc.scalar.activation(ab[:, :], c["w1q"][:, :, :].rearrange("p a b -> p (a b)"), ACT.Abs,
                                 accum_out=asum[:, 0:1]).then_inc(act_step, 1)
            act.wait_ge(act_step, 3)
            nc.scalar.activation(ab[:, 0:FM * D], c["w2q"][:, :, :].rearrange("p a b -> p (a b)"), ACT.Abs,
                                 accum_out=asum[:, 1:2]).then_inc(act_step, 1)
            for l in range(LAYERS):
                act.wait_ge(lay_ld, 16 * 10 * (l + 1))
                nc.scalar.activation(pa[:, 0:MT * NS], pa[:, 0:MT * NS], ACT.Exp).then_inc(pa_exp, 1)

        @block.tensor
        def _(pe):
            pe.wait_ge(act_step, 4)
            pe.wait_ge(zeroed, 6)
            nc.tensor.matmul(tot[:, :], onesq[:, :], asum[:, :], start=True, stop=True).then_inc(summed, 1)

        @block.vector
        def _(dve):
            n = [0]

            def then(ins):
                n[0] += 1
                ins.then_inc(step, 1)
                dve.wait_ge(step, n[0])

            dve.wait_ge(loads, 16 * len(rows))
            then(nc.vector.tensor_scalar(v1[:, :], v1[:, :], EPS, None, ALU.add))
            then(nc.vector.tensor_scalar(v2[:, :], v2[:, :], EPS, None, ALU.add))
            dve.wait_ge(act_step, 2)
            ws, wd, wb = c["ws"], c["wd"], c["wb"]
            then(nc.vector.reciprocal(v1[:, :], v1[:, :]))
            then(nc.vector.tensor_tensor(g1[:, :], g1[:, :], v1[:, :], ALU.mult))
            then(nc.vector.tensor_tensor(ws[:, :], ws[:, :], g1[:, :], ALU.mult))
            then(nc.vector.tensor_tensor(m1[:, :], m1[:, :], g1[:, :], ALU.mult))
            then(nc.vector.tensor_tensor(b1[:, :], b1[:, :], m1[:, :], ALU.subtract))
            then(nc.vector.tensor_tensor(ws[:, :], ws[:, :], b1[:, :], ALU.add))
            then(nc.vector.reciprocal(v2[:, :], v2[:, :]))
            then(nc.vector.tensor_tensor(g2[:, :], g2[:, :], v2[:, :], ALU.mult))
            then(nc.vector.tensor_tensor(wd[:, :, :], wd[:, :, :],
                                         g2[:, :].unsqueeze(1).to_broadcast([128, NKT, D]), ALU.mult))
            then(nc.vector.tensor_tensor(wb[:, :], wb[:, :], g2[0:1, :], ALU.mult))
            then(nc.vector.tensor_tensor(m2[:, :], m2[:, :], g2[0:1, :], ALU.mult))
            then(nc.vector.tensor_tensor(b2[:, :], b2[:, :], m2[:, :], ALU.subtract))
            then(nc.vector.tensor_tensor(wb[:, :], wb[:, :], b2[:, :], ALU.add))
            then(nc.vector.tensor_tensor(c["base"][:, :, :], c["base"][:, :, :],
                                         offb[:, :].unsqueeze(1).to_broadcast([QP, 2, 32]), ALU.add))
            then(nc.vector.tensor_copy(c["sel"][:, :, :], self32[:, :, :]))
            dve.wait_ge(summed, 1)
            then(nc.vector.tensor_scalar(gam[:, :], tot[:, :], 1.0 / (FH * D), EPS, ALU.mult, ALU.add))
            then(nc.vector.tensor_scalar(half[:, :], gam[:, :], 0.5, None, ALU.mult))
            then(nc.vector.tensor_scalar(nhalf[:, :], gam[:, :], -0.5, None, ALU.mult))
            for i, q in enumerate((c["w1q"], c["w2q"])):
                q = q[:, :, :].rearrange("p a b -> p (a b)")
                k = q.shape[1]
                then(nc.vector.tensor_scalar(neg[:, 0:k], q, nhalf[:, i:i + 1], gam[:, i:i + 1], ALU.is_lt, ALU.mult))
                then(nc.vector.tensor_scalar(q, q, half[:, i:i + 1], gam[:, i:i + 1], ALU.is_gt, ALU.mult))
                then(nc.vector.tensor_tensor(q, q, neg[:, 0:k], ALU.subtract))
            for l in range(LAYERS):
                dve.wait_ge(lay_ld, 16 * 10 * (l + 1))
                dve.wait_ge(lay_st, 32 * l)
                nc.vector.tensor_tensor(wc[:, 0:4, :], cw[:, 0:4, :],
                                        wx[:, 0, :].unsqueeze(1).to_broadcast([128, 4, DI]), ALU.mult)
                nc.vector.tensor_tensor(wc[:, 4:6, :], cw[:, 4:6, :],
                                        wx[:, 1, :].unsqueeze(1).to_broadcast([128, 2, DI]),
                                        ALU.mult).then_inc(lay_done, 1)
                dve.wait_ge(pa_exp, l + 1)
                nc.vector.tensor_scalar(pa[:, 0:MT * NS], pa[:, 0:MT * NS], -1.0, None,
                                        ALU.mult).then_inc(lay_done, 1)


def tokens(nc, w, c, tab, h0, NB):
    with ExitStack() as ctx:
        sb = lambda n, s, d=F32: ctx.enter_context(nc.sbuf_tensor(n, s, d))
        ps = lambda n, s: ctx.enter_context(nc.psum_tensor(n, s, F32))
        sem = lambda n: ctx.enter_context(nc.semaphore(n))
        HR = HS // 2
        YS, YN = (0, 16), (16, 12)
        xh = [sb(f"xh{i}", [64, YN[i], 2, 224]) for i in range(2)]
        hp = [sb(f"hp{i}", [2 * HS, HR, CO]) for i in range(2)]
        hc = sb("hc", [CO, HS * HS])
        G = [sb(f"G{i}", [QP, TAPS, 4, CO]) for i in range(2)]
        sg = [sb(f"sg{i}", [QP, TAPS * CO]) for i in range(2)]
        sk = [sb(f"sk{i}", [128, NKT, QP]) for i in range(2)]
        pos = sb("pos", [QP, 64])
        fli = sb("fli", [QP, 64], I32)
        flo = sb("flo", [QP, 64])
        fgt = sb("fgt", [QP, 64])
        fr = sb("fr", [QP, 64])
        om = sb("om", [QP, 64])
        idf = sb("idf", [QP, 32])
        idx = [sb(f"idx{i}", [QP, 32], U32) for i in range(2)]
        wt = [sb(f"wt{i}", [QP, 32, 4]) for i in range(2)]
        lk2 = sb("lk2", [QP, 2, D])
        scr, one = sb("scr", [1, 2]), sb("one", [1, 2])
        ot = [sb(f"ot{i}", [QP, D]) for i in range(2)]
        pc = ps("pc", [128, 2, 512])
        po = ps("po", [128, 512])
        pt = ps("pt", [128, 2, 512])
        pd = ps("pd", [128, 2, 512])
        ready = sem("ready")
        x_raw, x_ld = [sem(f"x_raw{i}") for i in range(2)], [sem(f"x_ld{i}") for i in range(2)]
        cv_full, cv_used = sem("cv_full"), sem("cv_used")
        hp_done, hc_done = sem("hp_done"), sem("hc_done_t")
        tab_st = [sem(f"tab_st{i}") for i in range(2)]
        off_full, idx_done, dstep = sem("off_full"), sem("idx_done"), sem("dstep")
        g_done = [sem(f"g_done{i}") for i in range(2)]
        ip_step, ip_done = sem("ip_step"), sem("ip_done")
        tr_full, tr_used, dc_full, dc_leak, dc_used = (sem(n) for n in (
            "tr_full", "tr_used", "dc_full", "dc_leak", "dc_used"))
        ot_st = [sem(f"ot_st{i}") for i in range(2)]
        mark = sem("mark")
        START = 2
        x4 = w["x"].rearrange("b c (h y kh) w -> b c kh y h w", h=2, kh=4)
        slot = tab.rearrange("(s y x) c -> s y x c", s=2, y=PIT)
        hc5 = hc[:, :].rearrange("p (kh oh ow kw) -> p kh (oh ow) kw", kh=4, oh=GRID, kw=4)
        hcw = hc[:, :].rearrange("p (kh oh x) -> p oh kh x", kh=4, oh=GRID)
        hch = hc[:, :].rearrange("p (kh h x) -> p kh h x", kh=4, h=2)
        PIX = [[(y, 4) for y in range(YS[i], YS[i] + YN[i], 4)] for i in range(2)]
        ROWS = [[(h, y, 8) for h in range(2) for y in (0, 8)], [(0, 16, 8), (1, 16, 8), (slice(0, 2), 24, 4)]]
        NCH = [len(PIX[i]) + len(ROWS[i]) for i in range(2)]
        NCV = sum(NCH)
        TAB_LD = 16 * 16

        def walk(eng, conv, tail, points, finish, conv_first):

            def tile(b, j, t, ahead=True, new_points=True, before=True):
                if conv_first and ahead:
                    conv(b + 2, j, t)
                tail(b, j, t)
                if points is not None and eng is nc.tensor and t == 1 and ahead:
                    points(b + 2, j)
                if points is not None and eng is not nc.tensor and t == 0 and new_points:
                    points(b + 1, 1 - j)
                if not conv_first and ahead:
                    conv(b + 2, j, t)
                if before:
                    finish(*((b, j, 0) if t else (b - 1, 1 - j, 1)))

            tiles = 2 * NB
            for b in range(2):
                conv(b, b, 0)
                conv(b, b, 1)
                if points is not None:
                    points(b, b)
            tile(0, 0, 0, new_points=False, before=False)
            loops = (tiles - 5) // 4
            if loops > 0:
                with eng.Fori(0, loops) as i:
                    tile(2 * i, 0, 1)
                    tile(2 * i + 1, 1, 0)
                    tile(2 * i + 1, 1, 1)
                    tile(2 * i + 2, 0, 0)
            for g in range(1 + 4 * loops, tiles):
                tile(g // 2, g // 2 % 2, g % 2, ahead=g + 4 < tiles, new_points=g + 2 < tiles)
            finish(NB - 1, 1, 1)

        block = ctx.enter_context(nc.Block())

        @block.sync
        def _(sp):
            sp.dma_start(h0[0:NB // 2, NPOS:T, :], w["txt"][0:NB // 2]).then_inc(ot_st[0], 16)
            sp.dma_start(h0[NB // 2:NB, NPOS:T, :], w["txt"][NB // 2:NB]).then_inc(ot_st[1], 16)
            sp.wait_ge(ready, 3)

            def load_x(b, part, slot_free=None):
                for ch in range(3):
                    for h in range(2):
                        if slot_free is not None and (ch, h) == (2, 1):
                            slot_free()
                        sp.dma_start(xh[part][4 * ch:4 * ch + 4, :, h, :],
                                     x4[b, ch, :, YS[part]:YS[part] + YN[part], h, :]).then_inc(x_raw[part], 16)

            def shift_x(b, part):
                sp.wait_ge(x_raw[part], (b + 1) * (16 * 6))
                flat = xh[part][:, :, :, :].rearrange("p y h x -> p (y h x)")
                n = YN[part] * 2 * 224
                for kw in range(1, 4):
                    sp.dma_start(flat[12 * kw:12 * kw + 12, 0:n - kw], flat[0:12, kw:n]).then_inc(x_ld[part], 16)

            def store(dst, j, h, y, n, w):
                rows = hp[j][h * HS:(h + 1) * HS, y:y + 1, :]
                sp.dma_start(dst, bass.AP(tensor=rows.tensor, offset=rows.offset,
                                          ap=[rows.ap[0], [CO, n], [1, w]])).then_inc(tab_st[j], 16)

            def store_table(j, part):
                for dx in range(2):
                    for h in range(2):
                        ent = slot[j, :, 2 - dx:2 - dx + HS, :].rearrange("y x c -> x y c")
                        e0 = 2 + h * HR
                        lo, both = slice(2 * dx * CO, (2 * dx + 1) * CO), slice(2 * dx * CO, (2 * dx + 2) * CO)
                        hi = slice((2 * dx + 1) * CO, (2 * dx + 2) * CO)
                        if part == 0:
                            store(ent[:, e0:e0 + 15, both], j, h, 0, 15, 2 * CO)
                            store(ent[:, e0 - 1:e0, hi], j, h, 0, 1, CO)
                        else:
                            store(ent[:, e0 + 15:e0 + 27, both], j, h, 15, 12, 2 * CO)
                            store(ent[:, e0 + 27:e0 + 28, lo], j, h, 27, 1, CO)

            def image(b, j, more=True):
                gathered = None if isinstance(b, int) and b < 2 else lambda: sp.wait_ge(g_done[1], (b - 1) * (16 * TAPS))
                if more:
                    sp.wait_ge(cv_full, b * NCV + NCH[0])
                    load_x(b + 1, 0, gathered)
                else:
                    gathered()
                sp.wait_ge(hp_done, 2 * b + 1)
                store_table(j, 0)
                if more:
                    shift_x(b + 1, 0)
                sp.wait_ge(hp_done, 2 * b + 2)
                store_table(j, 1)
                if more:
                    sp.wait_ge(cv_full, b * NCV + NCV)
                    load_x(b + 1, 1)
                    shift_x(b + 1, 1)

            for part in range(2):
                load_x(0, part)
            for part in range(2):
                shift_x(0, part)
            image(0, 0)
            image(1, 1)
            if NB > 4:
                with sp.Fori(0, (NB - 4) // 2) as i:
                    image(2 * i + 2, 0)
                    image(2 * i + 3, 1)
            image(NB - 2, 0)
            image(NB - 1, 1, more=False)
            for j in range(2):
                sp.wait_ge(tab_st[j], TAB_LD * (NB // 2))
                sp.wait_ge(ot_st[j], 16 * (NB + 1))

        @block.gpsimd
        def _(pool):
            nc.gpsimd.memset(scr[:, :], 1.0).then_inc(ready, 1)
            for i in range(2):
                nc.gpsimd.memset(xh[i][:, :, :, :], 1.0).then_inc(ready, 1)

            pool.wait_ge(ready, 3)

            def tail(b, j, t):
                pool.wait_ge(idx_done, b + 1)
                pool.wait_ge(tab_st[j], (b // 2 + 1) * TAB_LD if isinstance(b, int) else
                             b * (TAB_LD // 2) + TAB_LD - j * (TAB_LD // 2))
                if not isinstance(b, int) or b >= 1:
                    pool.wait_ge(ip_done, 2 * b + t - 1)
                g = G[t][:, :, :, :].rearrange("p k a c -> p k (a c)")
                if not isinstance(b, int) or b or t:
                    pool.wait_ge(mark, 2 * b + t)
                nc.gpsimd.tensor_tensor(scr[:, 1:2], scr[:, 0:1], scr[:, 0:1], ALU.mult).then_inc(mark, 1)
                for k in range(TAPS):
                    nc.gpsimd.indirect_dma_start(
                        g[:, k, :], None, tab,
                        bass.IndirectOffsetOnAxis(ap=idx[j][:, t * TAPS + k:t * TAPS + k + 1], axis=0),
                    ).then_inc(g_done[t], 16)

            for b in range(2):
                for t in range(2):
                    tail(b, b, t)
            if NB > 2:
                with pool.Fori(0, (NB - 2) // 2) as i:
                    for j in range(2):
                        for t in range(2):
                            tail(2 * i + 2 + j, j, t)

        @block.tensor
        def _(pe):
            pe.wait_ge(ready, 3)
            ident = c["ident"]

            def conv(b, j, part):
                n = part * NCH[0]
                x = xh[part]
                pe.wait_ge(x_ld[part], (b + 1) * (16 * 3))

                def free(n):
                    if not isinstance(b, int) or b * NCV + n >= 2:
                        pe.wait_ge(cv_used, b * NCV + n - 1)

                for y0, ny in PIX[part]:
                    free(n)
                    for g in range(ny):
                        mm = nc.tensor.matmul(pc[0:2 * HS, n % 2, g * CO:(g + 1) * CO],
                                              x[0:49, y0 - YS[part] + g, :, 0:224:4], c["ws"][:, :],
                                              start=True, stop=True)
                    mm.then_inc(cv_full, 1)
                    n += 1
                for h, y, nr in ROWS[part]:
                    free(n)
                    nc.tensor.matmul(pc[0:CO, n % 2, 0:8 * HS], c["ws"][:, :],
                                     x[0:49, y - YS[part]:y - YS[part] + nr, h, 0:224:4],
                                     start=True, stop=True).then_inc(cv_full, 1)
                    n += 1

            def offsets(b, j):
                pe.wait_ge(hc_done, 2 * b + 2)
                if not isinstance(b, int) or b:
                    pe.wait_ge(idx_done, b)
                for t in range(2):
                    for k in range(TAPS):
                        mm = nc.tensor.matmul(po[0:QP, t * 32:(t + 1) * 32],
                                              hc5[:, k // 4, t * QP:(t + 1) * QP, k % 4], c["wo"][:, k, :],
                                              start=(k == 0), stop=(k == TAPS - 1))
                mm.then_inc(off_full, 1)

            def tail(b, j, t):
                pe.wait_ge(ip_done, 2 * b + t + 1)
                for f in range(NKT // 4):
                    pe.wait_ge(tr_used, START + (2 * b + t) * (NKT // 4) + f - 1)
                    for q in range(4):
                        k = 4 * f + q
                        mm = nc.tensor.transpose(pt[:, (t + f) % 2, q * QP:(q + 1) * QP],
                                                 sg[t][:, k * 128:(k + 1) * 128], ident[0:QP, 0:QP])
                    mm.then_inc(tr_full, 1)
                pe.wait_ge(tr_used, START + (2 * b + t + 1) * (NKT // 4))
                pe.wait_ge(dc_used, START + 2 * b + t - 1)
                for k in range(NKT):
                    nc.tensor.matmul(pd[0:QP, t, 0:D], sk[t][:, k, :], c["wd"][:, k, :], start=(k == 0), stop=False)
                mm = nc.tensor.matmul(pd[0:QP, t, 0:D], c["ones"][:, 0:QP], c["wb"][:, :], start=False, stop=True)
                mm.then_inc(dc_full, 1)

            walk(pe, conv, tail, offsets, lambda b, j, t: None, conv_first=True)

        @block.scalar
        def _(act):
            act.wait_ge(ready, 3)
            nc.scalar.activation(one[:, 0:1], scr[:, 0:1], ACT.Copy).then_inc(tr_used, START)

            def conv(b, j, part):
                n = part * NCH[0]
                if part == 0 and (not isinstance(b, int) or b >= 2):
                    act.wait_ge(tab_st[j], (TAB_LD // 2) * b - (TAB_LD // 2) * j)
                for y, ny in PIX[part]:
                    act.wait_ge(cv_full, b * NCV + n + 1)
                    nc.scalar.activation(hp[j][:, y:y + ny, :].rearrange("p g c -> p (g c)"),
                                         pc[0:2 * HS, n % 2, 0:ny * CO], ACT.Copy).then_inc(cv_used, 1)
                    n += 1
                if part == 0 and (not isinstance(b, int) or b):
                    act.wait_ge(off_full, b)
                for h, y, nr in ROWS[part]:
                    act.wait_ge(cv_full, b * NCV + n + 1)
                    if isinstance(h, int):
                        o0 = (h * HR + y) // 4
                        o = hcw[:, o0:o0 + nr // 4, :, :]
                        v = pc[0:CO, n % 2, 0:8 * HS].rearrange("p (oh kh x) -> p oh kh x", kh=4, x=HS)
                    else:
                        o = hcw[:, y // 4:GRID:HR // 4, :, :]
                        v = pc[0:CO, n % 2, 0:8 * HS].rearrange("p (kh oh x) -> p oh kh x", kh=4, x=HS)
                    nc.scalar.activation(o, v, ACT.Copy).then_inc(cv_used, 1)
                    n += 1

            def tail(b, j, t):
                for f in range(NKT // 4):
                    act.wait_ge(tr_full, (2 * b + t) * (NKT // 4) + f + 1)
                    nc.scalar.activation(sk[t][:, 4 * f:4 * f + 4, :],
                                         pt[:, (t + f) % 2, 0:4 * QP].rearrange("p (a b) -> p a b", a=4),
                                         ACT.Copy).then_inc(tr_used, 1)
                act.wait_ge(dc_full, 2 * b + t + 1)
                nc.scalar.activation(lk2[:, t, :], pd[0:QP, t, 0:D], ACT.Copy,
                                     scale=SLOPE).then_inc(dc_leak, 1)

            def finish(b, j, t):
                act.wait_ge(dc_used, START + 2 * b + t + 1)
                act.dma_start(h0[b, t * QP:(t + 1) * QP, :], ot[t][:, :]).then_inc(ot_st[t], 16)

            walk(act, conv, tail, None, finish, conv_first=True)

        @block.vector
        def _(dve):
            nc.vector.memset(one[:, 1:2], 0.0).then_inc(dc_used, START)

            def leaky(v, done):
                nc.vector.scalar_tensor_tensor(out=v, in0=v, scalar=SLOPE, in1=v, op0=ALU.mult,
                                               op1=ALU.max).then_inc(done, 1)

            def conv(b, j, part):
                y, n = YS[part], YN[part]
                dve.wait_ge(cv_used, b * NCV + part * NCH[0] + len(PIX[part]))
                leaky(hp[j][:, y:y + n, :].rearrange("p g c -> p (g c)"), hp_done)
                dve.wait_ge(cv_used, b * NCV + part * NCH[0] + NCH[part])
                leaky(hch[:, :, :, y // 4 * HS:(y + n) // 4 * HS], hc_done)

            def points(b, j):
                m = [0]

                def then(ins):
                    m[0] += 1
                    ins.then_inc(dstep, 1)
                    dve.wait_ge(dstep, b * 10 + m[0])

                dve.wait_ge(off_full, b + 1)
                then(nc.vector.tensor_tensor(pos[:, :], po[0:QP, 0:64],
                                             c["base"][:, :, :].rearrange("p a b -> p (a b)"), ALU.add))
                then(nc.vector.tensor_scalar(pos[:, :], pos[:, :], -2.0, HS + 0.5, ALU.max, ALU.min))
                then(nc.vector.tensor_copy(fli[:, :], pos[:, :]))
                then(nc.vector.tensor_copy(flo[:, :], fli[:, :]))
                then(nc.vector.tensor_tensor(fgt[:, :], flo[:, :], pos[:, :], ALU.is_gt))
                then(nc.vector.tensor_tensor(flo[:, :], flo[:, :], fgt[:, :], ALU.subtract))
                then(nc.vector.tensor_tensor(fr[:, :], pos[:, :], flo[:, :], ALU.subtract))
                then(nc.vector.tensor_scalar(om[:, :], fr[:, :], -1.0, 1.0, ALU.mult, ALU.add))
                f2 = flo[:, :].rearrange("p (k a) -> p k a", a=2)
                r2 = fr[:, :].rearrange("p (k a) -> p k a", a=2)
                o2 = om[:, :].rearrange("p (k a) -> p k a", a=2)
                then(nc.vector.tensor_scalar(idf[:, :], f2[:, :, 0], float(PIT), float(2 * PIT + 2 + j * NENT),
                                             ALU.mult, ALU.add))
                then(nc.vector.tensor_tensor(idf[:, :], idf[:, :], f2[:, :, 1], ALU.add))
                nc.vector.tensor_copy(idx[j][:, :], idf[:, :])
                nc.vector.tensor_tensor(wt[j][:, :, 0], o2[:, :, 0], o2[:, :, 1], ALU.mult)
                nc.vector.tensor_tensor(wt[j][:, :, 1], r2[:, :, 0], o2[:, :, 1], ALU.mult)
                nc.vector.tensor_tensor(wt[j][:, :, 2], o2[:, :, 0], r2[:, :, 1], ALU.mult)
                nc.vector.tensor_tensor(wt[j][:, :, 3], r2[:, :, 0], r2[:, :, 1],
                                        ALU.mult).then_inc(idx_done, 1)

            def tail(b, j, t):
                dve.wait_ge(g_done[t], (b + 1) * (16 * TAPS))
                g = G[t]
                g3 = g[:, :, :, :].rearrange("p k a c -> p (k a) c")
                wv = wt[j][:, t * TAPS:(t + 1) * TAPS, :].rearrange("p k a -> p (k a)")
                nc.vector.tensor_tensor(g3, g3, wv.unsqueeze(2).to_broadcast([QP, 4 * TAPS, CO]),
                                        ALU.mult).then_inc(ip_step, 1)
                dve.wait_ge(ip_step, (2 * b + t) * 2 + 1)
                nc.vector.tensor_tensor(g[:, :, 0:2, :], g[:, :, 0:2, :], g[:, :, 2:4, :],
                                        ALU.add).then_inc(ip_step, 1)
                dve.wait_ge(ip_step, (2 * b + t) * 2 + 2)
                nc.vector.tensor_tensor(sg[t][:, :].rearrange("p (k c) -> p k c", k=TAPS), g[:, :, 0, :], g[:, :, 1, :],
                                        ALU.add).then_inc(ip_done, 1)

            def finish(b, j, t):
                dve.wait_ge(dc_leak, 2 * b + t + 1)
                dve.wait_ge(ot_st[t], 16 * (b + 1))
                nc.vector.tensor_tensor(ot[t][:, :], pd[0:QP, t, 0:D], lk2[:, t, :],
                                        ALU.max).then_inc(dc_used, 1)

            walk(dve, conv, tail, points, finish, conv_first=False)


NR = 8
AHEAD = 4
HCR = 8
PAIRS = 7
SUMS = PAIRS + 2
BXR = 4
POOL_BX = (4, 6, 8, 10)
ND = NS - len(POOL_BX)
OUT_FILL = len(POOL_BX)
FRONT_FILL = OUT_FILL + 2
FILLS = FRONT_FILL + 10
ONE = 1


def mixer(nc, w, c, h0, wcd, pad, out, NB):
    with ExitStack() as ctx:
        sb = lambda n, s, d=F32: ctx.enter_context(nc.sbuf_tensor(n, s, d))
        ps = lambda n, s: ctx.enter_context(nc.psum_tensor(n, s, F32))
        sem = lambda n: ctx.enter_context(nc.semaphore(n))
        two = lambda n, s, d=F32: [sb(f"{n}{i}", s, d) for i in range(2)]
        NP = NB // 2
        UNITS = 8 * NP
        ident, sel = c["ident"], c["sel"]
        wc = sb("wct", [128, 6, DI])
        wz = sb("wz", [128, 2, DI])
        xpw = sb("xpw", [128, MT, XDR])
        dtw = sb("dtw", [128, DI])
        cdb = sb("cdb", [128, 2 * MT])
        ow = sb("ow", [128, MT, 256])
        pa = two("pa_", [128, MT * NS + MT])
        hw1, hw2 = sb("hw1", [128, 2, D]), sb("hw2", [128, 2, D])
        hb1, fb1 = sb("hb1", [128, 2]), sb("fb1", [128, FM])
        fb2 = sb("fb2", [1, D])
        HI, HT = two("HI", [TT, 3, D]), two("HT", [TT, 3, D])
        OT = sb("OT", [TT, 3, D])
        X0, X1 = two("X0", [128, 276]), two("X1", [128, 277])
        XC, Z, DT, U, YF = (two(n, [128, MT, T]) for n in ("XC", "Z", "DT", "U", "YF"))
        XD = two("XD", [128, T])
        SPL = two("SPL", [96, T], BF16)
        rem, unit = sb("rem", [96, T]), sb("unit", [96, T])
        AB = sb("AB", [128, MT, T])
        tiny, pause, pool_one = sb("tiny", [1, 2]), sb("pause", [1, 4]), sb("pool_one", [1, 1])
        dA = sb("dA", [128, NR, MT, T])
        bx = sb("bx", [128, BXR, MT, T])
        bs = sb("bs", [128, len(POOL_BX), T])
        hh = sb("hh", [128, 2, MT, T])
        hcr = sb("hcr", [128, HCR, MT, T])
        st6, mv = sb("st6", [TT, 3, 6]), sb("mv", [TT, 3, 2])
        var, lg, rs, nt = (sb(n, [TT, 3]) for n in ("var", "lg", "rs", "nt"))
        xn = sb("xn", [TT, 3, 256])
        xh, xf = sb("xh_m", [128, 2, T]), sb("xf", [128, 2, T])
        h1 = sb("h1", [128, 2, T])
        f1 = sb("f1", [128, FM, T])
        pY = ps("pY", [128, 1024])
        pB = ps("pB", [128, 512])
        pC = ps("pC", [128, 512])
        pF = ps("pF", [128, 2, 512])
        pQ = ps("pQ", [128, 2, 512])

        const_ld, zeroed = sem("const_ld"), sem("zeroed_m")
        front_ld, ow_ld = sem("front_ld"), sem("ow_ld")
        pa_ld = [sem(f"pa_ld{i}") for i in range(2)]
        hi_ld = [sem(f"hi_ld{i}") for i in range(2)]
        out_st = sem("out_st")
        fr_full, fr_used = sem("fr_full"), sem("fr_used")
        silu_x, silu_z = sem("silu_x"), sem("silu_z")
        dt_log, split_step, split_done, dt_done, u_done = (sem(n) for n in (
            "dt_log", "split_step", "split_done", "dt_done", "u_done"))
        ab_step = sem("ab_step")
        b_full, c_full, decay, bx_done, scan_done, hc_done, pair_done, y_done = (sem(n) for n in (
            "b_full", "c_full", "decay", "bx_done", "scan_done", "hc_done", "pair_done", "y_done"))
        yf_done, gated = sem("yf_done"), sem("gated")
        q_full, q_act, q_dve = sem("q_full"), sem("q_act"), sem("q_dve")
        pool_bx = sem("pool_bx")
        f1_done, ot_done, hi_used = sem("f1_done"), sem("ot_done"), sem("hi_used")
        ln_step, ln_var, ln_log, ln_exp, xn_done = (sem(n) for n in (
            "ln_step", "ln_var", "ln_log", "ln_exp", "xn_done"))

        consts = [(hw1[:, 0, :], w["head_w1"][0:KLO, :]), (hw1[0:KHI, 1, :], w["head_w1"][KLO:D, :]),
                  (hw2[:, 0, :], w["head_w2"][0:KLO, :]), (hw2[0:KHI, 1, :], w["head_w2"][KLO:D, :]),
                  (hw2[KHI:KHI + 1, 1, :], bcast(w["head_b2"], 1)),
                  (hb1[0:KLO, 0:1], w["head_b1"][0:KLO].unsqueeze(1)), (hb1[0:KHI, 1:2], w["head_b1"][KLO:D].unsqueeze(1)),
                  (fb1[:, :], w["ffn_b1"]), (fb2[:, :], bcast(w["ffn_b2"], 1))]
        FRONT_LD = 16 * 6
        LN_STEPS = 6

        TURNS = 4

        class Change:

            def __init__(self, pair, before, bank, head, incoming, tail, again):
                self.fills, self.act, self.dve, self.norms, self.nth = before
                self.head, self.incoming, self.tail = head, incoming, tail
                self.pair, self.bank, self.again = pair, bank, again
                self.seq = ""
                self.w1 = self.add("A" * FM, tail is not None)
                self.t1 = self.add("AA", incoming)
                self.h1 = self.add("AA", head is not None)
                self.hd = self.add("DD", head is not None)
                self.t2 = self.add("AA", head is not None)
                self.w2 = self.add("DD", tail is not None)
                self.norm2 = self.norms + (1 if incoming else 0)
                self.after = (self.fills + len(self.seq), self.act + self.seq.count("A"), self.dve + self.seq.count("D"),
                              self.norm2 + (0 if head is None else 1), self.nth + (0 if tail is None else 1))

            def add(self, fills, here):
                n = len(self.seq)
                self.seq += fills if here else ""
                return n

            def count(self, n, kind):
                return (self.act if kind == "A" else ONE + self.dve) + self.seq[:n + 1].count(kind)

        FILLS_PAIR, ACTS_PAIR, DVES_PAIR = 2 * (2 + 2 + 2 + 2 + FM + 2), 2 * (2 + 2 + 2 + FM), 2 * (2 + 2)

        def changes(p, incoming):
            before = (FILLS_PAIR * p + TURNS, ACTS_PAIR * p + TURNS, DVES_PAIR * p, 4 * p + 2, 2 * p)
            a = Change(p, before, 0, 0, incoming, None, incoming)
            b = Change(p, a.after, len(a.seq) % 2, 1, incoming, 0, incoming)
            return a, b, Change(p, b.after, (len(a.seq) + len(b.seq)) % 2, None, False, 1, incoming)

        def steps(eng, enter, step, leave):
            enter()
            step(0, 0, 0, 0, False, True, None)
            with eng.Fori(0, LAYERS - 1) as l:
                step(2 * l + 1, 1, 0, l + 1, True, True, None)
                step(2 * l + 2, 0, 0, l + 1, True, True, None)
            if NP > 1:
                with eng.Fori(0, NP - 1) as p:
                    a, b, c_ = changes(p, True)
                    step(8 * p + 7, 1, p + 1, 0, True, True, a)
                    step(8 * p + 8, 0, p + 1, 0, True, True, b)
                    step(8 * p + 9, 1, p + 1, 1, True, True, c_)
                    step(8 * p + 10, 0, p + 1, 1, True, True, None)
                    with eng.Fori(0, LAYERS - 2) as l:
                        step(8 * p + 2 * l + 11, 1, p + 1, l + 2, True, True, None)
                        step(8 * p + 2 * l + 12, 0, p + 1, l + 2, True, True, None)
            a, b, c_ = changes(NP - 1, False)
            step(UNITS - 1, 1, 0, 0, True, False, a)
            leave(b, c_)

        XP_FILL = 5
        CONV_AT = {2: (0, 3), 3: (3, 7), 4: (7, 11), 5: (11, 15), 6: (15, 18)}

        LAST_SUMS = {0: 4, 2: 3, 4: 1, 7: 0}

        def pieces(i, late):
            if i <= 7 + late:
                return [i - late] if i > late else []
            return {8: [], 9: [8, 9], 10: [10]}.get(i, [i]) if late else [i]

        SUM_AT = {7: (0,), 8: (2,), 9: (4,), 10: (6,), 11: (8,), 13: (10,), 14: (14,), 15: (12, 15)}

        W2_AT = (11, 12, 13)

        def before(i):
            return i - sum(n < i for n in POOL_BX)

        def fbase(u):
            return FILLS * u + 8

        LAST_OUT = fbase(UNITS - 1) + FRONT_FILL

        block = ctx.enter_context(nc.Block())

        @block.sync
        def _(sp):
            sp.wait_ge(zeroed, 7)
            for n, (dst, src) in enumerate(consts):
                sp.dma_start(dst, src).then_inc(const_ld if n < len(consts) - 1 else out_st, 16)

            def load_front(l):
                for dst, src in ((wc[:, :, :].rearrange("p a b -> p (a b)"), wcd[l]),
                                 (wz[:, 0, :], w["in_z"][l, 0:KLO]), (wz[0:KHI, 1, :], w["in_z"][l, KLO:D]),
                                 (xpw[:, :, :], w["xp"][l]), (dtw[96:96 + RANK, :], w["dtw"][l]),
                                 (cdb[:, :], w["cdb"][l])):
                    sp.dma_start(dst, src).then_inc(front_ld, 16)

            def load_h(n, s):
                sp.dma_start(HI[s][:, :, :], h0[n].rearrange("(t q) d -> q t d", q=TT)).then_inc(hi_ld[s], 16)

            def layers(p, u):
                with sp.Fori(0, LAYERS - 1) as l:
                    sp.wait_ge(fr_used, ONE + fbase(8 * p + 2 * l + 1))
                    load_front(l + 1)
                    sp.wait_ge(yf_done, ONE + 8 * p + 2 * l + 1)
                    sp.dma_start(pa[0][:, :], pad[l + 1]).then_inc(pa_ld[0], 16)
                    sp.wait_ge(yf_done, ONE + 8 * p + 2 * l + 2)
                    sp.dma_start(pa[1][:, :], pad[l + 1]).then_inc(pa_ld[1], 16)
                    sp.wait_ge(fr_used, ONE + fbase(8 * p + 2 * l + 2) + FRONT_FILL)
                    sp.dma_start(ow[:, :, :], w["ow"][l + 1]).then_inc(ow_ld, 16)

            for s in range(2):
                load_h(s, s)
            load_front(0)
            sp.dma_start(ow[:, :, :], w["ow"][0]).then_inc(ow_ld, 16)
            for s in range(2):
                sp.dma_start(pa[s][:, :], pad[0]).then_inc(pa_ld[s], 16)
            if NP > 1:
                with sp.Fori(0, NP - 1) as p:
                    layers(p, 8 * p)
                    for s in range(2):
                        sp.wait_ge(hi_used, 2 * p + s + 1)
                        load_h(2 * p + 2 + s, s)
                    sp.wait_ge(fr_used, ONE + fbase(8 * p + 7))
                    load_front(0)
                    sp.wait_ge(yf_done, ONE + 8 * p + 7)
                    sp.dma_start(pa[0][:, :], pad[0]).then_inc(pa_ld[0], 16)
                    sp.wait_ge(yf_done, ONE + 8 * p + 8)
                    sp.dma_start(pa[1][:, :], pad[0]).then_inc(pa_ld[1], 16)
                    sp.wait_ge(fr_used, ONE + fbase(8 * p + 8) + FRONT_FILL)
                    sp.dma_start(ow[:, :, :], w["ow"][0]).then_inc(ow_ld, 16)
            layers(NP - 1, UNITS - 8)
            sp.wait_ge(out_st, 16 * (NB + 1))

        @block.gpsimd
        def _(pool):
            for i in range(2):
                nc.gpsimd.memset(X0[i][:, :], 0.0).then_inc(zeroed, 1)
                nc.gpsimd.memset(X1[i][:, :], 0.0).then_inc(zeroed, 1)
            nc.gpsimd.memset(dA[:, :, :, :], 0.0).then_inc(zeroed, 1)
            pool.wait_ge(zeroed, 5)
            nc.gpsimd.memset(h1[KHI:KHI + 1, 1, :], 1.0).then_inc(zeroed, 1)
            pool.wait_ge(zeroed, 6)
            nc.gpsimd.memset(unit[:, :], 1.0).then_inc(zeroed, 1)
            pool.wait_ge(zeroed, 7)
            nc.gpsimd.memset(pool_one[:, :], 0.0).then_inc(u_done, ONE)

            def pair(u, j):
                pool.wait_ge(hc_done, ONE + u * NS + 2 * j + 2)
                a, b = (2 * j) % HCR, (2 * j + 1) % HCR
                nc.gpsimd.tensor_tensor(hcr[:, a, :, :], hcr[:, a, :, :], hcr[:, b, :, :], ALU.add).then_inc(pair_done, 1)
                if j < PAIRS - 1:
                    pool.wait_ge(pair_done, u * PAIRS + j + 1)

            def split(u, s):
                hi, x = SPL[s], XD[s]
                n = [0]

                def then(ins):
                    n[0] += 1
                    ins.then_inc(split_step, 1)
                    pool.wait_ge(split_step, u * 5 + n[0])

                pool.wait_ge(fr_used, ONE + (fbase(u - 1) + FRONT_FILL if not isinstance(u, int) or u else 0) + XP_FILL + 1)
                then(nc.gpsimd.tensor_tensor(hi[:, :], x[0:96, :], unit[:, :], ALU.mult))
                then(nc.gpsimd.tensor_tensor(rem[:, :], x[0:96, :], hi[:, :], ALU.subtract))
                then(nc.gpsimd.tensor_tensor(hi[32:64, :], rem[32:64, :], unit[32:64, :], ALU.mult))
                then(nc.gpsimd.tensor_tensor(hi[64:96, :], rem[64:96, :], unit[64:96, :], ALU.mult))
                then(nc.gpsimd.tensor_tensor(rem[64:96, :], rem[64:96, :], hi[64:96, :], ALU.subtract))
                nc.gpsimd.tensor_tensor(hi[64:96, :], rem[64:96, :], unit[64:96, :], ALU.mult).then_inc(split_done, 1)
                pool.wait_ge(split_done, u + 1)

            def bx_op(u, s, n):
                i = POOL_BX[n]
                pool.wait_ge(fr_used, ONE + fbase(u) + n + 1 + (0 if not isinstance(u, int) or u else 2))
                pool.wait_ge(scan_done, u * NS + i - BXR + 1)
                nc.gpsimd.tensor_tensor(bx[:, i % BXR, :, :], U[s][:, :, :],
                                        bs[:, n, :].unsqueeze(1).to_broadcast([128, MT, T]), ALU.mult).then_inc(pool_bx, 1)
                pool.wait_ge(pool_bx, u * len(POOL_BX) + n + 1)

            def step_size(u, s):
                pool.wait_ge(dt_log, u + 1)
                nc.gpsimd.tensor_tensor(DT[s][:, :, :], DT[s][:, :, :], AB[:, :, :], ALU.add).then_inc(dt_done, 1)
                pool.wait_ge(dt_done, u + 1)
                nc.gpsimd.tensor_tensor(U[s][:, :, :], DT[s][:, :, :], XC[s][:, :, :], ALU.mult).then_inc(u_done, 1)
                pool.wait_ge(u_done, ONE + u + 1)

            def gate(v, s):
                pool.wait_ge(pair_done, (v + 1) * PAIRS)
                pool.wait_ge(yf_done, ONE + v + 1)
                pool.wait_ge(silu_z, v + 1)
                nc.gpsimd.tensor_tensor(YF[s][:, :, :], YF[s][:, :, :], Z[s][:, :, :], ALU.mult).then_inc(gated, 1)
                pool.wait_ge(gated, v + 1)

            def enter():
                pool.wait_ge(u_done, ONE)
                split(0, 0)
                step_size(0, 0)

            def step(u, s, p, l, has_out, has_front, ch):
                if has_out:
                    gate(u - 1, 1 - s)
                for j in range(PAIRS):
                    if has_front and j == 5:
                        split(u + 1, 1 - s)
                    if has_front and j == 6:
                        step_size(u + 1, 1 - s)
                    pair(u, j)
                    if j < len(POOL_BX):
                        bx_op(u, s, j)

            steps(pool, enter, step, lambda b, c_: gate(UNITS - 1, 1))

        @block.tensor
        def _(pe):
            pe.wait_ge(const_ld, 16 * (len(consts) - 1))
            pe.wait_ge(out_st, 16)
            pe.wait_ge(zeroed, 7)

            def fill_free(f, n):
                pe.wait_ge(fr_used, ONE + f + n - 1)

            def out_mm(v, f, s, n):
                if n == 0:
                    pe.wait_ge(gated, v + 1)
                fill_free(f, n)
                for k in range(MT):
                    mm = nc.tensor.matmul(pF[:, n, 0:T], ow[:, k, n * 128:(n + 1) * 128], YF[s][:, k, :],
                                          start=(k == 0), stop=(k == MT - 1))
                mm.then_inc(fr_full, 1)

            def conv_mm(f, s, k):
                m, j = k // 6, k % 6
                if j == 0 and (not isinstance(f, int) or f + m):
                    fill_free(f, m)
                rhs = X0[s][:, j:j + T] if j < 4 else X1[s][:, 3 - 2 * (j - 4):3 - 2 * (j - 4) + T]
                mm = nc.tensor.matmul(pF[:, m % 2, 0:T], wc[:, j, m * 128:(m + 1) * 128], rhs,
                                      start=(j == 0), stop=(j == 5))
                if j == 5:
                    mm.then_inc(fr_full, 1)

            def z_mm(f, s, m, n):
                fill_free(f, n)
                o = pF[:, n % 2, 0:T]
                nc.tensor.matmul(o, wz[:, 0, m * 128:(m + 1) * 128], X0[s][:, 3:3 + T], start=True, stop=False)
                nc.tensor.matmul(o, wz[0:KHI, 1, m * 128:(m + 1) * 128], X1[s][0:KHI, 3:3 + T],
                                 start=False, stop=True).then_inc(fr_full, 1)

            def xp_mm(u, f, s, n):
                pe.wait_ge(silu_x, u + 1)
                fill_free(f, n)
                for k in range(MT):
                    mm = nc.tensor.matmul(pF[0:XDR, n % 2, 0:T], xpw[:, k, :], XC[s][:, k, :],
                                          start=(k == 0), stop=(k == MT - 1))
                mm.then_inc(fr_full, 1)

            def dt_mm(f, s, m, n):
                pe.wait_ge(fr_used, ONE + f + XP_FILL + 1)
                fill_free(f, n)
                nc.tensor.matmul(pF[:, n % 2, 0:T], dtw[96:96 + RANK, m * 128:(m + 1) * 128],
                                 XD[s][96:96 + RANK, :], start=True, stop=True).then_inc(fr_full, 1)

            def front_mm(u, f, s, i):
                for k in range(*CONV_AT.get(i, (0, 0))):
                    conv_mm(f, s, k)
                if i == 6:
                    z_mm(f, s, 0, 3)
                if i == 7:
                    z_mm(f, s, 1, 4)
                if i == 8:
                    xp_mm(u, f, s, XP_FILL)
                if i == 10:
                    dt_mm(f, s, 0, 6)
                    dt_mm(f, s, 1, 7)
                if i == 11:
                    dt_mm(f, s, 2, 8)
                if i == 12:
                    z_mm(f, s, 2, 9)

            def b_mm(u, s, i):
                pe.wait_ge(bx_done, ONE + u * ND + before(i))
                nc.tensor.matmul(pB[:, 0:T], sel[:, i, :], SPL[s][:, :], start=True, stop=True).then_inc(b_full, 1)

            def c_mm(u, s, i):
                pe.wait_ge(hc_done, ONE + u * NS + i)
                nc.tensor.matmul(pC[:, 0:T], sel[:, NS + i, :], SPL[s][:, :], start=True, stop=True).then_inc(c_full, 1)

            def y_mm(u, i):
                if i < 2 * PAIRS:
                    pe.wait_ge(pair_done, u * PAIRS + i // 2 + 1)
                else:
                    pe.wait_ge(hc_done, ONE + u * NS + i + 1)
                if i == 0:
                    pe.wait_ge(yf_done, ONE + u)
                y = hcr[:, i % HCR, :, :].rearrange("p m t -> p (m t)")
                nc.tensor.matmul(pY[:, 0:512], ident[:, :], y[:, 0:512], start=(i == 0), stop=(i == NS - 1))
                nc.tensor.matmul(pY[:, 512:NY], ident[:, :], y[:, 512:NY], start=(i == 0),
                                 stop=(i == NS - 1)).then_inc(y_done, 1)

            def q_free(ch, n):
                if n >= 2:
                    k = ch.seq[n - 2]
                    pe.wait_ge(q_act if k == "A" else q_dve, ch.count(n - 2, k))
                else:
                    pe.wait_ge(q_act, ch.act)
                    pe.wait_ge(q_dve, ONE + ch.dve)

            def transposes(bank):
                for h in range(2):
                    for t in range(3):
                        mm = nc.tensor.transpose(pQ[:, (bank + h) % 2, t * TT:(t + 1) * TT],
                                                 xn[:, t, h * 128:(h + 1) * 128], ident[0:TT, 0:TT])
                    mm.then_inc(q_full, 1)

            def ffn_hidden(ch, i):
                if i < FM // 2:
                    for m in range(2 * i, 2 * i + 2):
                        q_free(ch, ch.w1 + m)
                        o = pQ[:, (ch.w1 + m + ch.bank) % 2, 0:T]
                        nc.tensor.matmul(o, c["w1q"][:, 0, m * 128:(m + 1) * 128], xf[:, 0, :], start=True, stop=False)
                        nc.tensor.matmul(o, c["w1q"][0:KHI, 1, m * 128:(m + 1) * 128], xf[0:KHI, 1, :],
                                         start=False, stop=True).then_inc(q_full, 1)

            def change(ch, i, out_done):
                bank = lambda n: (n + ch.bank) % 2
                if ch.incoming and i == 2:
                    pe.wait_ge(xn_done, ch.norms + 1)
                    q_free(ch, ch.t1)
                    q_free(ch, ch.t1 + 1)
                    transposes(bank(ch.t1))
                if ch.head is not None and i == 3:
                    pe.wait_ge(fr_used, ONE + out_done)
                    for m in range(2):
                        R, n = (KLO, KHI)[m], ch.h1 + m
                        q_free(ch, n)
                        o = pQ[0:R, bank(n), 0:T]
                        nc.tensor.matmul(o, hw1[:, 0, m * 128:m * 128 + R], xh[:, 0, :], start=True, stop=False)
                        nc.tensor.matmul(o, hw1[0:KHI, 1, m * 128:m * 128 + R], xh[0:KHI, 1, :],
                                         start=False, stop=True).then_inc(q_full, 1)
                if ch.head is not None and i == 5:
                    pe.wait_ge(q_act, ch.count(ch.h1 + 1, "A"))
                    for k in range(3):
                        n, col = ch.hd + k // 2, k % 2 * D
                        if k % 2 == 0:
                            q_free(ch, n)
                        o = pQ[0:TT, bank(n), col:col + D]
                        nc.tensor.matmul(o, h1[:, 0, k * TT:(k + 1) * TT], hw2[:, 0, :], start=True, stop=False)
                        mm = nc.tensor.matmul(o, h1[0:KHI + 1, 1, k * TT:(k + 1) * TT], hw2[0:KHI + 1, 1, :],
                                              start=False, stop=True)
                        if k:
                            mm.then_inc(q_full, 1)
                if ch.head is not None and i == 10:
                    pe.wait_ge(xn_done, ch.norm2 + 1)
                    q_free(ch, ch.t2)
                    q_free(ch, ch.t2 + 1)
                    transposes(bank(ch.t2))
                if ch.tail is not None and i in W2_AT:
                    k = W2_AT.index(i)
                    pe.wait_ge(f1_done, ch.nth + 1)
                    n, col = ch.w2 + k // 2, k % 2 * D
                    if k % 2 == 0:
                        q_free(ch, n)
                    o = pQ[0:TT, bank(n), col:col + D]
                    for m in range(FM):
                        nc.tensor.matmul(o, f1[:, m, k * TT:(k + 1) * TT], c["w2q"][:, m, :], start=(m == 0), stop=False)
                    mm = nc.tensor.matmul(o, c["ones"][:, 0:TT], fb2[:, :], start=False, stop=True)
                    if k:
                        mm.then_inc(q_full, 1)

            def step(u, s, p, l, has_out, has_front, ch):
                f, o = fbase(u), 1 - s
                for i in range(NS):
                    if i == NS - 2 and has_front:
                        pe.wait_ge(split_done, u + 2)
                    if i < NS - 1:
                        c_mm(u, s, i + 1)
                    elif has_front:
                        c_mm(u + 1, o, 0)
                    if i < NS - 2 and i + 2 not in POOL_BX:
                        b_mm(u, s, i + 2)
                    elif i >= NS - 2 and has_front:
                        b_mm(u + 1, o, i - (NS - 2))
                    if i == 0:
                        b0 = f + (0 if has_out else 2)
                        for n in range(len(POOL_BX)):
                            fill_free(b0, n)
                            nc.tensor.matmul(pF[:, n % 2, 0:T], sel[:, POOL_BX[n], :], SPL[s][:, :],
                                             start=True, stop=True).then_inc(fr_full, 1)
                    for k in SUM_AT.get(i, ()):
                        y_mm(u, k)
                    if ch is not None and ch.tail is not None:
                        ffn_hidden(ch, i)
                    if has_out and i < 2:
                        if i == 0:
                            pe.wait_ge(ow_ld, 16 * (4 * p + l + (0 if has_front else UNITS // 2)))
                        out_mm(u - 1, f + OUT_FILL, o, i)
                    if ch is not None:
                        change(ch, i, f + FRONT_FILL)
                    late = 1 if ch is not None and ch.incoming else 0
                    if has_front:
                        if i == 2 + late:
                            pe.wait_ge(front_ld, FRONT_LD * (4 * p + l + 1))
                            if late:
                                pe.wait_ge(q_act, ch.count(ch.t1 + 1, "A"))
                            elif has_out:
                                pe.wait_ge(fr_used, ONE + f + FRONT_FILL)
                            else:
                                pe.wait_ge(q_act, 4)
                        for k in pieces(i, late):
                            front_mm(u + 1, f + FRONT_FILL, o, k)

            def enter():
                for s in range(2):
                    pe.wait_ge(xn_done, s + 1)
                    if s:
                        pe.wait_ge(q_act, 2)
                    transposes(0)
                pe.wait_ge(front_ld, FRONT_LD)
                pe.wait_ge(q_act, 2)
                for i in range(NS):
                    front_mm(0, 0, 0, i)
                pe.wait_ge(split_done, 1)
                b_mm(0, 0, 0)
                c_mm(0, 0, 0)
                b_mm(0, 0, 1)

            def leave(b, c_):
                f = LAST_OUT
                for n in range(2):
                    out_mm(UNITS - 1, f, 1, n)
                for ch in (b, c_):
                    for i in range(NS):
                        ffn_hidden(ch, i)
                        change(ch, i, f + 2)

            steps(pe, enter, step, leave)

        @block.scalar
        def _(act):
            act.wait_ge(const_ld, 16 * (len(consts) - 1))
            act.wait_ge(zeroed, 7)
            nc.scalar.activation(tiny[:, 1:2], c["ones"][:, 0:1], ACT.Copy).then_inc(fr_used, ONE)

            def evac_head(f):
                for m in range(2):
                    R = (KLO, KHI)[m]
                    act.wait_ge(fr_full, f + m + 1)
                    nc.scalar.activation(xh[0:R, m, :], pF[0:R, m, 0:T], ACT.Copy).then_inc(fr_used, 1)

            def evac_out(f, s):
                act.wait_ge(fr_full, f + 1)
                nc.scalar.activation(X0[s][:, 3:3 + T], pF[:, 0, 0:T], ACT.Copy).then_inc(fr_used, 1)
                act.wait_ge(fr_full, f + 2)
                nc.scalar.activation(X1[s][0:KHI, 3:3 + T], pF[0:KHI, 1, 0:T], ACT.Copy)
                nc.scalar.activation(X1[s][KHI:128, 4:4 + T], pF[KHI:128, 1, 0:T], ACT.Copy).then_inc(fr_used, 1)

            def decays(u, s, i, fresh=False):
                if not fresh:
                    act.wait_ge(scan_done, u * NS + i - (NR - 1))
                for m in range(MT):
                    a = nc.scalar.activation(dA[:, i % NR, m, 1:T], DT[s][:, m, 1:T], ACT.Exp,
                                             scale=pa[s][:, m * NS + i:m * NS + i + 1])
                a.then_inc(decay, 1)

            def z_evac(f, s, m, n):
                act.wait_ge(fr_full, f + n + 1)
                nc.scalar.activation(Z[s][:, m, :], pF[:, n % 2, 0:T], ACT.Copy).then_inc(fr_used, 1)

            def gate_silu(s, f):
                act.wait_ge(fr_used, ONE + f)
                nc.scalar.activation(Z[s][:, :, :], Z[s][:, :, :], ACT.Silu).then_inc(silu_z, 1)

            def log_exp_table():
                act.preload_act_table_set("natural_log_exp_and_others")

            def dt_evac(f, s, m, n):
                act.wait_ge(fr_full, f + n + 1)
                b = cdb[:, MT + m:MT + m + 1]
                nc.scalar.activation(AB[:, m, :], pF[:, n % 2, 0:T], ACT.Abs, bias=b)
                nc.scalar.activation(DT[s][:, m, :], pF[:, n % 2, 0:T], ACT.Relu, bias=b).then_inc(fr_used, 1)

            def front(u, f, s, i, scanned):
                if i in (4, 6, 7):
                    m = {4: 0, 6: 1, 7: 2}[i]
                    act.wait_ge(fr_full, f + m + 1)
                    nc.scalar.activation(XC[s][:, m, :], pF[:, m % 2, 0:T], ACT.Identity,
                                         bias=cdb[:, m:m + 1]).then_inc(fr_used, 1)
                if i == 7:
                    z_evac(f, s, 0, 3)
                    act.wait_ge(fr_used, ONE + f + 3)
                    nc.scalar.activation(XC[s][:, :, :], XC[s][:, :, :], ACT.Silu).then_inc(silu_x, 1)
                    if scanned:
                        gate_silu(1 - s, f)
                    z_evac(f, s, 1, 4)
                    log_exp_table()
                if i == 9:
                    act.wait_ge(fr_full, f + XP_FILL + 1)
                    nc.scalar.activation(XD[s][0:XDR, :], pF[0:XDR, XP_FILL % 2, 0:T], ACT.Copy).then_inc(fr_used, 1)
                if i == 10:
                    dt_evac(f, s, 0, 6)
                if i == 11:
                    dt_evac(f, s, 1, 7)
                    dt_evac(f, s, 2, 8)
                    act.wait_ge(fr_used, ONE + f + 9)
                    nc.scalar.activation(AB[:, :, :], AB[:, :, :], ACT.Exp, scale=-1.0).then_inc(ab_step, 1)
                    act.wait_ge(ab_step, u + 1)
                    nc.scalar.activation(AB[:, :, :], AB[:, :, :], ACT.Ln, bias=1.0).then_inc(dt_log, 1)
                if i == 12:
                    z_evac(f, s, 2, 9)

            def rstd(g):
                act.wait_ge(ln_var, g + 1)
                nc.scalar.activation(lg[:, :], var[:, :], ACT.Ln).then_inc(ln_log, 1)
                act.wait_ge(ln_log, g + 1)
                nc.scalar.activation(rs[:, :], lg[:, :], ACT.Exp, scale=-0.5).then_inc(ln_exp, 1)

            def take_x(fills, s, b):
                act.wait_ge(q_full, fills + 1)
                nc.scalar.activation(X0[s][:, 3:3 + T], pQ[:, b, 0:T], ACT.Copy).then_inc(q_act, 1)
                act.wait_ge(q_full, fills + 2)
                nc.scalar.activation(X1[s][0:KHI, 3:3 + T], pQ[0:KHI, 1 - b, 0:T], ACT.Copy)
                nc.scalar.activation(X1[s][KHI:128, 4:4 + T], pQ[KHI:128, 1 - b, 0:T], ACT.Copy).then_inc(q_act, 1)

            def change(ch, i):
                bank = lambda n: (n + ch.bank) % 2
                if ch.tail is not None and i < FM // 2:
                    for m in range(2 * i, 2 * i + 2):
                        n = ch.w1 + m
                        act.wait_ge(q_full, ch.fills + n + 1)
                        nc.scalar.activation(f1[:, m, :], pQ[:, bank(n), 0:T], ACT.Identity,
                                             bias=fb1[:, m:m + 1]).then_inc(q_act, 1)
                if ch.tail is not None and i == 4:
                    act.wait_ge(q_act, ch.count(ch.w1 + FM - 1, "A"))
                    nc.scalar.activation(f1[:, :, :], f1[:, :, :], ACT.Gelu).then_inc(f1_done, 1)
                    log_exp_table()
                if ch.incoming and i == 0:
                    rstd(ch.norms)
                if ch.incoming and i == 2:
                    take_x(ch.fills + ch.t1, ch.head, bank(ch.t1))
                if ch.head is not None:
                    if i == 3:
                        for m in range(2):
                            R, n = (KLO, KHI)[m], ch.h1 + m
                            act.wait_ge(q_full, ch.fills + n + 1)
                            nc.scalar.activation(h1[0:R, m, :], pQ[0:R, bank(n), 0:T], ACT.Relu,
                                                 bias=hb1[0:R, m:m + 1]).then_inc(q_act, 1)
                    if i == 8:
                        rstd(ch.norm2)
                    if i == 11:
                        for m in range(2):
                            R, n = (KLO, KHI)[m], ch.t2 + m
                            act.wait_ge(q_full, ch.fills + n + 1)
                            nc.scalar.activation(xf[0:R, m, :], pQ[0:R, bank(n), 0:T], ACT.Copy).then_inc(q_act, 1)
                if ch.tail is not None and i == NS - 1:
                    act.wait_ge(ot_done, ch.nth + 1)
                    act.dma_start(out[ch.nth].rearrange("(t q) d -> q t d", q=TT), OT[:, :, :]).then_inc(out_st, 16)

            def step(u, s, p, l, has_out, has_front, ch):
                f, o = fbase(u), 1 - s
                for i in range(NS):
                    if i == 0:
                        b0 = f + (0 if has_out else 2)
                        for n in range(len(POOL_BX)):
                            act.wait_ge(fr_full, b0 + n + 1)
                            if n == 0 and (not isinstance(u, int) or u):
                                act.wait_ge(pool_bx, u * len(POOL_BX))
                            nc.scalar.activation(bs[:, n, :], pF[:, n % 2, 0:T], ACT.Copy).then_inc(fr_used, 1)
                    if i < NS - AHEAD:
                        decays(u, s, i + AHEAD, fresh=isinstance(u, int) and u == 0 and i + AHEAD < NR)
                    elif has_front:
                        if i == NS - AHEAD:
                            act.wait_ge(pa_ld[o], 16 * (4 * p + l + 1))
                        else:
                            act.wait_ge(dt_done, u + 2)
                            for k in {13: (0,), 14: (1, 2), 15: (3,)}[i]:
                                decays(u + 1, o, k)
                    if i == 1 and has_out:
                        evac_out(f + OUT_FILL, o) if ch is None or ch.head is None else evac_head(f + OUT_FILL)
                    if ch is not None:
                        change(ch, i)
                    if has_front:
                        if i == 4:
                            act.wait_ge(front_ld, FRONT_LD * (4 * p + l + 1))
                        for k in pieces(i, 1 if ch is not None and ch.incoming else 0):
                            front(u + 1, f + FRONT_FILL, o, k, True)
                    elif i == 8:
                        gate_silu(s, f)
                        log_exp_table()

            def enter():
                log_exp_table()
                for s in range(2):
                    rstd(s)
                    take_x(2 * s, s, 0)
                act.wait_ge(front_ld, FRONT_LD)
                for i in range(NS):
                    front(0, 0, 0, i, False)
                act.wait_ge(dt_done, 1)
                act.wait_ge(pa_ld[0], 16)
                for i in range(AHEAD):
                    decays(0, 0, i, fresh=True)

            def leave(b, c_):
                evac_head(LAST_OUT)
                for ch in (b, c_):
                    for i in range(NS):
                        change(ch, i)

            steps(act, enter, step, leave)

        @block.vector
        def _(dve):
            dve.wait_ge(zeroed, 7)
            for n, q in enumerate((bx_done, hc_done, yf_done, q_dve)):
                nc.vector.memset(pause[:, n:n + 1], 0.0).then_inc(q, ONE)

            def then(ins, g, n):
                ins.then_inc(ln_step, 1)
                dve.wait_ge(ln_step, g * LN_STEPS + n)

            def moments(src, g):
                for t in range(3):
                    last = nc.vector.bn_stats(st6[:, t, :], src[:, t, :])
                then(last, g, 1)
                nc.vector.memset(nt[:, :], 0.0)
                for t in range(3):
                    last = nc.vector.bn_aggr(mv[:, t, :], st6[:, t, :])
                then(last, g, 2)
                nc.vector.tensor_scalar(var[:, :], mv[:, :, 1], EPS, None, ALU.add).then_inc(ln_var, 1)

            def normalize(src, g):
                dve.wait_ge(ln_exp, g + 1)
                then(nc.vector.tensor_tensor(nt[:, :], rs[:, :], rs[:, :], ALU.mult), g, 3)
                then(nc.vector.tensor_tensor(nt[:, :], nt[:, :], var[:, :], ALU.mult), g, 4)
                then(nc.vector.tensor_scalar(nt[:, :], nt[:, :], -0.5, 1.5, ALU.mult, ALU.add), g, 5)
                then(nc.vector.tensor_tensor(rs[:, :], rs[:, :], nt[:, :], ALU.mult), g, 6)
                for t in range(3):
                    nc.vector.tensor_scalar(xn[:, t, 0:D], src[:, t, :], mv[:, t, 0:1], rs[:, t:t + 1],
                                            ALU.subtract, ALU.mult)
                    last = nc.vector.tensor_scalar(xn[:, t, D:256], src[:, t, KLO:D], mv[:, t, 0:1], rs[:, t:t + 1],
                                                   ALU.subtract, ALU.mult)
                last.then_inc(xn_done, 1)

            def bx_op(u, s, i):
                dve.wait_ge(b_full, u * ND + before(i) + 1)
                nc.vector.tensor_tensor(bx[:, i % BXR, :, :], U[s][:, :, :],
                                        pB[:, 0:T].unsqueeze(1).to_broadcast([128, MT, T]),
                                        ALU.mult).then_inc(bx_done, 1)

            def scan_op(u, s, i):
                dve.wait_ge(decay, u * NS + i + 1)
                if i in POOL_BX:
                    dve.wait_ge(pool_bx, u * len(POOL_BX) + POOL_BX.index(i) + 1)
                else:
                    dve.wait_ge(bx_done, ONE + u * ND + before(i) + 1)
                flat = lambda t: t[:, :, :].rearrange("p m t -> p (m t)")
                nc.vector.tensor_tensor_scan(flat(hh[:, i % 2, :, :]), flat(dA[:, i % NR, :, :]),
                                             flat(bx[:, i % BXR, :, :]), 0.0, ALU.mult, ALU.add).then_inc(scan_done, 1)

            def hc_op(u, s, i):
                dve.wait_ge(c_full, u * NS + i + 1)
                dve.wait_ge(scan_done, u * NS + i + 1)
                if i >= HCR and i % 2 == 0:
                    dve.wait_ge(y_done, u * SUMS + (i - HCR) // 2 + 1)
                elif i in LAST_SUMS and (not isinstance(u, int) or u):
                    dve.wait_ge(y_done, u * SUMS - LAST_SUMS[i])
                nc.vector.tensor_tensor(hcr[:, i % HCR, :, :], hh[:, i % 2, :, :],
                                        pC[:, 0:T].unsqueeze(1).to_broadcast([128, MT, T]),
                                        ALU.mult).then_inc(hc_done, 1)

            def yf_op(v, s):
                dve.wait_ge(y_done, (v + 1) * SUMS)
                for m in range(MT):
                    last = nc.vector.scalar_tensor_tensor(out=YF[s][:, m, :], in0=XC[s][:, m, :],
                                                          scalar=pa[s][:, MT * NS + m:MT * NS + m + 1],
                                                          in1=pY[:, m * T:(m + 1) * T], op0=ALU.mult, op1=ALU.add)
                last.then_inc(yf_done, 1)

            def add_tiles(dst, src, k, ch, n):
                w = k.stop - k.start
                dve.wait_ge(q_full, ch.fills + n + 1)
                nc.vector.tensor_tensor(dst[:, k, :], src[:, k, :],
                                        pQ[0:TT, (n + ch.bank) % 2, 0:w * D].rearrange("p (k d) -> p k d", k=w),
                                        ALU.add).then_inc(q_dve, 1)

            def change(ch, i):
                s, q = ch.head, ch.tail
                if ch.incoming and i == 0:
                    dve.wait_ge(hi_ld[s], 16 * (ch.pair + 2))
                    moments(HI[s], ch.norms)
                if ch.incoming and i == 1:
                    normalize(HI[s], ch.norms)
                if s is not None and i == 7:
                    for k, n in ((slice(0, 2), ch.hd), (slice(2, 3), ch.hd + 1)):
                        add_tiles(HT[s], HT[s], k, ch, n)
                    dve.wait_ge(q_dve, ch.count(ch.hd + 1, "D"))
                    moments(HT[s], ch.norm2)
                if s is not None and i == 9:
                    dve.wait_ge(q_full, ch.fills + ch.t1 + (2 if ch.incoming else 0))
                    normalize(HT[s], ch.norm2)
                if q is not None and i == 14:
                    dve.wait_ge(out_st, 16 * (ch.nth + 1))
                    add_tiles(OT, HT[q], slice(0, 2), ch, ch.w2)
                if q is not None and i == 15:
                    add_tiles(OT, HT[q], slice(2, 3), ch, ch.w2 + 1)
                    dve.wait_ge(q_dve, ch.count(ch.w2 + 1, "D"))
                    if ch.again:
                        nc.vector.tensor_copy(HT[q][:, :, :], HI[q][:, :, :]).then_inc(hi_used, 1)
                    nc.vector.memset(pause[:, q:q + 1], 0.0).then_inc(ot_done, 1)

            def step(u, s, p, l, has_out, has_front, ch):
                o = 1 - s
                for i in range(NS):
                    scan_op(u, s, i)
                    if i < NS - 1:
                        if i + 1 not in POOL_BX:
                            bx_op(u, s, i + 1)
                    elif has_front:
                        dve.wait_ge(u_done, ONE + u + 2)
                        bx_op(u + 1, o, 0)
                    hc_op(u, s, i)
                    if i == 0 and has_out:
                        yf_op(u - 1, o)
                    if ch is not None:
                        change(ch, i)

            def enter():
                for s in range(2):
                    dve.wait_ge(hi_ld[s], 16)
                    if s:
                        dve.wait_ge(q_full, 2)
                    moments(HI[s], s)
                    normalize(HI[s], s)
                    nc.vector.tensor_copy(HT[s][:, :, :], HI[s][:, :, :]).then_inc(hi_used, 1)
                dve.wait_ge(u_done, ONE + 1)
                bx_op(0, 0, 0)

            def leave(b, c_):
                yf_op(UNITS - 1, 1)
                for ch in (b, c_):
                    for i in range(NS):
                        change(ch, i)

            steps(dve, enter, step, leave)


def host_layouts(x):
    import numpy as np

    a = {}
    a["x"], a["txt"] = x["x"], x["txt"]
    stem = x["L0_tok_stem_w"].transpose(3, 1, 2, 0).reshape(48, CO)
    a["stem"] = np.concatenate([stem, x["L0_tok_stem_b"][None]], 0)
    for k in ("g", "b", "m", "v"):
        a[f"bn1_{k}"], a[f"bn2_{k}"] = x[f"L0_tok_bn1_{k}"], x[f"L0_tok_bn2_{k}"]
    a["dcn_w"] = x["L0_tok_dcn_w"].transpose(2, 3, 1, 0).reshape(NKT, 128, D).transpose(1, 0, 2)
    a["dcn_b"] = x["L0_tok_dcn_b"]
    a["off_w"] = x["L0_tok_off_w"].transpose(1, 2, 3, 0).reshape(CO, TAPS, 32)
    a["off_b"] = x["L0_tok_off_b"]
    q, t, k = np.arange(QP)[:, None, None], np.arange(2)[None, :, None], np.arange(TAPS)[None, None, :]
    y = 4 * (7 * t + q // GRID) + k // 4
    xx = 4 * (q % GRID) + k % 4 + 0 * t
    a["base"] = np.stack(np.broadcast_arrays(y, xx), -1).reshape(QP, 2, 32).astype(np.float32)
    a["ident"] = np.eye(128, dtype=np.float32)
    sel = np.zeros((96, 2 * NS, 128), np.float32)
    for r in range(96):
        sel[r, r % 32, :] = 1
    a["sel"] = sel
    w = x["L0_attn_in_proj_w"]
    wx = w[:, :, :DI]
    a["in_x"] = np.stack([wx[:, 0:128], np.concatenate([wx[:, 128:], wx[:, 128:]], 1)], 2)
    a["in_z"] = w[:, :, DI:]
    a["conv_w"] = x["L0_attn_conv_w"].transpose(0, 2, 1)
    xp = x["L0_attn_x_proj_w"].reshape(LAYERS, MT, 128, RANK + 2 * NS).transpose(0, 2, 1, 3)
    bc = xp[..., RANK:]
    a["xp"] = np.concatenate([bc, bc, bc, xp[..., :RANK]], -1)
    a["dtw"] = x["L0_attn_dt_proj_w"]
    col = lambda v: v.reshape(LAYERS, MT, 128).transpose(0, 2, 1)
    a["cdb"] = np.concatenate([col(x["L0_attn_conv_b"]), col(x["L0_attn_dt_proj_b"])], -1)
    al = x["L0_attn_A_log"].reshape(LAYERS, MT, 128, NS).transpose(0, 2, 1, 3).reshape(LAYERS, 128, MT * NS)
    a["pa"] = np.concatenate([al, col(x["L0_attn_D"])], -1)
    o = x["L0_attn_out_proj_w"]
    o = np.concatenate([o, o[..., KLO:]], -1)
    a["ow"] = o.reshape(LAYERS, MT, 128, 256).transpose(0, 2, 1, 3)
    a["head_w1"], a["head_w2"] = x["L0_attn_head_w1"], x["L0_attn_head_w2"]
    a["head_b1"], a["head_b2"] = x["L0_attn_head_b1"], x["L0_attn_head_b2"]
    a["ffn_w1"] = x["L0_ffn_w1"].T
    a["ffn_w2"] = x["L0_ffn_w2"].T.reshape(FM, 128, D).transpose(1, 0, 2)
    a["ffn_b1"] = x["L0_ffn_b1"].reshape(FM, 128).T
    a["ffn_b2"] = x["L0_ffn_b2"]
    return {k: np.ascontiguousarray(v) for k, v in a.items()}


def kernel(**inputs):
    import numpy as np
    import concourse.bacc as bacc
    from concourse.bass_utils import run_bass_kernel_spmd

    arrays = host_layouts({k: np.asarray(v) for k, v in inputs.items()})
    nc = bacc.Bacc("TRN2", target_bir_lowering=False, num_devices=1)
    w = {k: nc.dram_tensor(f"in_{k}", v.shape, mybir.dt.from_np(v.dtype), kind="ExternalInput").ap()
         for k, v in arrays.items()}
    NB = arrays["x"].shape[0]
    out = nc.dram_tensor("out_0", [NB, T, D], F32, kind="ExternalOutput").ap()
    program(nc, w, out)
    r = run_bass_kernel_spmd(nc, [{f"in_{k}": v for k, v in arrays.items()}], core_ids=[0])
    return r.results[0]["out_0"]
```
